# Optimizing a Trainium2 kernel written in Bass

```python
import numpy as np
import jax
import jax.numpy as jnp

def _softmax(x, axis=-1):
    return jax.nn.softmax(x, axis=axis)

def _gelu(x):
    return jax.nn.gelu(x, approximate=True)

def _silu(x):
    return jax.nn.silu(x)

def _sigmoid(x):
    return jax.nn.sigmoid(x)

def _layernorm(x, axis=-1, eps=1e-05):
    m = jnp.mean(x, axis=axis, keepdims=True)
    v = jnp.var(x, axis=axis, keepdims=True)
    return (x - m) / jnp.sqrt(v + eps)

def _scatter_add(tgt, idx, src, axis=0):
    return tgt.at[idx].add(src)

def _segment_sum(src, seg, n):
    return jax.ops.segment_sum(src, seg, n)
kernel_name = 'mk_decoder_postln_d1_seqx_r4_98a34b'

def setup_inputs(seed: int=0):
    np.random.seed(seed)
    _w = jnp.asarray

    def _rec_inputs():
        import jax
        import jax.numpy as jnp
        _rk = jax.random.key(seed)
        x = -0.0002928 + 1 * jax.random.normal(jax.random.fold_in(_rk, 1), (4, 512, 256), jnp.float32)
        _lenS = 512 - jax.random.randint(jax.random.fold_in(_rk, 7), (4,), 0, max(1, 512 // 4) + 1, jnp.int32)
        _lenS2 = 512 - jax.random.randint(jax.random.fold_in(_rk, 8), (4,), 0, max(1, 512 // 4) + 1, jnp.int32)
        _ctx_1024P = jax.random.normal(jax.random.fold_in(_rk, 11), (4, 16, 256), jnp.float32)
        _ctx_1024c = jax.random.dirichlet(jax.random.fold_in(_rk, 511), 0.3 * jnp.ones((16,), jnp.float32), (4, 512))
        _ctx_1024t = jnp.einsum('bsk,bkd->bsd', _ctx_1024c, _ctx_1024P)
        _ctx_1024t = _ctx_1024t * jax.lax.rsqrt(jnp.mean(jnp.square(_ctx_1024t)) + 1e-12) * 0.953939
        ctx_1024 = -1.39393e-06 + 0.999914 * (_ctx_1024t + 0.3 * jax.random.normal(jax.random.fold_in(_rk, 611), (4, 512, 256), jnp.float32))
        return (x, ctx_1024)
    x, ctx_1024 = _rec_inputs()

    def _L0_attn_setup():
        import jax, jax.numpy as jnp
        import numpy as np
        import math
        B, T, D = (4, 1024, 256)
        K, H, KH, C = (64, 4, 16, 64)
        MLP = 1024
        EPS = 1e-05

        def _layernorm(x, g, b):
            m = jnp.mean(x, axis=-1, keepdims=True)
            v = jnp.mean((x - m) ** 2, axis=-1, keepdims=True)
            return (x - m) / jnp.sqrt(v + EPS) * g + b

        def _chunked_eigenstate(log_decay, frequency, beta_r, beta_i):
            Bt, Tt, Kt = beta_r.shape
            T_pad = (Tt + C - 1) // C * C
            if T_pad > Tt:
                beta_r = jnp.pad(beta_r, ((0, 0), (0, T_pad - Tt), (0, 0)))
                beta_i = jnp.pad(beta_i, ((0, 0), (0, T_pad - Tt), (0, 0)))
            n_chunks = T_pad // C
            mag = jax.nn.sigmoid(log_decay)
            powers = jnp.arange(C, dtype=log_decay.dtype)
            mag_pow = mag[:, None] ** powers[None, :]
            phases = frequency[:, None] * powers[None, :]
            kr = mag_pow * jnp.cos(phases)
            ki = mag_pow * jnp.sin(phases)
            ii = jnp.arange(C)
            idx = ii[None, :] - ii[:, None]
            mask = (idx >= 0).astype(kr.dtype)
            idxc = jnp.clip(idx, 0, C - 1)
            L_r = kr[:, idxc] * mask[None]
            L_i = ki[:, idxc] * mask[None]
            br = beta_r.reshape(Bt, n_chunks, C, Kt)
            bi = beta_i.reshape(Bt, n_chunks, C, Kt)
            intra_r = jnp.einsum('kjs,bnsk->bnjk', L_r, br) - jnp.einsum('kjs,bnsk->bnjk', L_i, bi)
            intra_i = jnp.einsum('kjs,bnsk->bnjk', L_r, bi) + jnp.einsum('kjs,bnsk->bnjk', L_i, br)
            first_col_r = L_r[:, :, 0]
            first_col_i = L_i[:, :, 0]

            def step(carry, intra):
                sr, si = carry
                ir, im = intra
                cr = first_col_r[None] * sr[:, :, None] - first_col_i[None] * si[:, :, None]
                ci = first_col_r[None] * si[:, :, None] + first_col_i[None] * sr[:, :, None]
                o_r = ir + jnp.transpose(cr, (0, 2, 1))
                o_i = im + jnp.transpose(ci, (0, 2, 1))
                return ((o_r[:, -1, :], o_i[:, -1, :]), (o_r, o_i))
            xs = (jnp.transpose(intra_r, (1, 0, 2, 3)), jnp.transpose(intra_i, (1, 0, 2, 3)))
            init = (jnp.zeros((Bt, Kt), beta_r.dtype), jnp.zeros((Bt, Kt), beta_r.dtype))
            _, (out_r, out_i) = jax.lax.scan(step, init, xs)
            c_r = jnp.transpose(out_r, (1, 0, 2, 3)).reshape(Bt, T_pad, Kt)[:, :Tt]
            c_i = jnp.transpose(out_i, (1, 0, 2, 3)).reshape(Bt, T_pad, Kt)[:, :Tt]
            return (c_r, c_i)
        key = jax.random.key(seed)
        ks = jax.random.split(key, 8)

        def n(k, shape, scale):
            return jax.random.normal(k, shape, dtype=jnp.float32) * scale
        return {'x': jax.random.normal(ks[0], (B, T, D), dtype=jnp.float32), 'w_in': n(ks[1], (2 * K, D), D ** (-0.5)), 'w_out': n(ks[2], (D, 2 * K), (2 * K) ** (-0.5)), 'w_gate': n(ks[3], (D, D), D ** (-0.5)), 'b_gate': jnp.full((D,), -2.0, dtype=jnp.float32), 'log_decay': jax.random.uniform(ks[4], (K,), minval=-3.0, maxval=-0.1, dtype=jnp.float32), 'frequency': jnp.linspace(0.0, 2.0 * math.pi * (1.0 - 1.0 / K), K, dtype=jnp.float32), 'coupling': jnp.eye(KH, dtype=jnp.float32)[None] + 0.01 * jax.random.normal(ks[5], (H, KH, KH), dtype=jnp.float32) / math.sqrt(KH), 'w_mlp1': n(ks[6], (MLP, D), D ** (-0.5)), 'b_mlp1': jnp.zeros((MLP,), jnp.float32), 'w_mlp2': n(ks[7], (D, MLP), MLP ** (-0.5)), 'b_mlp2': jnp.zeros((D,), jnp.float32), 'ln1_g': jnp.ones((D,), jnp.float32), 'ln1_b': jnp.zeros((D,), jnp.float32), 'ln2_g': jnp.ones((D,), jnp.float32), 'ln2_b': jnp.zeros((D,), jnp.float32)}
    _L0_attn_all = _L0_attn_setup()
    _L0_attn_in = {k: v for k, v in _L0_attn_all.items() if k in ('w_in', 'w_out', 'w_gate', 'b_gate', 'log_decay', 'frequency', 'coupling', 'w_mlp1', 'b_mlp1', 'w_mlp2', 'b_mlp2', 'ln1_g', 'ln1_b', 'ln2_g', 'ln2_b')}
    del _L0_attn_all

    def _L0_xattn_setup():
        import jax, jax.numpy as jnp
        import numpy as np
        D_MODEL = 256
        NHEAD = 16
        HEAD_DIM = D_MODEL // NHEAD
        key = jax.random.key(seed)
        ks = jax.random.split(key, 11)
        B, S = (2, 512)
        s = 1.0 / np.sqrt(D_MODEL)
        return {'query': jax.random.normal(ks[0], (B, S, D_MODEL), jnp.float32), 'key': jax.random.normal(ks[1], (B, S, D_MODEL), jnp.float32), 'value': jax.random.normal(ks[2], (B, S, D_MODEL), jnp.float32), 'wq_w': jax.random.normal(ks[3], (D_MODEL, D_MODEL), jnp.float32) * s, 'wq_b': jax.random.normal(ks[4], (D_MODEL,), jnp.float32) * s, 'wk_w': jax.random.normal(ks[5], (D_MODEL, D_MODEL), jnp.float32) * s, 'wk_b': jax.random.normal(ks[6], (D_MODEL,), jnp.float32) * s, 'wv_w': jax.random.normal(ks[7], (D_MODEL, D_MODEL), jnp.float32) * s, 'wv_b': jax.random.normal(ks[8], (D_MODEL,), jnp.float32) * s, 'wo_w': jax.random.normal(ks[9], (D_MODEL, D_MODEL), jnp.float32) * s, 'wo_b': jax.random.normal(ks[10], (D_MODEL,), jnp.float32) * s}
    _L0_xattn_all = _L0_xattn_setup()
    _L0_xattn_in = {k: v for k, v in _L0_xattn_all.items() if k in ('wq_w', 'wq_b', 'wk_w', 'wk_b', 'wv_w', 'wv_b', 'wo_w', 'wo_b')}
    del _L0_xattn_all

    def _L0_ffn_setup():
        import jax, jax.numpy as jnp
        import numpy as np
        CAP_FACTOR = 1.5
        key = jax.random.key(seed)
        ks = jax.random.split(key, 6)
        E, S, D, M = (48, 4, 256, 256)
        K = D // S
        x = jax.random.normal(ks[0], (4, 1024, D), dtype=jnp.float32)
        Wr = jax.random.normal(ks[1], (E, D), dtype=jnp.float32) * 0.02
        W1 = jax.random.normal(ks[2], (E, S, D, M), dtype=jnp.float32) * (1.0 / np.sqrt(D))
        b1 = jnp.zeros((E, S, M), dtype=jnp.float32)
        W2 = jax.random.normal(ks[3], (E, S, M, K), dtype=jnp.float32) * (1.0 / np.sqrt(M))
        b2 = jnp.zeros((E, S, K), dtype=jnp.float32)
        return {'x': x, 'Wr': Wr, 'W1': W1, 'b1': b1, 'W2': W2, 'b2': b2}
    _L0_ffn_all = _L0_ffn_setup()
    _L0_ffn_in = {k: v for k, v in _L0_ffn_all.items() if k in ('Wr', 'W1', 'b1', 'W2', 'b2')}
    del _L0_ffn_all
    return {'x': x, 'ctx_1024': ctx_1024, 'L0_attn_w_in': _L0_attn_in['w_in'], 'L0_attn_w_out': _L0_attn_in['w_out'], 'L0_attn_w_gate': _L0_attn_in['w_gate'], 'L0_attn_b_gate': _L0_attn_in['b_gate'], 'L0_attn_log_decay': _L0_attn_in['log_decay'], 'L0_attn_frequency': _L0_attn_in['frequency'], 'L0_attn_coupling': _L0_attn_in['coupling'], 'L0_attn_w_mlp1': _L0_attn_in['w_mlp1'], 'L0_attn_b_mlp1': _L0_attn_in['b_mlp1'], 'L0_attn_w_mlp2': _L0_attn_in['w_mlp2'], 'L0_attn_b_mlp2': _L0_attn_in['b_mlp2'], 'L0_attn_ln1_g': _L0_attn_in['ln1_g'], 'L0_attn_ln1_b': _L0_attn_in['ln1_b'], 'L0_attn_ln2_g': _L0_attn_in['ln2_g'], 'L0_attn_ln2_b': _L0_attn_in['ln2_b'], 'L0_xattn_wq_w': _L0_xattn_in['wq_w'], 'L0_xattn_wq_b': _L0_xattn_in['wq_b'], 'L0_xattn_wk_w': _L0_xattn_in['wk_w'], 'L0_xattn_wk_b': _L0_xattn_in['wk_b'], 'L0_xattn_wv_w': _L0_xattn_in['wv_w'], 'L0_xattn_wv_b': _L0_xattn_in['wv_b'], 'L0_xattn_wo_w': _L0_xattn_in['wo_w'], 'L0_xattn_wo_b': _L0_xattn_in['wo_b'], 'L0_ffn_Wr': _L0_ffn_in['Wr'], 'L0_ffn_W1': _L0_ffn_in['W1'], 'L0_ffn_b1': _L0_ffn_in['b1'], 'L0_ffn_W2': _L0_ffn_in['W2'], 'L0_ffn_b2': _L0_ffn_in['b2']}

def reference(x, ctx_1024, L0_attn_w_in, L0_attn_w_out, L0_attn_w_gate, L0_attn_b_gate, L0_attn_log_decay, L0_attn_frequency, L0_attn_coupling, L0_attn_w_mlp1, L0_attn_b_mlp1, L0_attn_w_mlp2, L0_attn_b_mlp2, L0_attn_ln1_g, L0_attn_ln1_b, L0_attn_ln2_g, L0_attn_ln2_b, L0_xattn_wq_w, L0_xattn_wq_b, L0_xattn_wk_w, L0_xattn_wk_b, L0_xattn_wv_w, L0_xattn_wv_b, L0_xattn_wo_w, L0_xattn_wo_b, L0_ffn_Wr, L0_ffn_W1, L0_ffn_b1, L0_ffn_W2, L0_ffn_b2):
    import jax
    import jax.numpy as jnp

    def _L0_attn_ref(x, w_in, w_out, w_gate, b_gate, log_decay, frequency, coupling, w_mlp1, b_mlp1, w_mlp2, b_mlp2, ln1_g, ln1_b, ln2_g, ln2_b):
        import jax, jax.numpy as jnp
        import numpy as np
        import math
        B, T, D = (4, 1024, 256)
        K, H, KH, C = (64, 4, 16, 64)
        MLP = 1024
        EPS = 1e-05

        def _layernorm(x, g, b):
            m = jnp.mean(x, axis=-1, keepdims=True)
            v = jnp.mean((x - m) ** 2, axis=-1, keepdims=True)
            return (x - m) / jnp.sqrt(v + EPS) * g + b

        def _chunked_eigenstate(log_decay, frequency, beta_r, beta_i):
            Bt, Tt, Kt = beta_r.shape
            T_pad = (Tt + C - 1) // C * C
            if T_pad > Tt:
                beta_r = jnp.pad(beta_r, ((0, 0), (0, T_pad - Tt), (0, 0)))
                beta_i = jnp.pad(beta_i, ((0, 0), (0, T_pad - Tt), (0, 0)))
            n_chunks = T_pad // C
            mag = jax.nn.sigmoid(log_decay)
            powers = jnp.arange(C, dtype=log_decay.dtype)
            mag_pow = mag[:, None] ** powers[None, :]
            phases = frequency[:, None] * powers[None, :]
            kr = mag_pow * jnp.cos(phases)
            ki = mag_pow * jnp.sin(phases)
            ii = jnp.arange(C)
            idx = ii[None, :] - ii[:, None]
            mask = (idx >= 0).astype(kr.dtype)
            idxc = jnp.clip(idx, 0, C - 1)
            L_r = kr[:, idxc] * mask[None]
            L_i = ki[:, idxc] * mask[None]
            br = beta_r.reshape(Bt, n_chunks, C, Kt)
            bi = beta_i.reshape(Bt, n_chunks, C, Kt)
            intra_r = jnp.einsum('kjs,bnsk->bnjk', L_r, br) - jnp.einsum('kjs,bnsk->bnjk', L_i, bi)
            intra_i = jnp.einsum('kjs,bnsk->bnjk', L_r, bi) + jnp.einsum('kjs,bnsk->bnjk', L_i, br)
            first_col_r = L_r[:, :, 0]
            first_col_i = L_i[:, :, 0]

            def step(carry, intra):
                sr, si = carry
                ir, im = intra
                cr = first_col_r[None] * sr[:, :, None] - first_col_i[None] * si[:, :, None]
                ci = first_col_r[None] * si[:, :, None] + first_col_i[None] * sr[:, :, None]
                o_r = ir + jnp.transpose(cr, (0, 2, 1))
                o_i = im + jnp.transpose(ci, (0, 2, 1))
                return ((o_r[:, -1, :], o_i[:, -1, :]), (o_r, o_i))
            xs = (jnp.transpose(intra_r, (1, 0, 2, 3)), jnp.transpose(intra_i, (1, 0, 2, 3)))
            init = (jnp.zeros((Bt, Kt), beta_r.dtype), jnp.zeros((Bt, Kt), beta_r.dtype))
            _, (out_r, out_i) = jax.lax.scan(step, init, xs)
            c_r = jnp.transpose(out_r, (1, 0, 2, 3)).reshape(Bt, T_pad, Kt)[:, :Tt]
            c_i = jnp.transpose(out_i, (1, 0, 2, 3)).reshape(Bt, T_pad, Kt)[:, :Tt]
            return (c_r, c_i)
        residual = x
        x_norm = _layernorm(x, ln1_g, ln1_b)
        beta = x_norm @ w_in.T
        beta_r, beta_i = jnp.split(beta, 2, axis=-1)
        c_r, c_i = _chunked_eigenstate(log_decay, frequency, beta_r, beta_i)
        c_rh = c_r.reshape(x.shape[0], x.shape[1], H, KH)
        c_ih = c_i.reshape(x.shape[0], x.shape[1], H, KH)
        c_r = jnp.einsum('hjk,bthk->bthj', coupling, c_rh).reshape(x.shape[0], x.shape[1], K)
        c_i = jnp.einsum('hjk,bthk->bthj', coupling, c_ih).reshape(x.shape[0], x.shape[1], K)
        h = jnp.concatenate([c_r, c_i], axis=-1) @ w_out.T
        gate = jax.nn.sigmoid(x_norm @ w_gate.T + b_gate)
        x1 = residual + gate * h
        x2n = _layernorm(x1, ln2_g, ln2_b)
        mlp = jax.nn.silu(x2n @ w_mlp1.T + b_mlp1) @ w_mlp2.T + b_mlp2
        return x1 + mlp

    def _L0_xattn_ref(query, key, value, wq_w, wq_b, wk_w, wk_b, wv_w, wv_b, wo_w, wo_b):
        import jax, jax.numpy as jnp
        import numpy as np
        D_MODEL = 256
        NHEAD = 16
        HEAD_DIM = D_MODEL // NHEAD
        B, S, _ = query.shape

        def proj(x, w, b):
            y = x @ w.T + b
            return y.reshape(B, S, NHEAD, HEAD_DIM).transpose(0, 2, 1, 3)
        Q = proj(query, wq_w, wq_b)
        K = proj(key, wk_w, wk_b)
        V = proj(value, wv_w, wv_b)
        scale = 1.0 / np.sqrt(HEAD_DIM).astype(np.float32)
        scores = jnp.einsum('bhqd,bhkd->bhqk', Q, K) * scale
        causal = jnp.tril(jnp.ones((S, S), dtype=bool))
        scores = jnp.where(causal, scores, -jnp.inf)
        attn = jax.nn.softmax(scores, axis=-1)
        out = jnp.einsum('bhqk,bhkd->bhqd', attn, V)
        out = out.transpose(0, 2, 1, 3).reshape(B, S, D_MODEL)
        return out @ wo_w.T + wo_b

    def _L0_ffn_ref(x, Wr, W1, b1, W2, b2):
        import jax, jax.numpy as jnp
        import numpy as np
        CAP_FACTOR = 1.5
        orig_shape = x.shape
        D = x.shape[-1]
        E = Wr.shape[0]
        xf = x.reshape(-1, D)
        T = xf.shape[0]
        cap = int(CAP_FACTOR * T / E)
        logits = xf @ Wr.T
        vals, idx = jax.lax.top_k(logits.T, cap)
        w = jax.nn.softmax(vals, axis=-1)
        xg = xf[idx]
        h = jax.nn.gelu(jnp.einsum('ecd,esdm->ecsm', xg, W1) + b1[:, None], approximate=False)
        y = jnp.einsum('ecsm,esmk->ecsk', h, W2) + b2[:, None]
        y = y.reshape(E, cap, D) * w[..., None]
        out = jnp.zeros_like(xf).at[idx.reshape(-1)].add(y.reshape(-1, D))
        return out.reshape(orig_shape)
    x = _layernorm(x + _L0_attn_ref(x, L0_attn_w_in, L0_attn_w_out, L0_attn_w_gate, L0_attn_b_gate, L0_attn_log_decay, L0_attn_frequency, L0_attn_coupling, L0_attn_w_mlp1, L0_attn_b_mlp1, L0_attn_w_mlp2, L0_attn_b_mlp2, L0_attn_ln1_g, L0_attn_ln1_b, L0_attn_ln2_g, L0_attn_ln2_b), axis=-1)
    x = _layernorm(x + _L0_xattn_ref(x, ctx_1024, ctx_1024, L0_xattn_wq_w, L0_xattn_wq_b, L0_xattn_wk_w, L0_xattn_wk_b, L0_xattn_wv_w, L0_xattn_wv_b, L0_xattn_wo_w, L0_xattn_wo_b), axis=-1)
    x = _layernorm(x + _L0_ffn_ref(x, L0_ffn_Wr, L0_ffn_W1, L0_ffn_b1, L0_ffn_W2, L0_ffn_b2), axis=-1)
    return x

_drawn_inputs = setup_inputs


def setup_inputs(seed=0):
    import zlib

    import numpy as np

    out = dict(_drawn_inputs(seed))
    spreads = {'L0_attn_b_gate': (-2.0, 0.577),
     'L0_attn_b_mlp1': (0.0, 0.286),
     'L0_attn_b_mlp2': (0.0, 0.1),
     'L0_attn_ln1_g': (1.0, 0.594),
     'L0_attn_ln1_b': (0.0, 0.638),
     'L0_attn_ln2_g': (1.0, 0.2),
     'L0_attn_ln2_b': (0.0, 0.28),
     'L0_ffn_b1': (0.0, 0.8),
     'L0_ffn_b2': (0.0, 0.8)}
    factors = {'L0_attn_log_decay': 3.661, 'L0_xattn_wq_b': 4.164, 'L0_xattn_wk_b': 8.0}
    for name, (base, spread) in spreads.items():
        noise = np.random.default_rng([zlib.crc32(name.encode()), seed]).standard_normal(out[name].shape)
        drawn = base * np.exp(spread * noise) if base else spread * noise
        out[name] = jnp.asarray(drawn.astype(out[name].dtype))
    for name, factor in factors.items():
        out[name] = (out[name] * factor).astype(out[name].dtype)
    return out
```

```python
from contextlib import ExitStack

import numpy as np
import concourse.bass as bass
from concourse import mybir

F32 = mybir.dt.float32
BF16 = mybir.dt.bfloat16
U32 = mybir.dt.uint32
I32 = mybir.dt.int32
ALU = mybir.AluOpType
ACT = mybir.ActivationFunctionType
AX = mybir.AxisListType

P = 128
B, T, D = 4, 512, 256
TT = T // P
KT = D // P
NK = 64
C = 64
NCH = T // C
CH, CK = 4, 16
MLP = 1024
MT = MLP // P
NH, HD = 16, 16
GH = 4
NG = NH // GH
NPC = 3
NPR = 6
SK = NPR * HD
VW = 32
E, S = 48, 4
M2 = 256
KO = D // S
CAP = int(1.5 * B * T / E)
NP = E // 2
RING = 6
W1C = 2 * KT * S * M2
W2C = 2 * S * (M2 // P) * KO
EPS = 1e-5
NEG = -3.0e38
TWO_PI_HI = 6.28125
TWO_PI_LO = 2 * np.pi - 6.28125
ROUND = 12582912.0

V_G1, V_B1, V_G2, V_B2, V_BM, V_DEC, V_FRQ = 0, 2, 4, 6, 8, 16, 17
VCOLS = 18
R_GATE, R_M2, R_K, R_V, R_Q, R_O = (256 * n for n in range(6))
RCOLS = 6 * 256


class Signal:

    def __init__(self, sem, per, unit=1):
        self.s, self.per, self.unit = sem, per, unit

    def now(self, b, k):
        return (b * self.per + (self.per + k)) * self.unit

    def before(self, b, k):
        return (b * self.per + k) * self.unit


def build(nc, x, ctx_in, w_in, w_gate, w_out, coupling, w_mlp1, w_mlp2, w_q, w_kv, w_o, w_r,
          vecs, rows, b1, b2, experts, out):
    x2_rows = nc.dram_tensor("x2_rows", (B * T, D), F32, kind="Internal").ap()
    sums = nc.dram_tensor("sums", (2 * B * T, D), F32, kind="Internal").ap()

    stack = ExitStack()
    with stack:
        def sb(name, shape, dt=F32):
            return stack.enter_context(nc.sbuf_tensor(name, shape, dt))

        def sem(name):
            return stack.enter_context(nc.semaphore(name))

        def signal(name, per, unit=1):
            s = Signal(sem(name), per, unit)
            signals.append(s)
            return s

        signals = []

        PS = stack.enter_context(nc.psum_tensor("PS", [P, 8 * 512], F32))

        def bank(n, k=1):
            return PS[:, n * 512:(n + k) * 512]

        X = sb("X", [P, B * TT, D])
        Y = sb("Y", [P, B * TT, D])
        A = sb("arena", [P, 20992])
        ring_a = sb("ring_a", [P, 3, W1C + W2C])
        ident = sb("ident", [P, P])
        identb = sb("identb", [P, P], BF16)
        cos_t = sb("cos_t", [P, C])
        sin_t = sb("sin_t", [P, C])
        vec = sb("vec", [P, VCOLS])
        row = sb("row", [P, RCOLS])
        wq_s = sb("wq_s", [P, KT, D])
        wkv_s = sb("wkv_s", [P, KT, 2 * D])
        wo_s = sb("wo_s", [P, KT, D])
        wr_s = sb("wr_s", [P, KT, 64])
        stats = sb("stats", [P, TT, 6])
        mv = sb("mv", [P, TT, 2])
        ve = sb("ve", [P, TT])
        rstd = sb("rstd", [P, TT])
        mhalf = sb("mhalf", [P, TT])
        causal = sb("causal", [P, T], BF16)
        junk = sb("junk", [P, 2, T], BF16)
        sel = sb("sel", [NPC * GH, GH, P], BF16)
        Mx = sb("Mx", [P, 2, TT, GH])
        Mr = sb("Mr", [P, TT, GH])
        nst = sb("nst", [P, 2, TT, NPC, GH], BF16)
        NT = sb("NT", [NPC * GH, 2, T], BF16)
        zrow = sb("zrow", [P, D])
        smz = sb("smz", [P, 1])
        rden = sb("rden", [P, TT, GH])

        used = [0]

        def carve(n):
            a = used[0]
            used[0] += n
            assert used[0] <= 20992, used
            return A[:, a:a + n]

        wi_s = carve(KT * 256).rearrange("p (k n) -> p k n", k=KT)
        wg_s = carve(KT * D).rearrange("p (k n) -> p k n", k=KT)
        wm1_s = carve(KT * MLP).rearrange("p (k n) -> p k n", k=KT)
        wm2_s = carve(MT * D).rearrange("p (k n) -> p k n", k=MT)
        wc_s = carve(2 * D).rearrange("p (k n) -> p k n", k=2)
        wout_s = carve(2 * D).rearrange("p (k n) -> p k n", k=2)
        cb_s = carve(P)
        decay = carve(T)
        rot = carve(T)
        rot2 = carve(T)
        ysc = carve(T)
        yc = carve(T)
        ys = carve(T)
        xT = carve(KT * T).rearrange("p (k n) -> p k n", k=KT)
        gz = carve(TT * D).rearrange("p (t n) -> p t n", t=TT)
        hg = carve(TT * D).rearrange("p (t n) -> p t n", t=TT)
        hid = carve(MT * T).rearrange("p (k n) -> p k n", k=MT)
        ph_i = carve(C).bitcast(I32)
        ph = carve(C)
        ph_n = carve(C)
        ph_m = carve(C)
        mag = carve(1)
        xn = carve(TT * D).rearrange("p (t n) -> p t n", t=TT)
        used[0] = 0
        cT = carve(KT * T).rearrange("p (k n) -> p k n", k=KT)
        aT = carve(KT * T).rearrange("p (k n) -> p k n", k=KT)
        kq = carve(TT * D)
        Vb = carve(TT * NH * VW).rearrange("p (t h v) -> p t h v", t=TT, h=NH)
        st = carve(TT * NH * SK // 2).bitcast(BF16).rearrange("p (t h s) -> p t h s", t=TT, h=NH)
        KTs = carve(NH * T // 2).bitcast(BF16).rearrange("p (h n) -> p h n", h=NH)
        QTs = carve(NH * T // 2).bitcast(BF16).rearrange("p (h n) -> p h n", h=NH)
        pbs = carve(2 * GH * T)
        pb = [pbs[:, n * GH * T:(n + 1) * GH * T].rearrange("p (h n) -> p h n", h=GH)
              for n in range(2)]
        stq = pbs[:, 0:TT * NH * SK // 2].bitcast(BF16)\
            .rearrange("p (t h s) -> p t h s", t=TT, h=NH)
        oTs = carve(T)
        yr = Y[:, :, :].rearrange("p a d -> p (a d)")
        ctxb = yr[:, 0:1024].rearrange("p (t n) -> p t n", t=TT)
        otok = yr[:, 1024:2048].rearrange("p (t n) -> p t n", t=TT)
        oT2 = yr[:, 2048:3072].rearrange("p (k n) -> p k n", k=KT)
        xs = yr[:, 3072:4096].rearrange("p (t n) -> p t n", t=TT)
        kqt = kq.rearrange("p (t n) -> p t n", t=TT)
        x2T = cT
        LGs = sb("LGs", [64, B, T])
        used[0] = 0
        ring_b = [carve(W1C + W2C) for _ in range(3)]
        slot = [ring_a[:, n, :] for n in range(3)] + ring_b
        w1_of = [s_[:, 0:W1C].rearrange("p (e k n) -> p e k n", e=2, k=KT) for s_ in slot]
        w2_of = [s_[:, W1C:].rearrange("p (e s m k) -> p e s m k", e=2, s=S, m=M2 // P)
                 for s_ in slot]
        xr_ = X[:, :, :].rearrange("p a d -> p (a d)")
        LG2 = yr[:, 0:1024]
        top_v = yr[:, 1024:1088]
        top_i = yr[:, 1088:1152].bitcast(U32)
        top_f = yr[:, 1152:1216]
        pick = yr[:, 1216:1280]
        sel_v = yr[:, 1280:1344]
        sel_i = yr[:, 1344:1408]
        far_v = yr[:, 1408:1472]
        far_i = yr[:, 1472:1536]
        tw = yr[0:32, 1536:1664]
        ti = yr[0:32, 1664:1792]
        smx = yr[:, 1792:1800]
        wcol = yr[:, 1800:1824]
        icol = yr[:, 1824:1848].bitcast(U32)
        jcol = yr[:, 1848:1872].bitcast(U32)
        icf = yr[:, 1872:1896]
        jcf = yr[:, 1896:1920]
        off = yr[:, 1920:1921]
        gidx = [yr[:, 1922 + n:1923 + n].bitcast(U32) for n in range(2)]
        sidx = [yr[:, 1924 + n:1925 + n].bitcast(U32) for n in range(2)]
        b1_s = yr[:, 2048:2432].rearrange("p (e c a) -> p e c a", e=NP, a=2)
        pair_of = yr[0:2, 2432:2560]
        HB = xr_[:, 0:1024]
        hb = xr_[:, 1024:2048]
        b2_s = [xr_[0:2, 2048 + n * D:2048 + (n + 1) * D] for n in range(4)]
        b2_s += [yr[0:2, 3072 + n * D:3072 + (n + 1) * D] for n in range(2)]
        xg = [xr_[:, 3072 + 256 * n:3328 + 256 * n] for n in range(2)]
        xgT = xr_[:, 3584:3840].rearrange("p (k n) -> p k n", k=KT)
        ye = [yr[:, 2560 + 256 * n:2816 + 256 * n] for n in range(2)]


        w_one = sem("w_one")
        w_mlp = sem("w_mlp")
        w_att = sem("w_att")
        consts = sem("consts")
        setup = sem("setup")
        trig = sem("trig")
        wc_mm = sem("wc_mm")
        x_in = signal("x_in", 1, 16)
        ln1 = signal("ln1", 2 * TT + TT)
        rs1 = signal("rs1", 2)
        xt1 = signal("xt1", 1)
        xe1 = signal("xe1", 2)
        beta = signal("beta", 2)
        rots = signal("rots", 5)
        gpre = signal("gpre", 1)
        gact = signal("gact", 1)
        yrot = signal("yrot", 2)
        hmm = signal("hmm", 1)
        hgs = signal("hgs", 1)
        res = signal("res", 3)
        ln2 = signal("ln2", 3 * TT)
        rs2 = signal("rs2", 2)
        xt2 = signal("xt2", 1)
        xe2 = signal("xe2", 2)
        m1 = signal("m1", MT)
        silu = signal("silu", MT)
        m2 = signal("m2", 1)
        ln3 = signal("ln3", 1 + 3 * TT)
        rs3 = signal("rs3", 2)
        c_in = signal("c_in", 1, 16)
        xcp = signal("xcp", 2)
        tps = signal("tps", 2)
        tev = signal("tev", 2 * KT)
        kvp = signal("kvp", TT)
        qpr = signal("qpr", 1)
        kvq = signal("kvq", 2 * TT + 1)
        ksp = signal("ksp", 6)
        qsp = signal("qsp", 7)
        stk = signal("stk", 2 * TT)
        sea = signal("sea", 2 * TT)
        sed = signal("sed", 2 * TT)
        smm = signal("smm", NG * 16)
        mxs = signal("mxs", NG * 16)
        mneg = signal("mneg", NG * 4)
        ntp = signal("ntp", NG)
        nte = signal("nte", NG)
        stm = signal("stm", NG * 2 * TT)
        exq = signal("exq", NG * 2 * TT)
        msk = signal("msk", NG * TT)
        pvs = signal("pvs", NG * TT)
        oev = signal("oev", NG)
        otp = signal("otp", NG)
        odv = signal("odv", NG * 2)
        o2t = signal("o2t", 1)
        o2e = signal("o2e", KT)
        omm = signal("omm", 1)
        ln4 = signal("ln4", 1 + 3 * TT)
        rs4 = signal("rs4", 2)
        x2t = signal("x2t", 1)
        x2e = signal("x2e", KT)
        lgm = signal("lgm", 1)
        lge = signal("lge", 1)
        x2o = signal("x2o", 2, 16)
        zsum = sem("zsum")
        b1_in = sem("b1_in")
        topk = sem("topk")
        wexp = sem("wexp")
        icm = sem("icm")
        w_ring = [signal(f"w_ring{n}", 1, 16) for n in range(RING)]
        b_ring = [signal(f"b_ring{n}", 1, 16) for n in range(RING)]
        gix = signal("gix", 1)
        six = signal("six", 1)
        gathered = [sem(f"gathered{n}") for n in range(2)]
        scattered = sem("scattered")
        added = signal("added", 2)
        xgt = signal("xgt", 1)
        xge = signal("xge", 1)
        h1m = signal("h1m", 2)
        hea = signal("hea", 1)
        hed = signal("hed", 1)
        htm = signal("htm", 2)
        hbs = signal("hbs", 2)
        gel = signal("gel", 2)
        y2m = signal("y2m", 1)
        yws = signal("yws", 1)
        fin_in = [sem(f"fin_in{n}") for n in range(B)]
        fin = sem("fin")
        froot = sem("froot")
        stored = sem("stored")
        vset = sem("vset")
        pool_held = sem("pool_held")
        dve_held = sem("dve_held")
        setup_cb = sem("setup_cb")
        offs = sem("offs")
        SHIFTED, CHOSEN, TOPK = 36, 42, 47
        CONSTS, SETUP, W_ONE = 16, 19, 16 * 13

        x_v = x.rearrange("b (t p) d -> b p t d", p=P)
        ctx_v = ctx_in.rearrange("b (t p) d -> b p t d", p=P)
        out_v = out.rearrange("b (t p) d -> p (b t) d", p=P)
        x2_v = x2_rows.rearrange("(b t p) d -> b p t d", p=P, b=B)
        sums_v = sums.rearrange("(a b t p) d -> a b p t d", p=P, b=B, a=2)

        def wide(ap, n):
            return ap.unsqueeze(1).to_broadcast([ap.shape[0], n, ap.shape[1]])

        block = stack.enter_context(nc.Block())

        @block.sync
        def _(sp):
            sp.sem_inc(x_in.s, 16)
            with sp.Fori(0, B) as b:
                sp.wait_ge(x_in.s, x_in.before(b, 1))
                sp.dma_start(X[:, bass.ts(b, TT), :], x_v[b]).then_inc(x_in.s, 16)

            for u in range(3):
                sp.dma_start(slot[u], experts[u]).then_inc(w_ring[u].s, 16)
            sp.wait_ge(consts, CONSTS)
            sp.dma_start(sums[B * T:, :].rearrange("(a p) d -> p a d", p=P), wide(zrow[:], B * TT))\
                .then_inc(zsum, 16)
            sp.sem_inc(c_in.s, 16)
            sp.sem_inc(x2o.s, 32)
            sp.wait_ge(ln2.s, ln2.now(B - 1, 3 * TT))
            with sp.Fori(0, B) as b:
                sp.wait_ge(tps.s, tps.before(b, 1))
                sp.dma_start(ctxb, ctx_v[b]).then_inc(c_in.s, 16)
                sp.wait_ge(ln4.s, ln4.now(b, 1 + 3 * TT))
                sp.dma_start(x2_v[b], kqt).then_inc(x2o.s, 16)
                sp.dma_start(sums_v[0, b], kqt).then_inc(x2o.s, 16)

            for g in w_ring + b_ring:
                sp.sem_inc(g.s, 16)
            sp.wait_ge(lge.s, lge.now(B - 1, 1))
            sp.dma_start(b1_s, b1).then_inc(b1_in, 16)
            for u in range(RING):
                if u >= 3:
                    sp.dma_start(slot[u], experts[u]).then_inc(w_ring[u].s, 16)
                sp.dma_start(b2_s[u], b2[u]).then_inc(b_ring[u].s, 16)
            with sp.Fori(1, NP // RING) as r:
                for u in range(RING):
                    sp.wait_ge(y2m.s, y2m.now((r - 1) * RING + u, 1))
                    sp.dma_start(slot[u], experts[r * RING + u]).then_inc(w_ring[u].s, 16)
                    sp.dma_start(b2_s[u], b2[r * RING + u]).then_inc(b_ring[u].s, 16)
            sp.wait_ge(scattered, 16 * NP)
            for b in range(B):
                sp.dma_start(X[:, b * TT:(b + 1) * TT, :], sums_v[0, b]).then_inc(fin_in[b], 16)
                sp.dma_start(Y[:, b * TT:(b + 1) * TT, :], sums_v[1, b]).then_inc(fin_in[b], 16)
            for b in range(B):
                sp.wait_ge(fin, (b + 1) * (2 + 3 * TT))
                sp.dma_start(out_v[:, b * TT:(b + 1) * TT, :], X[:, b * TT:(b + 1) * TT, :])\
                    .then_inc(stored, 16)
            sp.wait_ge(stored, 16 * B)

        @block.gpsimd
        def _(pool):
            for g in (rs1, yrot, res, rs2, rs3):
                pool.sem_inc(g.s, g.per)
            step = [0]

            def const(ins):
                step[0] += 1
                ins.then_inc(consts, 1)

            def settle():
                pool.wait_ge(consts, step[0])

            const(pool.memset(ident[:], 0.0))
            pool.memset(cb_s, 0.0).then_inc(setup_cb, 1)
            const(pool.memset(identb[:], 0.0))
            const(pool.memset(causal[:], 0.0))
            const(pool.memset(sel[:], 0.0))
            const(pool.memset(mhalf[:], -0.5))
            const(pool.memset(wr_s[:], 0.0))
            const(pool.memset(zrow[:], 0.0))
            const(pool.memset(decay, 1.0))
            const(pool.iota(ph_i, pattern=[[1, C]], base=0, channel_multiplier=0))
            settle()
            for m in (ident, identb):
                const(pool.affine_select(out=m[:], in_=m[:], compare_op=ALU.not_equal, fill=1.0,
                                         base=0, pattern=[[-1, P]], channel_multiplier=1))
            const(pool.affine_select(out=causal[:, T - P:], in_=causal[:, T - P:],
                                     compare_op=ALU.is_ge, fill=NEG, base=0,
                                     pattern=[[-1, P]], channel_multiplier=1))
            for n in range(NPC):
                const(pool.affine_select(out=sel[:], in_=sel[:], compare_op=ALU.not_equal, fill=1.0,
                                         base=-GH * n, pattern=[[-1, GH], [0, P]],
                                         channel_multiplier=1))
                settle()
            const(pool.memset(decay.rearrange("p (n c) -> p n c", c=C)[:, :, C - 1:C], 0.0))

            def root(norm, rs, b, k):
                pool.wait_ge(norm.s, norm.now(b, k))
                pool.sem_inc(pool_held, 1)
                pool.tensor_scalar(ve[:], mv[:, :, 1], EPS, None, ALU.add).then_inc(rs.s, 1)
                pool.wait_ge(rs.s, rs.now(b, 1))
                pool.tensor_tensor(rstd[:], ve[:], mhalf[:], ALU.pow).then_inc(rs.s, 1)

            def rotated(b):
                pool.wait_ge(rots.s, rots.now(b, 5))
                pool.wait_ge(hmm.s, hmm.before(b, 1))
                y3 = ysc.rearrange("p (n c) -> p n c", c=C)
                pool.tensor_tensor(yc.rearrange("p (n c) -> p n c", c=C), y3,
                                   wide(cos_t[:], NCH), ALU.mult).then_inc(yrot.s, 1)
                pool.tensor_tensor(ys.rearrange("p (n c) -> p n c", c=C), y3,
                                   wide(sin_t[:], NCH), ALU.mult).then_inc(yrot.s, 1)

            def residual(b):
                pool.wait_ge(hgs.s, hgs.now(b, 1))
                pool.sem_inc(pool_held, 1)
                xb, yb = X[:, bass.ts(b, TT), :], Y[:, bass.ts(b, TT), :]
                pool.tensor_tensor(yb, xb, hg, ALU.add).then_inc(res.s, 1)
                pool.wait_ge(res.s, res.now(b, 1))
                pool.sem_inc(pool_held, 1)
                pool.tensor_tensor(xb, xb, yb, ALU.add).then_inc(res.s, 1)
                pool.wait_ge(res.s, res.now(b, 2))
                pool.sem_inc(pool_held, 1)
                pool.tensor_tensor(xb, xb, wide(row[:, R_M2:R_M2 + D], TT), ALU.add)\
                    .then_inc(res.s, 1)

            pool.wait_ge(w_one, W_ONE)
            root(ln1, rs1, 0, 2 * TT)
            with pool.Fori(1, B) as b:
                root(ln1, rs1, b, 2 * TT)
                rotated(b - 1)
                residual(b - 1)
            rotated(B - 1)
            residual(B - 1)
            root(ln2, rs2, 0, 2 * TT)
            with pool.Fori(0, B - 1) as b:
                root(ln2, rs2, b + 1, 2 * TT)
                root(ln3, rs3, b, 1 + 2 * TT)
            root(ln3, rs3, B - 1, 1 + 2 * TT)

            def split_k(b):
                src = kq.rearrange("p (a d) -> p a d", d=HD)
                d = st.rearrange("p t h s -> p (t h) s")
                pool.wait_ge(kvq.s, kvq.now(b, 2 * TT - 1))
                pool.wait_ge(stk.s, stk.before(b, TT))
                pool.sem_inc(pool_held, 1)
                pool.tensor_copy(d[:, :, 0:HD], src).then_inc(ksp.s, 1)
                pool.wait_ge(ksp.s, ksp.now(b, 1))
                pool.tensor_tensor(src, src, d[:, :, 0:HD], ALU.subtract).then_inc(ksp.s, 1)
                pool.wait_ge(ksp.s, ksp.now(b, 2))
                pool.sem_inc(pool_held, 1)
                pool.tensor_copy(d[:, :, HD:2 * HD], src).then_inc(ksp.s, 1)
                pool.wait_ge(ksp.s, ksp.now(b, 3))
                pool.tensor_tensor(d[:, :, 2 * HD:3 * HD], src, d[:, :, HD:2 * HD], ALU.subtract)\
                    .then_inc(ksp.s, 1)
                pool.tensor_copy(d[:, :, 3 * HD:5 * HD], d[:, :, 0:2 * HD]).then_inc(ksp.s, 1)
                pool.tensor_copy(d[:, :, 5 * HD:6 * HD], d[:, :, 0:HD]).then_inc(ksp.s, 1)

            for g in (xcp, ksp, msk, rs4):
                pool.sem_inc(g.s, g.per)
            with pool.Fori(0, B) as b:
                xb = X[:, bass.ts(b, TT), :]
                pool.wait_ge(ln3.s, ln3.now(b, 1 + 3 * TT))
                pool.wait_ge(tps.s, tps.before(b, 2))
                pool.sem_inc(pool_held, 1)
                pool.tensor_copy(xs, xb).then_inc(xcp.s, 1)
                pool.wait_ge(xcp.s, xcp.now(b, 1))
                pool.sem_inc(pool_held, 1)
                pool.tensor_tensor(xb, xb, wide(row[:, R_O:R_O + D], TT), ALU.add)\
                    .then_inc(xcp.s, 1)
                split_k(b)
                for n in range(NG * TT):
                    pool.wait_ge(exq.s, exq.now(b, 2 * n + 2))
                    pool.sem_inc(pool_held, 1)
                    pool.affine_select(out=pb[n % 2][:, :, 0:P], in_=pb[n % 2][:, :, 0:P],
                                       compare_op=ALU.is_ge, fill=0.0, base=0,
                                       pattern=[[0, GH], [1, P]], channel_multiplier=-1)\
                        .then_inc(msk.s, 1)
                root(ln4, rs4, b, 1 + 2 * TT)

            for g in (gix, six, added):
                pool.sem_inc(g.s, g.per * g.unit)
            pool.wait_ge(lge.s, lge.now(B - 1, 1))
            pool.wait_ge(tps.s, tps.now(B - 1, 2))
            pool.memset(off[0:64, :], 0.0).then_inc(offs, 1)
            pool.memset(off[64:P, :], float(B * T)).then_inc(offs, 1)
            pool.memset(pair_of, 0.0).then_inc(offs, 1)
            pool.wait_ge(offs, 3)
            pool.affine_select(out=pair_of, in_=pair_of, compare_op=ALU.not_equal, fill=1.0, base=0,
                               pattern=[[-1, 2], [0, CAP]], channel_multiplier=1).then_inc(offs, 1)
            pool.wait_ge(topk, TOPK)
            pool.wait_ge(zsum, 16)
            pool.wait_ge(x2o.s, x2o.now(B - 1, 2))

            def gather(p, u):
                pool.wait_ge(xgt.s, xgt.before(p - 1, 1))
                pool.sem_inc(pool_held, 1)
                pool.tensor_copy(gidx[u % 2], icol[:, bass.ds(p, 1)]).then_inc(gix.s, 1)
                pool.wait_ge(gix.s, gix.now(p, 1))
                pool.sem_inc(pool_held, 1)
                pool.indirect_dma_start(
                    xg[u % 2], None, x2_rows,
                    bass.IndirectOffsetOnAxis(ap=gidx[u % 2], axis=0)).then_inc(gathered[u % 2], 16)

            def scatter(p, u):
                pool.tensor_copy(sidx[u % 2], jcol[:, bass.ds(p, 1)]).then_inc(six.s, 1)
                pool.wait_ge(six.s, six.now(p, 1))
                pool.sem_inc(pool_held, 1)
                pool.wait_ge(yws.s, yws.now(p, 1))
                pool.sem_inc(pool_held, 1)
                pool.indirect_dma_start(
                    sums, bass.IndirectOffsetOnAxis(ap=sidx[u % 2], axis=0), ye[u % 2], None,
                    compute_op=ALU.add).then_inc(scattered, 16)

            def after_addition(p):
                pool.wait_ge(scattered, 16 * p)
                pool.sem_inc(added.s, 1)

            for p in range(2):
                pool.tensor_copy(gidx[p], icol[:, p:p + 1]).then_inc(gix.s, 1)
                pool.wait_ge(gix.s, gix.now(p, 1))
                pool.indirect_dma_start(
                    xg[p], None, x2_rows,
                    bass.IndirectOffsetOnAxis(ap=gidx[p], axis=0)).then_inc(gathered[p], 16)
            gather(2, 0)
            scatter(0, 0)
            with pool.Fori(0, NP // RING - 1) as r:
                for u in range(RING):
                    p = r * RING + (u + 1)
                    gather(p + 2, u + 1)
                    after_addition(p)
                    scatter(p, u + 1)
            for p in range(NP - RING + 1, NP):
                if p + 2 < NP:
                    gather(p + 2, p)
                after_addition(p)
                scatter(p, p)
            for b in range(B):
                pool.wait_ge(fin, b * (2 + 3 * TT) + 1 + 2 * TT)
                pool.tensor_scalar(ve[:], mv[:, :, 1], EPS, None, ALU.add).then_inc(froot, 1)
                pool.wait_ge(froot, 2 * b + 1)
                pool.tensor_tensor(rstd[:], ve[:], mhalf[:], ALU.pow).then_inc(froot, 1)

        @block.vector
        def _(dve):
            for g in (ln1, rots, gpre, hgs, ln2, ln3):
                dve.sem_inc(g.s, g.per)
            step = [0]

            def link(ins):
                step[0] += 1
                ins.then_inc(setup, 1)
                dve.wait_ge(setup, step[0])

            dve.wait_ge(consts, CONSTS)
            dve.wait_ge(w_one, W_ONE)
            link(dve.tensor_copy(ph, ph_i))
            link(dve.tensor_scalar(ph, ph, vec[:, V_FRQ:V_FRQ + 1], None, ALU.mult))
            for turn, dst in ((0.0, rot[:, 0:C]), (0.25, rot[:, C:2 * C])):
                link(dve.tensor_scalar(ph_n, ph, float(1 / (2 * np.pi)), turn, ALU.mult, ALU.add))
                link(dve.tensor_scalar(ph_n, ph_n, ROUND, None, ALU.add))
                link(dve.tensor_scalar(ph_n, ph_n, ROUND, None, ALU.subtract))
                link(dve.scalar_tensor_tensor(ph_m, ph_n, -TWO_PI_HI, ph, ALU.mult, ALU.add))
                link(dve.scalar_tensor_tensor(ph_m, ph_n, -TWO_PI_LO, ph_m, ALU.mult, ALU.add))
                link(dve.tensor_scalar(ph_m, ph_m, 2 * np.pi * turn, 3.1415925, ALU.add, ALU.min))
                link(dve.tensor_scalar(dst, ph_m, -3.1415925, None, ALU.max))
            dve.wait_ge(trig, 3)
            link(dve.tensor_scalar(decay, decay, mag, None, ALU.mult))
            link(dve.tensor_scalar(sin_t[0:NK, :], sin_t[0:NK, :], -1.0, None, ALU.mult))
            dve.wait_ge(wc_mm, 1)
            link(dve.tensor_copy(wc_s, bank(0).rearrange("p (k n) -> p k n", k=2)))
            assert step[0] == SETUP, step

            def norm(sig, rs, src, dst, first, k, before=None, at=None):
                b = first if at is None else at
                tile = lambda t: src[:, (0 if first is None else first * TT) + t, :]
                dve.sem_inc(dve_held, 1)
                for t in range(TT):
                    dve.bn_stats(stats[:, t, :], tile(t)).then_inc(sig.s, 1)
                dve.wait_ge(sig.s, sig.now(b, k + TT))
                dve.sem_inc(dve_held, 1)
                for t in range(TT):
                    dve.bn_aggr(mv[:, t, :], stats[:, t, :]).then_inc(sig.s, 1)
                dve.wait_ge(rs.s, rs.now(b, 2))
                if before is not None:
                    dve.wait_ge(before.s, before.before(b, 1))
                for t in range(TT):
                    dve.tensor_scalar(dst(t), tile(t),
                                      mv[:, t, 0:1], rstd[:, t:t + 1],
                                      ALU.subtract, ALU.mult).then_inc(sig.s, 1)

            def ln_in(b):
                dve.wait_ge(x_in.s, x_in.now(b, 1))
                norm(ln1, rs1, X, lambda t: xn[:, t, :], b, 0, xt1)

            def rotate(b):
                ps0 = bank(2).rearrange("p (n c) -> p n c", c=C)
                ps1 = bank(3).rearrange("p (n c) -> p n c", c=C)
                dve.wait_ge(beta.s, beta.now(b, 1))
                dve.tensor_tensor(rot.rearrange("p (n c) -> p n c", c=C), ps0,
                                  wide(cos_t[:], NCH), ALU.mult).then_inc(rots.s, 1)
                dve.tensor_tensor(rot2.rearrange("p (n c) -> p n c", c=C), ps1,
                                  wide(sin_t[:], NCH), ALU.mult).then_inc(rots.s, 1)
                dve.wait_ge(rots.s, rots.now(b, 2))
                dve.tensor_tensor(rot, rot, rot2, ALU.add).then_inc(rots.s, 1)
                dve.wait_ge(rots.s, rots.now(b, 3))
                dve.wait_ge(yrot.s, yrot.before(b, 2))
                dve.tensor_tensor_scan(ysc[:, ::-1], decay[:, ::-1], rot[:, ::-1], 0.0,
                                       ALU.mult, ALU.add).then_inc(rots.s, 1)
                dve.wait_ge(rots.s, rots.now(b, 4))
                first = ysc.rearrange("p (n c) -> p n c", c=C)[:, 1:, 0]
                dve.tensor_tensor(first, first, ps0[:, :NCH - 1, C - 1], ALU.add)\
                    .then_inc(rots.s, 1)

            def gate_in(b):
                dve.wait_ge(beta.s, beta.now(b, 2))
                dve.wait_ge(hgs.s, hgs.before(b, 1))
                dve.tensor_tensor(gz, bank(4, 2).rearrange("p (t n) -> p t n", t=TT),
                                  wide(row[:, R_GATE:R_GATE + D], TT), ALU.add)\
                    .then_inc(gpre.s, 1)

            def gate_out(b):
                dve.wait_ge(gact.s, gact.now(b, 1))
                dve.wait_ge(hmm.s, hmm.now(b, 1))
                dve.wait_ge(res.s, res.before(b, 1))
                dve.tensor_tensor(hg, bank(6, 2).rearrange("p (t n) -> p t n", t=TT), gz,
                                  ALU.mult).then_inc(hgs.s, 1)

            ln_in(0)
            with dve.Fori(1, B) as b:
                ln_in(b)
                rotate(b - 1)
                gate_in(b - 1)
                gate_out(b - 1)
            rotate(B - 1)
            gate_in(B - 1)
            gate_out(B - 1)

            def ln_mid(b):
                dve.wait_ge(res.s, res.now(b, 1))
                norm(ln2, rs2, Y, lambda t: xn[:, t, :], b, 0, xt2)

            def ln_out(b):
                dve.wait_ge(res.s, res.now(b, 3))
                dve.wait_ge(m2.s, m2.now(b, 1))
                xb = X[:, bass.ts(b, TT), :]
                dve.tensor_tensor(xb, bank(6, 2).rearrange("p (t n) -> p t n", t=TT), xb,
                                  ALU.add).then_inc(ln3.s, 1)
                dve.wait_ge(ln3.s, ln3.now(b, 1))
                norm(ln3, rs3, X, lambda t: X[:, b * TT + t, :], b, 1)

            ln_mid(0)
            with dve.Fori(0, B - 1) as b:
                ln_mid(b + 1)
                ln_out(b)
            ln_out(B - 1)

            for g in (kvq, qsp, sed, mxs, mneg, odv, ln4):
                dve.sem_inc(g.s, g.per)
            dve.wait_ge(ln3.s, ln3.now(B - 1, 1 + 3 * TT))
            dve.memset(Vb, 0.0).then_inc(vset, 1)
            dve.wait_ge(vset, 1)
            dve.memset(Vb[:, :, :, HD:HD + 1], 1.0).then_inc(vset, 1)

            def split_q(b):
                src = otok.rearrange("p t (h d) -> p (t h) d", d=HD)
                d = stq.rearrange("p t h s -> p (t h) s")
                at = lambda n: d[:, :, n * HD:(n + 1) * HD]
                dve.wait_ge(pvs.s, pvs.before(b, NG * TT))
                dve.wait_ge(kvq.s, kvq.now(b, 2 * TT + 1))
                dve.tensor_copy(at(0), src).then_inc(qsp.s, 1)
                dve.wait_ge(qsp.s, qsp.now(b, 1))
                dve.tensor_tensor(src, src, at(0), ALU.subtract).then_inc(qsp.s, 1)
                dve.wait_ge(qsp.s, qsp.now(b, 2))
                dve.tensor_copy(at(3), src).then_inc(qsp.s, 1)
                dve.wait_ge(qsp.s, qsp.now(b, 3))
                dve.tensor_tensor(at(5), src, at(3), ALU.subtract).then_inc(qsp.s, 1)
                dve.tensor_copy(at(1), at(0)).then_inc(qsp.s, 1)
                dve.tensor_copy(at(2), at(0)).then_inc(qsp.s, 1)
                dve.tensor_copy(at(4), at(3)).then_inc(qsp.s, 1)

            def half_stack(b, n, dst):
                dve.wait_ge(stk.s, stk.now(b, n + 1))
                t = n % TT
                dve.tensor_copy(dst[0:SK, NH // 2:, t * P:(t + 1) * P],
                                bank(3 + 2 * (n % 2)).bitcast(BF16)[0:SK, :]
                                .rearrange("p (h n) -> p h n", h=NH // 2)).then_inc(sed.s, 1)

            def maxima(b, g, i):
                for h in range(GH):
                    n = g * 16 + i * GH + h
                    dve.wait_ge(smm.s, smm.now(b, n + 1))
                    if g >= 2 and i == 0 and h == 0:
                        dve.wait_ge(mneg.s, mneg.now(b, 4 * (g - 1)))
                    if n >= 2:
                        dve.wait_ge(mxs.s, mxs.now(b, n - 1))
                    dve.sem_inc(dve_held, 1)
                    w = (i + 1) * P
                    dve.tensor_tensor_reduce(junk[:, n % 2, 0:w], bank(n % 2)[:, 0:w],
                                             causal[:, T - w:], 1.0, NEG, ALU.add, ALU.max,
                                             Mx[:, g % 2, i, h:h + 1]).then_inc(mxs.s, 1)

            def negate(b, g):
                m, d = Mx[:, g % 2], nst[:, g % 2]
                dve.wait_ge(mxs.s, mxs.now(b, 16 * (g + 1)))
                if g >= 2:
                    dve.wait_ge(ntp.s, ntp.now(b, g - 1))
                dve.tensor_scalar(d[:, :, 0, :], m, -1.0, None, ALU.mult).then_inc(mneg.s, 1)
                dve.wait_ge(mneg.s, mneg.now(b, 4 * g + 1))
                dve.scalar_tensor_tensor(Mr[:], m, -1.0, d[:, :, 0, :], ALU.mult, ALU.subtract)\
                    .then_inc(mneg.s, 1)
                dve.wait_ge(mneg.s, mneg.now(b, 4 * g + 2))
                dve.tensor_copy(d[:, :, 1, :], Mr[:]).then_inc(mneg.s, 1)
                dve.wait_ge(mneg.s, mneg.now(b, 4 * g + 3))
                dve.tensor_tensor(d[:, :, 2, :], Mr[:], d[:, :, 1, :], ALU.subtract)\
                    .then_inc(mneg.s, 1)

            def divide(b, g):
                o = bank(7).rearrange("p (t h v) -> p t h v", t=TT, h=GH)
                dve.wait_ge(otp.s, otp.now(b, g + 1))
                dve.reciprocal(rden[:], o[:, :, :, HD]).then_inc(odv.s, 1)
                dve.wait_ge(odv.s, odv.now(b, 2 * g + 1))
                dve.tensor_tensor(
                    otok[:, :, g * GH * HD:(g + 1) * GH * HD]
                    .rearrange("p t (h v) -> p t h v", h=GH), o[:, :, :, 0:HD],
                    rden[:].unsqueeze(3).to_broadcast([P, TT, GH, HD]), ALU.mult)\
                    .then_inc(odv.s, 1)

            with dve.Fori(0, B) as b:
                for t in range(TT):
                    dve.wait_ge(kvp.s, kvp.now(b, t + 1))
                    if t == 0:
                        dve.wait_ge(x2o.s, x2o.before(b, 2))
                    dve.tensor_tensor(kqt[:, t, :], bank(t % 2)[:, 0:D], row[:, R_K:R_K + D],
                                      ALU.add).then_inc(kvq.s, 1)
                    dve.tensor_tensor(Vb[:, t, :, 0:HD],
                                      bank(t % 2)[:, D:2 * D].rearrange("p (h d) -> p h d", h=NH),
                                      row[:, R_V:R_V + D].rearrange("p (h d) -> p h d", h=NH),
                                      ALU.add).then_inc(kvq.s, 1)
                dve.wait_ge(qpr.s, qpr.now(b, 1))
                dve.wait_ge(o2t.s, o2t.before(b, 1))
                dve.tensor_tensor(otok, bank(6, 2).rearrange("p (t n) -> p t n", t=TT),
                                  wide(row[:, R_Q:R_Q + D], TT), ALU.add).then_inc(kvq.s, 1)
                split_q(b)
                for n in range(2 * TT):
                    half_stack(b, n, KTs if n < TT else QTs)
                for i in range(TT):
                    maxima(b, 0, i)
                negate(b, 0)
                for g in range(NG):
                    for i in range(TT):
                        if g + 1 < NG:
                            maxima(b, g + 1, i)
                        if i == 1 and g > 0:
                            divide(b, g - 1)
                    if g + 1 < NG:
                        negate(b, g + 1)
                divide(b, NG - 1)
                dve.wait_ge(omm.s, omm.now(b, 1))
                dve.wait_ge(xcp.s, xcp.now(b, 2))
                dve.tensor_tensor(kqt, bank(4, 2).rearrange("p (t n) -> p t n", t=TT),
                                  X[:, bass.ts(b, TT), :], ALU.add).then_inc(ln4.s, 1)
                dve.wait_ge(ln4.s, ln4.now(b, 1))
                norm(ln4, rs4, kqt, lambda t: kqt[:, t, :], None, 1, at=b)

            for g in (hed, hbs, yws):
                dve.sem_inc(g.s, g.per)
            steps = [0]

            def then(ins):
                steps[0] += 1
                ins.then_inc(topk, 1)
                dve.wait_ge(topk, steps[0])

            dve.wait_ge(lge.s, lge.now(B - 1, 1))
            for a in range(2):
                then(dve.tensor_copy(LG2[64 * a:64 * a + 64, :].rearrange("p (b n) -> p b n", b=2),
                                     LGs[:, 2 * a:2 * a + 2, :]))
            for r in range(CAP // 8):
                v = top_v[:, 8 * r:8 * r + 8]
                then(dve.max(v, LG2))
                then(dve.max_index(top_i[:, 8 * r:8 * r + 8], v, LG2))
                if r + 1 < CAP // 8:
                    then(dve.match_replace(LG2, v, LG2, NEG))
            then(dve.tensor_copy(top_f, top_i))
            then(dve.tensor_scalar(top_f[64:P, :], top_f[64:P, :], float(B * T // 2), None, ALU.add))
            lo = slice(0, 64)
            then(dve.tensor_copy(far_v[lo, :], top_v[64:P, ::-1]))
            then(dve.tensor_copy(far_i[lo, :], top_f[64:P, ::-1]))
            then(dve.tensor_tensor(pick[lo, :], top_v[lo, :], far_v[lo, :], ALU.is_ge))
            then(dve.tensor_tensor(sel_v[lo, :], top_v[lo, :], far_v[lo, :], ALU.max))
            then(dve.tensor_tensor(sel_i[lo, :], top_f[lo, :], far_i[lo, :], ALU.subtract))
            then(dve.tensor_tensor(sel_i[lo, :], sel_i[lo, :], pick[lo, :], ALU.mult))
            then(dve.tensor_tensor(sel_i[lo, :], sel_i[lo, :], far_i[lo, :], ALU.add))
            then(dve.tensor_reduce(smx[lo, 0:1], sel_v[lo, :], AX.X, ALU.max))
            then(dve.tensor_scalar(smx[lo, 1:2], smx[lo, 0:1], -1.0, None, ALU.mult))
            shifted = steps[0]
            assert shifted == SHIFTED, shifted
            dve.wait_ge(wexp, 1)
            then(dve.reciprocal(smx[lo, 3:4], smx[lo, 2:3]))
            then(dve.tensor_scalar(sel_v[lo, :], sel_v[lo, :], smx[lo, 3:4], None, ALU.mult))
            for a in range(2):
                rows_a = slice(32 * a, 32 * a + 32)
                then(dve.tensor_copy(tw[:, CAP * a:CAP * a + CAP], sel_v[rows_a, :]))
                then(dve.tensor_copy(ti[:, CAP * a:CAP * a + CAP], sel_i[rows_a, :]))
            assert steps[0] == CHOSEN, steps
            dve.wait_ge(icm, 1)
            then(dve.tensor_copy(wcol, bank(0)[:, 0:NP]))
            then(dve.tensor_copy(icf, bank(0)[:, 32:32 + NP]))
            then(dve.tensor_copy(icol, icf))
            dve.wait_ge(offs, 4)
            then(dve.tensor_scalar(jcf, icf, off, None, ALU.add))
            then(dve.tensor_copy(jcol, jcf))
            assert steps[0] == TOPK, steps
            dve.wait_ge(b1_in, 16)

            def second_half(p):
                dve.wait_ge(h1m.s, h1m.now(p, 2))
                dve.wait_ge(htm.s, htm.before(p, 2))
                dve.tensor_copy(HB[:, 512:1024], bank(2)).then_inc(hed.s, 1)

            def hidden_bias(p):
                for a in range(2):
                    dve.wait_ge(htm.s, htm.now(p, a + 1))
                    if a == 0:
                        dve.wait_ge(y2m.s, y2m.before(p, 1))
                    dve.tensor_tensor(
                        hb[:, a * 512:(a + 1) * 512].rearrange("p (c n) -> p c n", c=8),
                        bank(3 + a).rearrange("p (c n) -> p c n", c=8),
                        b1_s[:, bass.ds(p, 1), 4 * a:4 * a + 4, :]
                        .rearrange("p e c a -> p (e c a)").unsqueeze(2).to_broadcast([P, 8, CAP]),
                        ALU.add).then_inc(hbs.s, 1)

            def weigh(p, u):
                dve.wait_ge(y2m.s, y2m.now(p, 1))
                dve.wait_ge(added.s, p + 1)
                dve.tensor_scalar(ye[u % 2], bank(5 + u % 2)[:, 0:D], wcol[:, bass.ds(p, 1)], None,
                                  ALU.mult).then_inc(yws.s, 1)

            second_half(0)
            hidden_bias(0)
            with dve.Fori(0, NP // RING - 1) as r:
                for u in range(RING):
                    p = r * RING + u
                    second_half(p + 1)
                    weigh(p, u)
                    hidden_bias(p + 1)
            for u in range(RING):
                p = NP - RING + u
                if p + 1 < NP:
                    second_half(p + 1)
                weigh(p, u)
                if p + 1 < NP:
                    hidden_bias(p + 1)

            steps[0] = 0

            def last(ins):
                steps[0] += 1
                ins.then_inc(fin, 1)
                dve.wait_ge(fin, steps[0])

            for b in range(B):
                dve.wait_ge(fin_in[b], 32)
                xb = X[:, b * TT:(b + 1) * TT, :]
                last(dve.tensor_tensor(xb, xb, Y[:, b * TT:(b + 1) * TT, :], ALU.add))
                for t in range(TT):
                    last(dve.bn_stats(stats[:, t, :], X[:, b * TT + t, :]))
                for t in range(TT):
                    last(dve.bn_aggr(mv[:, t, :], stats[:, t, :]))
                dve.wait_ge(froot, 2 * b + 2)
                for t in range(TT):
                    last(dve.tensor_scalar(X[:, b * TT + t, :], X[:, b * TT + t, :], mv[:, t, 0:1],
                                           rstd[:, t:t + 1], ALU.subtract, ALU.mult))
                last(dve.memset(smz[:], 0.0))

        @block.scalar
        def _(act):
            for g in (xe1, gact, xe2, silu):
                act.sem_inc(g.s, g.per)
            act.dma_start(vec[:], vecs).then_inc(w_one, 16)
            act.dma_start(row[:], rows.to_broadcast([P, RCOLS])).then_inc(w_one, 16)
            act.dma_start(wi_s, w_in.rearrange("(k p) n -> p k n", p=P)).then_inc(w_one, 16)
            act.dma_start(wout_s, w_out.rearrange("v p n -> p v n")).then_inc(w_one, 16)
            act.wait_ge(setup_cb, 1)
            for g in range(2 * CH):
                act.dma_start(cb_s[CK * g:CK * g + CK, CK * g:CK * g + CK],
                              coupling[g % CH]).then_inc(w_one, 16)
            act.dma_start(wg_s, w_gate.rearrange("(k p) n -> p k n", p=P)).then_inc(w_one, 16)
            act.dma_start(wm1_s, w_mlp1.rearrange("(k p) n -> p k n", p=P)).then_inc(w_mlp, 16)
            act.dma_start(wm2_s, w_mlp2.rearrange("(k p) n -> p k n", p=P)).then_inc(w_mlp, 16)
            act.dma_start(wkv_s[:], w_kv.rearrange("(k p) n -> p k n", p=P)).then_inc(w_att, 16)
            act.dma_start(wq_s[:], w_q.rearrange("(k p) n -> p k n", p=P)).then_inc(w_att, 16)
            act.dma_start(wo_s[:], w_o.rearrange("(k p) n -> p k n", p=P)).then_inc(w_att, 16)
            act.wait_ge(consts, CONSTS)
            act.dma_start(wr_s[:, :, 0:NP], w_r[0].rearrange("(k p) n -> p k n", p=P))\
                .then_inc(w_att, 16)
            act.dma_start(wr_s[:, :, 32:32 + NP], w_r[1].rearrange("(k p) n -> p k n", p=P))\
                .then_inc(w_att, 16)
            act.wait_ge(w_one, W_ONE)
            act.activation(mag, vec[:, V_DEC:V_DEC + 1], ACT.Sigmoid).then_inc(trig, 1)
            act.wait_ge(setup, 9)
            act.activation(sin_t[:], rot[:, 0:C], ACT.Sin).then_inc(trig, 1)
            act.wait_ge(setup, 16)
            act.activation(cos_t[:], rot[:, C:2 * C], ACT.Sin).then_inc(trig, 1)

            def turned(xt, xe, used, g, be, b):
                act.wait_ge(xt.s, xt.now(b, 1))
                act.wait_ge(used[0].s, used[0].before(b, used[1]))
                for k in range(KT):
                    act.activation(xT[:, k, :], bank(k), ACT.Identity, bias=vec[:, be + k:be + k + 1],
                                   scale=vec[:, g + k:g + k + 1]).then_inc(xe.s, 1)

            with act.Fori(0, B) as b:
                turned(xt1, xe1, (beta, 2), V_G1, V_B1, b)
                act.wait_ge(gpre.s, gpre.now(b, 1))
                act.activation(gz, gz, ACT.Sigmoid).then_inc(gact.s, 1)
            act.wait_ge(beta.s, beta.now(B - 1, 2))
            turned(xt2, xe2, (m1, MT), V_G2, V_B2, 0)
            def hidden(b):
                for m in range(MT):
                    act.wait_ge(m1.s, m1.now(b, m + 1))
                    act.wait_ge(m2.s, m2.before(b, 1))
                    act.activation(hid[:, m, :], bank(2 + m % 4), ACT.Silu,
                                   bias=vec[:, V_BM + m:V_BM + m + 1]).then_inc(silu.s, 1)
            with act.Fori(0, B - 1) as b:
                hidden(b)
                turned(xt2, xe2, (m1, MT), V_G2, V_B2, b + 1)
            hidden(B - 1)

            for g in (tev, sea, nte, exq, oev, o2e, x2e, lge):
                act.sem_inc(g.s, g.per)
            act.wait_ge(m2.s, m2.now(B - 1, 1))
            act.wait_ge(ln3.s, ln3.now(B - 1, 1 + 3 * TT))

            def half_stack(b, n, dst):
                act.wait_ge(stk.s, stk.now(b, n + 1))
                t = n % TT
                act.activation(dst[0:SK, 0:NH // 2, t * P:(t + 1) * P],
                               bank(2 + 2 * (n % 2)).bitcast(BF16)[0:SK, :]
                               .rearrange("p (h n) -> p h n", h=NH // 2), ACT.Copy)\
                    .then_inc(sea.s, 1)

            def minus_max(b, g):
                act.wait_ge(ntp.s, ntp.now(b, g + 1))
                act.activation(NT[:, g % 2, :], bank(7).bitcast(BF16)[0:NPC * GH, 0:T], ACT.Copy)\
                    .then_inc(nte.s, 1)

            def exponentials(b, g, j):
                n = g * TT + j
                w = T - j * P
                for hp in range(2):
                    act.wait_ge(stm.s, stm.now(b, 2 * n + hp + 1))
                    if n >= 2 and hp == 0:
                        act.wait_ge(pvs.s, pvs.now(b, n - 1))
                    act.activation(
                        pb[j % 2][:, 2 * hp:2 * hp + 2, 0:w],
                        bank(2 + 2 * hp, 2).rearrange("p (h n) -> p h n", h=2)[:, :, 0:w],
                        ACT.Exp, scale=float(HD) ** -0.5).then_inc(exq.s, 1)

            def group_out(b, g):
                act.wait_ge(pvs.s, pvs.now(b, TT * (g + 1)))
                if g == 0:
                    act.wait_ge(otp.s, otp.before(b, NG))
                else:
                    act.wait_ge(otp.s, otp.now(b, g))
                act.activation(oTs, bank(6), ACT.Copy).then_inc(oev.s, 1)

            with act.Fori(0, B) as b:
                act.wait_ge(tps.s, tps.now(b, 1))
                for k in range(KT):
                    act.activation(cT[:, k, :], bank(2 + k), ACT.Copy).then_inc(tev.s, 1)
                act.wait_ge(tps.s, tps.now(b, 2))
                for k in range(KT):
                    act.activation(aT[:, k, :], bank(4 + k), ACT.Copy).then_inc(tev.s, 1)
                for n in range(2 * TT):
                    half_stack(b, n, KTs if n < TT else QTs)
                minus_max(b, 0)
                for g in range(NG):
                    for j in range(TT):
                        exponentials(b, g, j)
                        if j == 0 and g > 0:
                            group_out(b, g - 1)
                    if g + 1 < NG:
                        minus_max(b, g + 1)
                group_out(b, NG - 1)
                act.wait_ge(o2t.s, o2t.now(b, 1))
                for k in range(KT):
                    act.activation(oT2[:, k, :], bank(2 + k), ACT.Copy).then_inc(o2e.s, 1)
                act.wait_ge(x2t.s, x2t.now(b, 1))
                for k in range(KT):
                    act.activation(x2T[:, k, :], bank(k), ACT.Copy).then_inc(x2e.s, 1)
                act.wait_ge(lgm.s, lgm.now(b, 1))
                act.activation(LGs[:, b, :], bank(6)[0:64, :], ACT.Copy).then_inc(lge.s, 1)

            for g in (xge, hea, gel):
                act.sem_inc(g.s, g.per)
            act.wait_ge(topk, SHIFTED)
            act.activation(sel_v[0:64, :], sel_v[0:64, :], ACT.Exp, bias=smx[0:64, 1:2],
                           accum_out=smx[0:64, 2:3]).then_inc(wexp, 1)

            def tokens(p):
                act.wait_ge(xgt.s, xgt.now(p, 1))
                act.wait_ge(h1m.s, h1m.before(p, 2))
                act.activation(xgT.rearrange("p k n -> p (k n)"), bank(0)[:, 0:KT * P], ACT.Copy)\
                    .then_inc(xge.s, 1)

            def first_half(p):
                act.wait_ge(h1m.s, h1m.now(p, 1))
                act.wait_ge(htm.s, htm.before(p, 1))
                act.activation(HB[:, 0:512], bank(1), ACT.Copy).then_inc(hea.s, 1)

            def gelu(p):
                for a in range(2):
                    act.wait_ge(hbs.s, hbs.now(p, a + 1))
                    act.activation(hb[:, a * 512:(a + 1) * 512], hb[:, a * 512:(a + 1) * 512],
                                   ACT.Gelu).then_inc(gel.s, 1)

            tokens(0)
            first_half(0)
            tokens(1)
            gelu(0)
            with act.Fori(0, NP // RING - 1) as r:
                for u in range(RING):
                    p = r * RING + u
                    first_half(p + 1)
                    tokens(p + 2)
                    gelu(p + 1)
            for u in range(RING):
                p = NP - RING + u
                if p + 1 < NP:
                    first_half(p + 1)
                if p + 2 < NP:
                    tokens(p + 2)
                if p + 1 < NP:
                    gelu(p + 1)

        @block.tensor
        def _(pe):
            for g in (xt1, beta, hmm, xt2, m1, m2):
                pe.sem_inc(g.s, g.per)
            pe.wait_ge(w_one, W_ONE)
            for v in range(2):
                mm = pe.matmul(PS[:, v * D:(v + 1) * D], cb_s, wout_s[:, v, :], start=True,
                               stop=True)
            mm.then_inc(wc_mm, 1)
            pe.wait_ge(consts, CONSTS)

            def turn(ln, xe, xt, b):
                pe.wait_ge(xe.s, xe.before(b, KT))
                for t in range(TT):
                    pe.wait_ge(ln.s, ln.now(b, 2 * TT + t + 1))
                    for j in range(KT):
                        mm = pe.transpose(bank(j)[:, t * P:(t + 1) * P],
                                          xn[:, t, j * P:(j + 1) * P], ident[:])
                mm.then_inc(xt.s, 1)

            def project(b):
                pe.wait_ge(xe1.s, xe1.now(b, KT))
                pe.wait_ge(rots.s, rots.before(b, 5))
                for v in range(2):
                    for k in range(KT):
                        mm = pe.matmul(bank(2 + v), wi_s[:, k, v * P:(v + 1) * P], xT[:, k, :],
                                       start=(k == 0), stop=(k == KT - 1))
                mm.then_inc(beta.s, 1)
                pe.wait_ge(gpre.s, gpre.before(b, 1))
                for t in range(TT):
                    for k in range(KT):
                        mm = pe.matmul(PS[:, 4 * 512 + t * D:4 * 512 + (t + 1) * D],
                                       xT[:, k, t * P:(t + 1) * P], wg_s[:, k, :],
                                       start=(k == 0), stop=(k == KT - 1))
                mm.then_inc(beta.s, 1)

            def mix(b):
                pe.wait_ge(yrot.s, yrot.now(b, 2))
                pe.wait_ge(hgs.s, hgs.before(b, 1))
                for t in range(TT):
                    for k, y in enumerate((yc, ys)):
                        mm = pe.matmul(PS[:, 6 * 512 + t * D:6 * 512 + (t + 1) * D],
                                       y[:, t * P:(t + 1) * P], wc_s[:, k, :],
                                       start=(k == 0), stop=(k == 1))
                mm.then_inc(hmm.s, 1)

            pe.wait_ge(setup, SETUP)
            turn(ln1, xe1, xt1, 0)
            project(0)
            with pe.Fori(1, B) as b:
                turn(ln1, xe1, xt1, b)
                mix(b - 1)
                project(b)
            mix(B - 1)

            def expand(b):
                pe.wait_ge(xe2.s, xe2.now(b, KT))
                for m in range(MT):
                    if m < 4:
                        pe.wait_ge(silu.s, silu.before(b, m + 5))
                    else:
                        pe.wait_ge(silu.s, silu.now(b, m - 3))
                    for k in range(KT):
                        mm = pe.matmul(bank(2 + m % 4), wm1_s[:, k, m * P:(m + 1) * P],
                                       xT[:, k, :], start=(k == 0), stop=(k == KT - 1))
                    mm.then_inc(m1.s, 1)

            def shrink(b):
                pe.wait_ge(silu.s, silu.now(b, MT))
                pe.wait_ge(ln3.s, ln3.before(b, 1))
                for t in range(TT):
                    for m in range(MT):
                        mm = pe.matmul(PS[:, 6 * 512 + t * D:6 * 512 + (t + 1) * D],
                                       hid[:, m, t * P:(t + 1) * P], wm2_s[:, m, :],
                                       start=(m == 0), stop=(m == MT - 1))
                mm.then_inc(m2.s, 1)

            pe.wait_ge(w_mlp, 32)
            pe.wait_ge(xe1.s, xe1.now(B - 1, KT))
            turn(ln2, xe2, xt2, 0)
            pe.wait_ge(gpre.s, gpre.now(B - 1, 1))
            pe.wait_ge(rots.s, rots.now(B - 1, 5))
            with pe.Fori(0, B - 1) as b:
                expand(b)
                turn(ln2, xe2, xt2, b + 1)
                shrink(b)
            expand(B - 1)
            shrink(B - 1)

            for g in (tps, kvp, qpr, stk, smm, ntp, stm, pvs, otp, o2t, omm, x2t, lgm):
                pe.sem_inc(g.s, g.per)
            pe.wait_ge(w_att, 16 * 5)
            pe.wait_ge(silu.s, silu.now(B - 1, MT))
            pe.wait_ge(ln3.s, ln3.now(B - 1, 1))
            pe.wait_ge(vset, 2)

            def turned(src, first):
                for t in range(TT):
                    for k in range(KT):
                        mm = pe.transpose(bank(first + k)[:, t * P:(t + 1) * P],
                                          src[:, t, k * P:(k + 1) * P], ident[:])
                return mm

            def stacks(b, n, src):
                if n < 2:
                    pe.wait_ge(tev.s, tev.now(b, 2 * KT))
                else:
                    pe.wait_ge(sea.s, sea.now(b, n - 1))
                    pe.wait_ge(sed.s, sed.now(b, n - 1))
                for h in range(NH):
                    ps = bank(2 + 2 * (n % 2) + h // 8).bitcast(BF16)
                    mm = pe.transpose(ps[0:SK, h % 8 * P:(h % 8 + 1) * P], src[:, n % TT, h, :],
                                      identb[:])
                mm.then_inc(stk.s, 1)

            def scores(b, g, i):
                for h in range(GH):
                    n = g * 16 + i * GH + h
                    if n >= 2:
                        pe.wait_ge(mxs.s, mxs.now(b, n - 1))
                    pe.matmul(bank(n % 2)[:, 0:(i + 1) * P],
                              QTs[0:SK, g * GH + h, i * P:(i + 1) * P],
                              KTs[0:SK, g * GH + h, 0:(i + 1) * P], start=True, stop=True)\
                        .then_inc(smm.s, 1)

            def minus_max(b, g):
                pe.wait_ge(mneg.s, mneg.now(b, 4 * (g + 1)))
                if g >= 2:
                    pe.wait_ge(odv.s, odv.now(b, 2 * (g - 1)))
                for i in range(TT):
                    mm = pe.transpose(bank(7).bitcast(BF16)[0:NPC * GH, i * P:(i + 1) * P],
                                      nst[:, g % 2, i].rearrange("p c h -> p (c h)"), identb[:])
                mm.then_inc(ntp.s, 1)

            def shifted(b, g, j):
                w = T - j * P
                for hp in range(2):
                    n = 2 * (g * TT + j) + hp
                    if n >= 2:
                        pe.wait_ge(exq.s, exq.now(b, n - 1))
                    if n % (2 * TT) == 0:
                        pe.wait_ge(nte.s, nte.now(b, g + 1))
                    for h in (2 * hp, 2 * hp + 1):
                        o = bank(2 + h)[:, 0:w]
                        pe.matmul(o, KTs[0:SK, g * GH + h, j * P:(j + 1) * P],
                                  QTs[0:SK, g * GH + h, j * P:T], start=True, stop=False)
                        mm = pe.matmul(o, sel[:, h, :], NT[:, g % 2, j * P:T], start=False,
                                       stop=True)
                    mm.then_inc(stm.s, 1)

            def values(b, g, j):
                n = g * TT + j
                pe.wait_ge(msk.s, msk.now(b, n + 1))
                if j == 0 and g > 0:
                    pe.wait_ge(oev.s, oev.now(b, g))
                for h in range(GH):
                    mm = pe.matmul(bank(6)[VW * h:VW * (h + 1), j * P:T], Vb[:, j, g * GH + h, :],
                                   pb[j % 2][:, h, 0:T - j * P], start=(j == 0),
                                   stop=(j == TT - 1))
                mm.then_inc(pvs.s, 1)

            def heads_out(b, g):
                pe.wait_ge(oev.s, oev.now(b, g + 1))
                if g + 1 < NG:
                    pe.wait_ge(nte.s, nte.now(b, g + 2))
                else:
                    pe.wait_ge(odv.s, odv.now(b, 2 * g))
                for t in range(TT):
                    mm = pe.transpose(bank(7)[:, t * P:(t + 1) * P], oTs[:, t * P:(t + 1) * P],
                                      ident[:])
                mm.then_inc(otp.s, 1)

            with pe.Fori(0, B) as b:
                pe.wait_ge(c_in.s, c_in.now(b, 1))
                pe.wait_ge(o2e.s, o2e.before(b, KT))
                turned(ctxb, 2).then_inc(tps.s, 1)
                pe.wait_ge(xcp.s, xcp.now(b, 1))
                pe.wait_ge(ln4.s, ln4.before(b, 1))
                turned(xs, 4).then_inc(tps.s, 1)
                pe.wait_ge(tev.s, tev.now(b, KT))
                pe.wait_ge(x2e.s, x2e.before(b, KT))
                for t in range(TT):
                    if t >= 2:
                        pe.wait_ge(kvq.s, kvq.now(b, 2 * t - 2))
                    for k in range(KT):
                        mm = pe.matmul(bank(t % 2), cT[:, k, t * P:(t + 1) * P], wkv_s[:, k, :],
                                       start=(k == 0), stop=(k == KT - 1))
                    mm.then_inc(kvp.s, 1)
                pe.wait_ge(tev.s, tev.now(b, 2 * KT))
                pe.wait_ge(lge.s, lge.before(b, 1))
                pe.wait_ge(odv.s, odv.before(b, 2 * NG))
                for t in range(TT):
                    for k in range(KT):
                        mm = pe.matmul(PS[:, 6 * 512 + t * D:6 * 512 + (t + 1) * D],
                                       aT[:, k, t * P:(t + 1) * P], wq_s[:, k, :],
                                       start=(k == 0), stop=(k == KT - 1))
                mm.then_inc(qpr.s, 1)
                pe.wait_ge(ksp.s, ksp.now(b, 6))
                for n in range(TT):
                    stacks(b, n, st)
                pe.wait_ge(qsp.s, qsp.now(b, 7))
                for n in range(TT, 2 * TT):
                    stacks(b, n, stq)
                pe.wait_ge(sea.s, sea.now(b, 2 * TT))
                pe.wait_ge(sed.s, sed.now(b, 2 * TT))
                for i in range(TT):
                    scores(b, 0, i)
                for g in range(NG):
                    minus_max(b, g)
                    for j in range(TT):
                        shifted(b, g, j)
                        if j == 2 and g > 0:
                            heads_out(b, g - 1)
                        if g + 1 < NG:
                            scores(b, g + 1, j)
                        if j > 0:
                            values(b, g, j - 1)
                    values(b, g, TT - 1)
                heads_out(b, NG - 1)
                pe.wait_ge(odv.s, odv.now(b, 2 * NG))
                turned(otok, 2).then_inc(o2t.s, 1)
                pe.wait_ge(o2e.s, o2e.now(b, KT))
                for t in range(TT):
                    for k in range(KT):
                        mm = pe.matmul(PS[:, 4 * 512 + t * D:4 * 512 + (t + 1) * D],
                                       oT2[:, k, t * P:(t + 1) * P], wo_s[:, k, :],
                                       start=(k == 0), stop=(k == KT - 1))
                mm.then_inc(omm.s, 1)
                pe.wait_ge(ln4.s, ln4.now(b, 1 + 3 * TT))
                turned(kqt, 0).then_inc(x2t.s, 1)
                pe.wait_ge(x2e.s, x2e.now(b, KT))
                for k in range(KT):
                    mm = pe.matmul(bank(6)[0:64, :], wr_s[:, k, :], x2T[:, k, :],
                                   start=(k == 0), stop=(k == KT - 1))
                mm.then_inc(lgm.s, 1)

            for g in (xgt, h1m, htm, y2m):
                pe.sem_inc(g.s, g.per)
            pe.wait_ge(topk, CHOSEN)
            pe.transpose(bank(0)[:, 0:32], tw, ident[0:32, 0:32])
            pe.transpose(bank(0)[:, 32:64], ti, ident[0:32, 0:32]).then_inc(icm, 1)
            pe.wait_ge(topk, TOPK)
            pe.wait_ge(lge.s, lge.now(B - 1, 1))

            def tokens(p, u, n):
                pe.wait_ge(gathered[u % 2], 16 * n)
                pe.wait_ge(xge.s, xge.before(p, 1))
                for k in range(KT):
                    mm = pe.transpose(bank(0)[:, k * P:(k + 1) * P],
                                      xg[u % 2][:, k * P:(k + 1) * P], ident[:])
                mm.then_inc(xgt.s, 1)

            def first(p, u, r):
                pe.wait_ge(xge.s, xge.now(p, 1))
                pe.wait_ge(w_ring[u].s, w_ring[u].now(r, 1))
                for n in range(2):
                    pe.wait_ge((hea, hed)[n].s, (hea, hed)[n].before(p, 1))
                    for k in range(KT):
                        for e in range(2):
                            mm = pe.matmul(bank(1 + n)[CAP * e:CAP * (e + 1), :],
                                           xgT[:, k, CAP * e:CAP * (e + 1)],
                                           w1_of[u][:, e, k, n * 512:(n + 1) * 512],
                                           start=(k == 0), stop=(k == KT - 1))
                    mm.then_inc(h1m.s, 1)

            def across(p):
                for a in range(2):
                    pe.wait_ge((hea, hed)[a].s, (hea, hed)[a].now(p, 1))
                    pe.wait_ge(hbs.s, hbs.before(p, a + 1))
                    for c in range(4):
                        n = 4 * a + c
                        mm = pe.transpose(bank(3 + a)[:, c * P:(c + 1) * P],
                                          HB[:, n * P:(n + 1) * P], ident[:])
                    mm.then_inc(htm.s, 1)

            def second(p, u, r):
                pe.wait_ge(b_ring[u].s, b_ring[u].now(r, 1))
                pe.wait_ge(gel.s, gel.now(p, 2))
                pe.wait_ge(yws.s, yws.before(p, 1))
                y = bank(5 + u % 2)
                pe.matmul(y[:, 0:D], pair_of, b2_s[u], start=True, stop=False,
                          skip_group_check=True)
                for sl in range(S):
                    for m in range(M2 // P):
                        c = sl * (M2 // P) + m
                        for e in range(2):
                            mm = pe.matmul(y[CAP * e:CAP * (e + 1), sl * KO:(sl + 1) * KO],
                                           hb[:, c * P + CAP * e:c * P + CAP * (e + 1)],
                                           w2_of[u][:, e, sl, m, :], start=False,
                                           stop=(m == M2 // P - 1), skip_group_check=True)
                mm.then_inc(y2m.s, 1)

            pe.wait_ge(offs, 4)
            tokens(0, 0, 1)
            first(0, 0, 0)
            tokens(1, 1, 1)
            across(0)
            with pe.Fori(0, NP // RING - 1) as r:
                for u in range(RING):
                    p = r * RING + u
                    v = (u + 1) % RING
                    first(p + 1, v, r + (u + 1) // RING)
                    tokens(p + 2, u, r * (RING // 2) + (u // 2 + 2))
                    second(p, u, r)
                    across(p + 1)
            r = NP // RING - 1
            for u in range(RING):
                p = NP - RING + u
                if p + 1 < NP:
                    first(p + 1, u + 1, r)
                if p + 2 < NP:
                    tokens(p + 2, u, r * (RING // 2) + (u // 2 + 2))
                second(p, u, r)
                if p + 1 < NP:
                    across(p + 1)


def kernel(**inputs):
    from concourse import bacc as _bacc
    from concourse.bass_utils import run_bass_kernel_spmd as _run

    i = {k: np.asarray(v) for k, v in inputs.items()}
    w = lambda n: i["L0_" + n]
    col = lambda v: v.reshape(-1, P).T
    twice = lambda v: np.concatenate([v, v])[:, None]
    swap = lambda m: np.concatenate([m[NK:], m[:NK]])
    wi, wo = w("attn_w_in"), w("attn_w_out").T
    w1 = w("ffn_W1").reshape(NP, 2, S, KT, P, M2).transpose(0, 4, 1, 3, 2, 5).reshape(NP, P, W1C)
    w2 = w("ffn_W2").reshape(NP, 2, S, M2 // P, P, KO).transpose(0, 4, 1, 2, 3, 5)\
        .reshape(NP, P, W2C)
    arrays = {
        "x": i["x"], "ctx_in": i["ctx_1024"],
        "w_in": np.concatenate([wi, swap(wi)]).T,
        "w_gate": w("attn_w_gate").T,
        "w_out": np.stack([wo, swap(wo)]),
        "coupling": w("attn_coupling"),
        "w_mlp1": w("attn_w_mlp1").T, "w_mlp2": w("attn_w_mlp2").T,
        "w_q": w("xattn_wq_w").T,
        "w_kv": np.concatenate([w("xattn_wk_w"), w("xattn_wv_w")]).T,
        "w_o": w("xattn_wo_w").T,
        "w_r": np.stack([w("ffn_Wr")[0::2].T, w("ffn_Wr")[1::2].T]),
        "vecs": np.concatenate([col(w("attn_ln1_g")), col(w("attn_ln1_b")), col(w("attn_ln2_g")),
                                col(w("attn_ln2_b")), col(w("attn_b_mlp1")),
                                twice(w("attn_log_decay")), twice(w("attn_frequency"))], axis=1),
        "rows": np.concatenate([w("attn_b_gate"), w("attn_b_mlp2"), w("xattn_wk_b"),
                                w("xattn_wv_b"), w("xattn_wq_b"), w("xattn_wo_b")])[None],
        "b1": w("ffn_b1").reshape(NP, 2, S * M2 // P, P).transpose(3, 0, 2, 1),
        "b2": w("ffn_b2").reshape(NP, 2, D),
        "experts": np.concatenate([w1, w2], axis=2),
    }
    arrays = {n: np.ascontiguousarray(a) for n, a in arrays.items()}
    nc = _bacc.Bacc("TRN2", target_bir_lowering=False, num_devices=1)
    args = [nc.dram_tensor(n, a.shape, mybir.dt.from_np(a.dtype), kind="ExternalInput").ap()
            for n, a in arrays.items()]
    out = nc.dram_tensor("out", (B, T, D), F32, kind="ExternalOutput").ap()
    build(nc, *args, out)
    return _run(nc, [arrays], core_ids=[0]).results[0]["out"]
```

```python
from contextlib import ExitStack

import numpy as np
import concourse.bass as bass
from concourse import mybir

F32 = mybir.dt.float32
BF16 = mybir.dt.bfloat16
U32 = mybir.dt.uint32
I32 = mybir.dt.int32
ALU = mybir.AluOpType
ACT = mybir.ActivationFunctionType
AX = mybir.AxisListType

P = 128
B, T, D = 4, 512, 256
TT = T // P
KT = D // P
NK = 64
C = 64
NCH = T // C
CH, CK = 4, 16
MLP = 1024
MT = MLP // P
NH, HD = 16, 16
GH = 4
NG = NH // GH
NPC = 3
NPR = 6
SK = NPR * HD
SX = SK + NPC
VW = 32
E, S = 48, 4
M2 = 256
KO = D // S
CAP = int(1.5 * B * T / E)
NP = E // 2
RING = 6
W1C = 2 * KT * S * M2
W2C = 2 * S * (M2 // P) * KO
EPS = 1e-5
NEG = -3.0e38
SHARED = [[(0,), (1,), (2,), (3,)], [(0,), (1,), (2,), (3,)], [(0, 1), (2, 3)], [(0, 1, 2, 3)]]
FIRST = [0, 4, 8, 10]
NSH = 11
SCORED = [(0, 1), (2,), (3,), ()]
PREPARE = {
    (1, 0): ([], [("context", 0), ("context", 1)], [("query_in", 0), ("query_in", 1)]),
    (1, 1): ([("key", 0)], [("key", 1)], [("split_k", 0)]),
    (1, 2): ([("query", 0), ("split_k", 1), ("split_k", 2)], [("query", 1)],
             [("split_k", 3), ("split_k", 4), ("split_q", 0)]),
    (1, 3): ([("split_q", 1), ("split_q", 2)], [("split_q", 3)], []),
    (2, 0): ([], [("value", 0)], []),
    (2, 1): ([("stack_k", 0)], [("stack_k", 1)], []),
    (2, 2): ([("stack_q", 0)], [("stack_q", 1)], []),
    (2, 3): ([("stack_k", 2)], [], []),
    (3, 0): ([], [("stack_k", 3)], []),
    (3, 1): ([("stack_q", 2)], [("stack_q", 3)], []),
    (3, 2): ([("stack_k", 4)], [("stack_k", 5)], []),
    (3, 3): ([("stack_q", 4)], [("stack_q", 5)], []),
}
ENTER = {
    (0, 0): ([], [("value", 1)], []),
    (0, 2): ([("stack_k", 6)], [("stack_k", 7)], []),
    (0, 3): ([("stack_q", 6)], [("stack_q", 7)], []),
}
FINISH = {
    (0, 0): ([], [], [("heads", 0), ("heads", 1)]),
    (0, 1): ([], [("output", 0)], [("output", 1)]),
    (0, 3): ([], [], [("turn", 0), ("turn", 1), ("logits", 0)]),
}
TWO_PI_HI = 6.28125
TWO_PI_LO = 2 * np.pi - 6.28125
ROUND = 12582912.0

V_G1, V_B1, V_G2, V_B2, V_BM, V_DEC, V_FRQ = 0, 2, 4, 6, 8, 16, 17
VCOLS = 18
R_GATE, R_M2, R_K, R_V, R_Q, R_O = (256 * n for n in range(6))
RCOLS = 6 * 256


class Signal:

    def __init__(self, sem, per, unit=1):
        self.s, self.per, self.unit = sem, per, unit

    def now(self, b, k):
        return (b * self.per + (self.per + k)) * self.unit

    def before(self, b, k):
        return (b * self.per + k) * self.unit


def build(nc, x, ctx_in, w_in, w_gate, w_out, coupling, w_mlp1, w_mlp2, w_q, w_kv, w_o, w_r,
          vecs, rows, b1, b2, experts, out):
    x2_rows = nc.dram_tensor("x2_rows", (B * T, D), F32, kind="Internal").ap()
    sums = nc.dram_tensor("sums", (2 * B * T, D), F32, kind="Internal").ap()

    stack = ExitStack()
    with stack:
        def sb(name, shape, dt=F32):
            return stack.enter_context(nc.sbuf_tensor(name, shape, dt))

        def sem(name):
            return stack.enter_context(nc.semaphore(name))

        def signal(name, per, unit=1):
            s = Signal(sem(name), per, unit)
            signals.append(s)
            return s

        signals = []

        PS = stack.enter_context(nc.psum_tensor("PS", [P, 8 * 512], F32))

        def bank(n, k=1):
            return PS[:, n * 512:(n + k) * 512]

        X = sb("X", [P, B * TT, D])
        Y = sb("Y", [P, B * TT, D])
        A = sb("arena", [P, 20992])
        ring_a = sb("ring_a", [P, 3, W1C + W2C])
        ident = sb("ident", [P, P])
        identb = sb("identb", [P, P], BF16)
        cos_t = sb("cos_t", [P, C])
        sin_t = sb("sin_t", [P, C])
        vec = sb("vec", [P, VCOLS])
        row = sb("row", [P, RCOLS])
        wq_s = sb("wq_s", [P, KT, D])
        wkv_s = sb("wkv_s", [P, KT, 2 * D])
        wo_s = sb("wo_s", [P, KT, D])
        wr_s = sb("wr_s", [P, KT, 64])
        stats = sb("stats", [P, TT, 6])
        mv = sb("mv", [P, TT, 2])
        ve = sb("ve", [P, TT])
        rstd = sb("rstd", [P, TT])
        mhalf = sb("mhalf", [P, TT])
        causal = sb("causal", [P, T], BF16)
        junk = sb("junk", [P, 2, T], BF16)
        Mx = sb("Mx", [P, 2, TT, GH])
        Mr = sb("Mr", [P, TT, GH])
        nst = sb("nst", [P, 2, TT, GH, NPC], BF16)
        zrow = sb("zrow", [P, D])
        smz = sb("smz", [P, 1])
        rden = sb("rden", [P, TT, GH])

        used = [0]

        def carve(n):
            a = used[0]
            used[0] += n
            assert used[0] <= 20992, used
            return A[:, a:a + n]

        wi_s = carve(KT * 256).rearrange("p (k n) -> p k n", k=KT)
        wg_s = carve(KT * D).rearrange("p (k n) -> p k n", k=KT)
        wm1_s = carve(KT * MLP).rearrange("p (k n) -> p k n", k=KT)
        wm2_s = carve(MT * D).rearrange("p (k n) -> p k n", k=MT)
        wc_s = carve(2 * D).rearrange("p (k n) -> p k n", k=2)
        wout_s = carve(2 * D).rearrange("p (k n) -> p k n", k=2)
        cb_s = carve(P)
        decay = carve(T)
        rot = carve(T)
        rot2 = carve(T)
        ysc = carve(T)
        yc = carve(T)
        ys = carve(T)
        xT = carve(KT * T).rearrange("p (k n) -> p k n", k=KT)
        gz = carve(TT * D).rearrange("p (t n) -> p t n", t=TT)
        hg = carve(TT * D).rearrange("p (t n) -> p t n", t=TT)
        hid = carve(MT * T).rearrange("p (k n) -> p k n", k=MT)
        ph_i = carve(C).bitcast(I32)
        ph = carve(C)
        ph_n = carve(C)
        ph_m = carve(C)
        mag = carve(1)
        xn = carve(TT * D).rearrange("p (t n) -> p t n", t=TT)
        used[0] = 0
        cT = carve(KT * T).rearrange("p (k n) -> p k n", k=KT)
        aT = carve(KT * T).rearrange("p (k n) -> p k n", k=KT)
        kq = carve(TT * D)
        Vb = carve(TT * NH * VW).rearrange("p (t h v) -> p t h v", t=TT, h=NH)
        st = carve(TT * NH * SK // 2).bitcast(BF16).rearrange("p (t h s) -> p t h s", t=TT, h=NH)
        KTs = carve(NH * T // 2).bitcast(BF16).rearrange("p (h n) -> p h n", h=NH)
        QTs = carve(NH * T // 2).bitcast(BF16).rearrange("p (h n) -> p h n", h=NH)
        pbs = carve(2 * GH * T)
        pb = [pbs[:, n * GH * T:(n + 1) * GH * T].rearrange("p (h n) -> p h n", h=GH)
              for n in range(2)]
        over = ring_a[:, 0, :]
        stq = over[:, 0:TT * NH * SK // 2].bitcast(BF16)\
            .rearrange("p (t h s) -> p t h s", t=TT, h=NH)
        qt = over[:, TT * NH * SK // 2:TT * NH * SK // 2 + TT * D]
        x2b = over[:, TT * NH * SK // 2 + TT * D:TT * NH * SK // 2 + 2 * TT * D]\
            .rearrange("p (t n) -> p t n", t=TT)
        oTs = carve(T)
        yr = Y[:, :, :].rearrange("p a d -> p (a d)")
        ctxb = yr[:, 0:1024].rearrange("p (t n) -> p t n", t=TT)
        otok = yr[:, 1024:2048].rearrange("p (t n) -> p t n", t=TT)
        oT2 = yr[:, 2048:3072].rearrange("p (k n) -> p k n", k=KT)
        xs = yr[:, 3072:4096].rearrange("p (t n) -> p t n", t=TT)
        x2T = aT
        LGs = sb("LGs", [64, B, T])
        used[0] = 0
        ring_b = [carve(W1C + W2C) for _ in range(3)]
        slot = [ring_a[:, n, :] for n in range(3)] + ring_b
        w1_of = [s_[:, 0:W1C].rearrange("p (e k n) -> p e k n", e=2, k=KT) for s_ in slot]
        w2_of = [s_[:, W1C:].rearrange("p (e s m k) -> p e s m k", e=2, s=S, m=M2 // P)
                 for s_ in slot]
        xr_ = X[:, :, :].rearrange("p a d -> p (a d)")
        LG2 = yr[:, 0:1024]
        top_v = yr[:, 1024:1088]
        top_i = yr[:, 1088:1152].bitcast(U32)
        top_f = yr[:, 1152:1216]
        pick = yr[:, 1216:1280]
        sel_v = yr[:, 1280:1344]
        sel_i = yr[:, 1344:1408]
        far_v = yr[:, 1408:1472]
        far_i = yr[:, 1472:1536]
        tw = yr[0:32, 1536:1664]
        ti = yr[0:32, 1664:1792]
        smx = yr[:, 1792:1800]
        wcol = yr[:, 1800:1824]
        icol = yr[:, 1824:1848].bitcast(U32)
        jcol = yr[:, 1848:1872].bitcast(U32)
        icf = yr[:, 1872:1896]
        jcf = yr[:, 1896:1920]
        off = yr[:, 1920:1921]
        b1_s = yr[:, 2048:2432].rearrange("p (e c a) -> p e c a", e=NP, a=2)
        pair_of = yr[0:2, 2432:2560]
        HB = xr_[:, 0:1024]
        hb = xr_[:, 1024:2048]
        b2_s = [xr_[0:2, 2048 + n * D:2048 + (n + 1) * D] for n in range(4)]
        b2_s += [yr[0:2, 3072 + n * D:3072 + (n + 1) * D] for n in range(2)]
        xg = [carve(D) for _ in range(RING)]
        xgT = xr_[:, 3584:3840].rearrange("p (k n) -> p k n", k=KT)
        ye = [carve(D) for _ in range(3)]
        gidx = [carve(1).bitcast(U32) for _ in range(RING)]
        sidx = [carve(1).bitcast(U32) for _ in range(3)]
        fstats = carve(B * TT * 6).rearrange("p (a n) -> p a n", n=6)
        fmv = carve(B * TT * 2).rearrange("p (a n) -> p a n", n=2)
        fve = carve(B * TT)
        frstd = carve(B * TT)
        fshift = carve(B * TT)


        w_one = sem("w_one")
        w_mlp = sem("w_mlp")
        w_att = sem("w_att")
        consts = sem("consts")
        setup = sem("setup")
        trig = sem("trig")
        wc_mm = sem("wc_mm")
        x_in = signal("x_in", 1, 16)
        ln1 = signal("ln1", 2 * TT + TT)
        rs1 = signal("rs1", 2)
        xt1 = signal("xt1", 1)
        xe1 = signal("xe1", 2)
        beta = signal("beta", 2)
        rots = signal("rots", 5)
        gpre = signal("gpre", 1)
        gact = signal("gact", 1)
        yrot = signal("yrot", 2)
        hmm = signal("hmm", 1)
        hgs = signal("hgs", 1)
        res = signal("res", 3)
        ln2 = signal("ln2", 3 * TT)
        rs2 = signal("rs2", 2)
        xt2 = signal("xt2", 1)
        xe2 = signal("xe2", 2)
        m1 = signal("m1", MT)
        silu = signal("silu", MT)
        m2 = signal("m2", 1)
        ln3 = signal("ln3", 1 + 3 * TT)
        rs3 = signal("rs3", 2)
        c_in = signal("c_in", 1, 16)
        xs_in = signal("xs_in", 1, 16)
        xob = signal("xob", 1)
        ctp = signal("ctp", KT)
        cte = signal("cte", KT)
        xtp = signal("xtp", KT)
        xte = signal("xte", KT)
        kpr = signal("kpr", 2)
        kev = signal("kev", 2)
        qpr = signal("qpr", 2)
        qev = signal("qev", 2)
        vpr = signal("vpr", 2)
        vev = signal("vev", 2)
        ksa = signal("ksa", 4)
        ksd = signal("ksd", 2)
        qsa = signal("qsa", 2)
        qsd = signal("qsd", 5)
        skt = signal("skt", 2 * NG)
        ske = signal("ske", 2 * NG)
        sqt = signal("sqt", 2 * NG)
        sqe = signal("sqe", 2 * NG)
        smm = signal("smm", NG * 16)
        mxs = signal("mxs", NG * 16)
        mneg = signal("mneg", NG * 4)
        ntp = signal("ntp", NG * 2)
        nte = signal("nte", NG * 2)
        stm = signal("stm", NG * NSH)
        exq = signal("exq", NG * NSH)
        msk = signal("msk", NG * TT)
        pvs = signal("pvs", NG * TT)
        oev = signal("oev", NG)
        otp = signal("otp", NG)
        odv = signal("odv", NG * 2)
        o2t = signal("o2t", KT)
        o2e = signal("o2e", KT)
        omm = signal("omm", 2)
        ln4 = signal("ln4", 2 + 3 * TT)
        rs4 = signal("rs4", 2)
        x2t = signal("x2t", KT)
        x2e = signal("x2e", KT)
        lgm = signal("lgm", 1)
        lge = signal("lge", 1)
        x2o = signal("x2o", 2, 16)
        zsum = sem("zsum")
        b1_in = sem("b1_in")
        topk = sem("topk")
        wexp = sem("wexp")
        icm = sem("icm")
        w_ring = [signal(f"w_ring{n}", 1, 16) for n in range(RING)]
        b_ring = [signal(f"b_ring{n}", 1, 16) for n in range(RING)]
        gix = signal("gix", 1)
        six = signal("six", 1)
        gathered = [sem(f"gathered{n}") for n in range(RING)]
        scattered = sem("scattered")
        added = signal("added", 3)
        xgt = signal("xgt", 1)
        xge = signal("xge", 1)
        h1m = signal("h1m", 2)
        hea = signal("hea", 1)
        hed = signal("hed", 1)
        htm = signal("htm", 2)
        hbs = signal("hbs", 2)
        gel = signal("gel", 2)
        y2m = signal("y2m", 1)
        yws = signal("yws", 1)
        fin_in = [sem(f"fin_in{n}") for n in range(B)]
        fsum = sem("fsum")
        fstat = sem("fstat")
        fvar = sem("fvar")
        froot = sem("froot")
        fout = sem("fout")
        stored = sem("stored")
        vset = sem("vset")
        pool_held = sem("pool_held")
        dve_held = sem("dve_held")
        setup_cb = sem("setup_cb")
        offs = sem("offs")
        SHIFTED, CHOSEN, TOPK = 36, 42, 47
        CONSTS, SETUP, W_ONE = 12, 19, 16 * 13

        x_v = x.rearrange("b (t p) d -> b p t d", p=P)
        ctx_v = ctx_in.rearrange("b (t p) d -> b p t d", p=P)
        out_v = out.rearrange("b (t p) d -> p (b t) d", p=P)
        x2_v = x2_rows.rearrange("(b t p) d -> b p t d", p=P, b=B)
        sums_v = sums.rearrange("(a b t p) d -> a b p t d", p=P, b=B, a=2)

        def wide(ap, n):
            return ap.unsqueeze(1).to_broadcast([ap.shape[0], n, ap.shape[1]])

        def spare(k):
            return bank((5, 7)[k % 2])

        def slots(b, do, first=False, last=False):
            for g in ([0] if first else range(1, NG) if last else [1, 2, 3, 0]):
                c = b + 1 if g == 0 and not first else b
                prev = None if first else (c, g - 1) if g > 0 else (b, NG - 1)
                then = None if last and g == NG - 1 else (c, g + 1) if g + 1 < NG else (c + 1, 0)
                for j in range(TT):
                    tables = []
                    if not first and not last:
                        tables.append((PREPARE, b + 1))
                        tables.append((FINISH, b))
                    if g == 0:
                        tables.append((ENTER, c))
                    steps = [], [], []
                    for table, batch in tables:
                        for n, names in enumerate(table.get((g, j), steps[:0])):
                            steps[n].extend((name, batch, k) for name, k in names)
                    do(c, g, j, prev, then, *steps)

        def all_steps(table):
            return [step for lists in table.values() for names in lists for step in names]

        block = stack.enter_context(nc.Block())

        @block.sync
        def _(sp):
            sp.sem_inc(x_in.s, 16)
            with sp.Fori(0, B) as b:
                sp.wait_ge(x_in.s, x_in.before(b, 1))
                sp.dma_start(X[:, bass.ts(b, TT), :], x_v[b]).then_inc(x_in.s, 16)

            for u in (1, 2):
                sp.dma_start(slot[u], experts[u]).then_inc(w_ring[u].s, 16)
            sp.wait_ge(consts, CONSTS)
            sp.dma_start(sums[B * T:, :].rearrange("(a p) d -> p a d", p=P), wide(zrow[:], B * TT))\
                .then_inc(zsum, 16)
            sp.sem_inc(c_in.s, 16)
            sp.sem_inc(xs_in.s, 16)
            sp.sem_inc(x2o.s, 32)

            def inputs(b):
                sp.wait_ge(ctp.s, ctp.before(b, KT))
                sp.dma_start(ctxb, ctx_v[b]).then_inc(c_in.s, 16)
                sp.wait_ge(ln3.s, ln3.now(b, 1 + 3 * TT))
                sp.wait_ge(xtp.s, xtp.before(b, KT))
                sp.dma_start(xs, X[:, bass.ts(b, TT), :]).then_inc(xs_in.s, 16)

            def outputs(b):
                sp.wait_ge(ln4.s, ln4.now(b, 2 + 3 * TT))
                sp.dma_start(x2_v[b], x2b).then_inc(x2o.s, 16)
                sp.dma_start(sums_v[0, b], x2b).then_inc(x2o.s, 16)

            sp.wait_ge(ln2.s, ln2.now(B - 1, 3 * TT))
            inputs(0)
            with sp.Fori(0, B - 1) as b:
                inputs(b + 1)
                outputs(b)
            outputs(B - 1)

            for g in w_ring + b_ring:
                sp.sem_inc(g.s, 16)
            sp.wait_ge(lge.s, lge.now(B - 1, 1))
            sp.dma_start(b1_s, b1).then_inc(b1_in, 16)
            sp.wait_ge(x2o.s, x2o.now(B - 1, 2))
            sp.wait_ge(x2t.s, x2t.now(B - 1, KT))
            for u in range(RING):
                if u not in (1, 2):
                    sp.dma_start(slot[u], experts[u]).then_inc(w_ring[u].s, 16)
                sp.dma_start(b2_s[u], b2[u]).then_inc(b_ring[u].s, 16)
            with sp.Fori(1, NP // RING) as r:
                for u in range(RING):
                    sp.wait_ge(y2m.s, y2m.now((r - 1) * RING + u, 1))
                    sp.dma_start(slot[u], experts[r * RING + u]).then_inc(w_ring[u].s, 16)
                    sp.dma_start(b2_s[u], b2[r * RING + u]).then_inc(b_ring[u].s, 16)
            sp.wait_ge(scattered, 16 * NP)
            for b in range(B):
                sp.dma_start(X[:, b * TT:(b + 1) * TT, :], sums_v[0, b]).then_inc(fin_in[b], 16)
                sp.dma_start(Y[:, b * TT:(b + 1) * TT, :], sums_v[1, b]).then_inc(fin_in[b], 16)
            for b in range(B):
                sp.wait_ge(fout, (b + 1) * TT)
                sp.dma_start(out_v[:, b * TT:(b + 1) * TT, :], X[:, b * TT:(b + 1) * TT, :])\
                    .then_inc(stored, 16)
            sp.wait_ge(stored, 16 * B)

        @block.gpsimd
        def _(pool):
            for g in (rs1, yrot, res, rs2, rs3):
                pool.sem_inc(g.s, g.per)
            step = [0]

            def const(ins):
                step[0] += 1
                ins.then_inc(consts, 1)

            def settle():
                pool.wait_ge(consts, step[0])

            const(pool.memset(ident[:], 0.0))
            pool.memset(cb_s, 0.0).then_inc(setup_cb, 1)
            const(pool.memset(identb[:], 0.0))
            const(pool.memset(causal[:], 0.0))
            const(pool.memset(mhalf[:], -0.5))
            const(pool.memset(wr_s[:], 0.0))
            const(pool.memset(zrow[:], 0.0))
            const(pool.memset(decay, 1.0))
            const(pool.iota(ph_i, pattern=[[1, C]], base=0, channel_multiplier=0))
            settle()
            for m in (ident, identb):
                const(pool.affine_select(out=m[:], in_=m[:], compare_op=ALU.not_equal, fill=1.0,
                                         base=0, pattern=[[-1, P]], channel_multiplier=1))
            const(pool.affine_select(out=causal[:, T - P:], in_=causal[:, T - P:],
                                     compare_op=ALU.is_ge, fill=NEG, base=0,
                                     pattern=[[-1, P]], channel_multiplier=1))
            settle()
            const(pool.memset(decay.rearrange("p (n c) -> p n c", c=C)[:, :, C - 1:C], 0.0))

            def root(norm, rs, b, k):
                pool.wait_ge(norm.s, norm.now(b, k))
                pool.sem_inc(pool_held, 1)
                pool.tensor_scalar(ve[:], mv[:, :, 1], EPS, None, ALU.add).then_inc(rs.s, 1)
                pool.wait_ge(rs.s, rs.now(b, 1))
                pool.tensor_tensor(rstd[:], ve[:], mhalf[:], ALU.pow).then_inc(rs.s, 1)

            def rotated(b):
                pool.wait_ge(rots.s, rots.now(b, 5))
                pool.wait_ge(hmm.s, hmm.before(b, 1))
                y3 = ysc.rearrange("p (n c) -> p n c", c=C)
                pool.tensor_tensor(yc.rearrange("p (n c) -> p n c", c=C), y3,
                                   wide(cos_t[:], NCH), ALU.mult).then_inc(yrot.s, 1)
                pool.tensor_tensor(ys.rearrange("p (n c) -> p n c", c=C), y3,
                                   wide(sin_t[:], NCH), ALU.mult).then_inc(yrot.s, 1)

            def residual(b):
                pool.wait_ge(hgs.s, hgs.now(b, 1))
                pool.sem_inc(pool_held, 1)
                xb, yb = X[:, bass.ts(b, TT), :], Y[:, bass.ts(b, TT), :]
                pool.tensor_tensor(yb, xb, hg, ALU.add).then_inc(res.s, 1)
                pool.wait_ge(res.s, res.now(b, 1))
                pool.sem_inc(pool_held, 1)
                pool.tensor_tensor(xb, xb, yb, ALU.add).then_inc(res.s, 1)
                pool.wait_ge(res.s, res.now(b, 2))
                pool.sem_inc(pool_held, 1)
                pool.tensor_tensor(xb, xb, wide(row[:, R_M2:R_M2 + D], TT), ALU.add)\
                    .then_inc(res.s, 1)

            pool.wait_ge(w_one, W_ONE)
            root(ln1, rs1, 0, 2 * TT)
            with pool.Fori(1, B) as b:
                root(ln1, rs1, b, 2 * TT)
                rotated(b - 1)
                residual(b - 1)
            rotated(B - 1)
            residual(B - 1)
            root(ln2, rs2, 0, 2 * TT)
            with pool.Fori(0, B - 1) as b:
                root(ln2, rs2, b + 1, 2 * TT)
                root(ln3, rs3, b, 1 + 2 * TT)
            root(ln3, rs3, B - 1, 1 + 2 * TT)

            for g in (xob, msk, rs4):
                pool.sem_inc(g.s, g.per)

            def with_bias(b):
                xb = X[:, bass.ts(b, TT), :]
                pool.wait_ge(xs_in.s, xs_in.now(b, 1))
                pool.sem_inc(pool_held, 1)
                pool.tensor_tensor(xb, xb, wide(row[:, R_O:R_O + D], TT), ALU.add)\
                    .then_inc(xob.s, 1)

            def pool_slot(b, g, j, prev, then, *steps):
                pool.wait_ge(exq.s, exq.now(b, g * NSH + FIRST[j] + len(SHARED[j])))
                pool.sem_inc(pool_held, 1)
                pool.affine_select(out=pb[j % 2][:, :, 0:P], in_=pb[j % 2][:, :, 0:P],
                                   compare_op=ALU.is_ge, fill=0.0, base=0,
                                   pattern=[[0, GH], [1, P]], channel_multiplier=-1)\
                    .then_inc(msk.s, 1)
                for name, c, k in steps[0] + steps[1] + steps[2]:
                    if name == "value" and k == 0:
                        with_bias(c)
                    elif name == "output" and k == 1:
                        root(ln4, rs4, c, 2 + 2 * TT)

            with_bias(0)
            slots(0, pool_slot, first=True)
            with pool.Fori(0, B - 1) as b:
                slots(b, pool_slot)
            slots(B - 1, pool_slot, last=True)
            root(ln4, rs4, B - 1, 2 + 2 * TT)

            for g in (gix, six, added):
                pool.sem_inc(g.s, g.per * g.unit)
            pool.wait_ge(lge.s, lge.now(B - 1, 1))
            pool.wait_ge(xtp.s, xtp.now(B - 1, KT))
            pool.memset(off[0:64, :], 0.0).then_inc(offs, 1)
            pool.memset(off[64:P, :], float(B * T)).then_inc(offs, 1)
            pool.memset(pair_of, 0.0).then_inc(offs, 1)
            pool.wait_ge(offs, 3)
            pool.affine_select(out=pair_of, in_=pair_of, compare_op=ALU.not_equal, fill=1.0, base=0,
                               pattern=[[-1, 2], [0, CAP]], channel_multiplier=1).then_inc(offs, 1)
            pool.wait_ge(topk, TOPK)
            pool.wait_ge(zsum, 16)
            pool.wait_ge(x2o.s, x2o.now(B - 1, 2))

            def gather(p, u, n=1):
                if n > 1:
                    pool.wait_ge(xgt.s, xgt.now(p - RING, 1))
                    pool.sem_inc(pool_held, 1)
                pool.tensor_copy(gidx[u], icol[:, bass.ds(p, 1)]).then_inc(gix.s, 1)
                pool.wait_ge(gix.s, gix.now(p, 1))
                pool.sem_inc(pool_held, 1)
                pool.indirect_dma_start(
                    xg[u], None, x2_rows,
                    bass.IndirectOffsetOnAxis(ap=gidx[u], axis=0)).then_inc(gathered[u], 16)

            def scatter(p, u):
                pool.tensor_copy(sidx[u % 3], jcol[:, bass.ds(p, 1)]).then_inc(six.s, 1)
                pool.wait_ge(six.s, six.now(p, 1))
                pool.sem_inc(pool_held, 1)
                pool.wait_ge(yws.s, yws.now(p, 1))
                pool.sem_inc(pool_held, 1)
                pool.indirect_dma_start(
                    sums, bass.IndirectOffsetOnAxis(ap=sidx[u % 3], axis=0), ye[u % 3], None,
                    compute_op=ALU.add).then_inc(scattered, 16)

            def after_addition(p):
                pool.wait_ge(scattered, 16 * p)
                pool.sem_inc(added.s, 1)

            for p in range(RING):
                gather(p, p)
            scatter(0, 0)
            with pool.Fori(0, NP // RING - 1) as r:
                for u in range(RING):
                    p = r * RING + (u + 1)
                    gather(p + (RING - 1), u, 2)
                    after_addition(p)
                    scatter(p, u + 1)
            for p in range(NP - RING + 1, NP):
                after_addition(p)
                scatter(p, p)
            for b in range(B):
                tiles = slice(b * TT, (b + 1) * TT)
                pool.wait_ge(fvar, (b + 1) * TT)
                pool.tensor_scalar(fve[:, tiles], fmv[:, tiles, 1], EPS, None, ALU.add)\
                    .then_inc(froot, 1)
                pool.wait_ge(froot, 4 * b + 1)
                pool.tensor_tensor(frstd[:, tiles], fve[:, tiles], mhalf[:], ALU.pow)\
                    .then_inc(froot, 1)
                pool.wait_ge(froot, 4 * b + 2)
                pool.tensor_tensor(fshift[:, tiles], fmv[:, tiles, 0], frstd[:, tiles], ALU.mult)\
                    .then_inc(froot, 1)
                pool.wait_ge(froot, 4 * b + 3)
                pool.tensor_scalar(fshift[:, tiles], fshift[:, tiles], -1.0, None, ALU.mult)\
                    .then_inc(froot, 1)

        @block.vector
        def _(dve):
            for g in (ln1, rots, gpre, hgs, ln2, ln3):
                dve.sem_inc(g.s, g.per)
            step = [0]

            def link(ins):
                step[0] += 1
                ins.then_inc(setup, 1)
                dve.wait_ge(setup, step[0])

            dve.wait_ge(consts, CONSTS)
            dve.wait_ge(w_one, W_ONE)
            link(dve.tensor_copy(ph, ph_i))
            link(dve.tensor_scalar(ph, ph, vec[:, V_FRQ:V_FRQ + 1], None, ALU.mult))
            for turn, dst in ((0.0, rot[:, 0:C]), (0.25, rot[:, C:2 * C])):
                link(dve.tensor_scalar(ph_n, ph, float(1 / (2 * np.pi)), turn, ALU.mult, ALU.add))
                link(dve.tensor_scalar(ph_n, ph_n, ROUND, None, ALU.add))
                link(dve.tensor_scalar(ph_n, ph_n, ROUND, None, ALU.subtract))
                link(dve.scalar_tensor_tensor(ph_m, ph_n, -TWO_PI_HI, ph, ALU.mult, ALU.add))
                link(dve.scalar_tensor_tensor(ph_m, ph_n, -TWO_PI_LO, ph_m, ALU.mult, ALU.add))
                link(dve.tensor_scalar(ph_m, ph_m, 2 * np.pi * turn, 3.1415925, ALU.add, ALU.min))
                link(dve.tensor_scalar(dst, ph_m, -3.1415925, None, ALU.max))
            dve.wait_ge(trig, 3)
            link(dve.tensor_scalar(decay, decay, mag, None, ALU.mult))
            link(dve.tensor_scalar(sin_t[0:NK, :], sin_t[0:NK, :], -1.0, None, ALU.mult))
            dve.wait_ge(wc_mm, 1)
            link(dve.tensor_copy(wc_s, bank(0).rearrange("p (k n) -> p k n", k=2)))
            assert step[0] == SETUP, step

            def norm(sig, rs, src, dst, first, k, before=None, at=None):
                b = first if at is None else at
                tile = lambda t: src[:, (0 if first is None else first * TT) + t, :]
                dve.sem_inc(dve_held, 1)
                for t in range(TT):
                    dve.bn_stats(stats[:, t, :], tile(t)).then_inc(sig.s, 1)
                dve.wait_ge(sig.s, sig.now(b, k + TT))
                dve.sem_inc(dve_held, 1)
                for t in range(TT):
                    dve.bn_aggr(mv[:, t, :], stats[:, t, :]).then_inc(sig.s, 1)
                dve.wait_ge(rs.s, rs.now(b, 2))
                if before is not None:
                    dve.wait_ge(before.s, before.before(b, 1))
                for t in range(TT):
                    dve.tensor_scalar(dst(t), tile(t),
                                      mv[:, t, 0:1], rstd[:, t:t + 1],
                                      ALU.subtract, ALU.mult).then_inc(sig.s, 1)

            def ln_in(b):
                dve.wait_ge(x_in.s, x_in.now(b, 1))
                norm(ln1, rs1, X, lambda t: xn[:, t, :], b, 0, xt1)

            def rotate(b):
                ps0 = bank(2).rearrange("p (n c) -> p n c", c=C)
                ps1 = bank(3).rearrange("p (n c) -> p n c", c=C)
                dve.wait_ge(beta.s, beta.now(b, 1))
                dve.tensor_tensor(rot.rearrange("p (n c) -> p n c", c=C), ps0,
                                  wide(cos_t[:], NCH), ALU.mult).then_inc(rots.s, 1)
                dve.tensor_tensor(rot2.rearrange("p (n c) -> p n c", c=C), ps1,
                                  wide(sin_t[:], NCH), ALU.mult).then_inc(rots.s, 1)
                dve.wait_ge(rots.s, rots.now(b, 2))
                dve.tensor_tensor(rot, rot, rot2, ALU.add).then_inc(rots.s, 1)
                dve.wait_ge(rots.s, rots.now(b, 3))
                dve.wait_ge(yrot.s, yrot.before(b, 2))
                dve.tensor_tensor_scan(ysc[:, ::-1], decay[:, ::-1], rot[:, ::-1], 0.0,
                                       ALU.mult, ALU.add).then_inc(rots.s, 1)
                dve.wait_ge(rots.s, rots.now(b, 4))
                first = ysc.rearrange("p (n c) -> p n c", c=C)[:, 1:, 0]
                dve.tensor_tensor(first, first, ps0[:, :NCH - 1, C - 1], ALU.add)\
                    .then_inc(rots.s, 1)

            def gate_in(b):
                dve.wait_ge(beta.s, beta.now(b, 2))
                dve.wait_ge(hgs.s, hgs.before(b, 1))
                dve.tensor_tensor(gz, bank(4, 2).rearrange("p (t n) -> p t n", t=TT),
                                  wide(row[:, R_GATE:R_GATE + D], TT), ALU.add)\
                    .then_inc(gpre.s, 1)

            def gate_out(b):
                dve.wait_ge(gact.s, gact.now(b, 1))
                dve.wait_ge(hmm.s, hmm.now(b, 1))
                dve.wait_ge(res.s, res.before(b, 1))
                dve.tensor_tensor(hg, bank(6, 2).rearrange("p (t n) -> p t n", t=TT), gz,
                                  ALU.mult).then_inc(hgs.s, 1)

            ln_in(0)
            with dve.Fori(1, B) as b:
                ln_in(b)
                rotate(b - 1)
                gate_in(b - 1)
                gate_out(b - 1)
            rotate(B - 1)
            gate_in(B - 1)
            gate_out(B - 1)

            def ln_mid(b):
                dve.wait_ge(res.s, res.now(b, 1))
                norm(ln2, rs2, Y, lambda t: xn[:, t, :], b, 0, xt2)

            def ln_out(b):
                dve.wait_ge(res.s, res.now(b, 3))
                dve.wait_ge(m2.s, m2.now(b, 1))
                xb = X[:, bass.ts(b, TT), :]
                dve.tensor_tensor(xb, bank(6, 2).rearrange("p (t n) -> p t n", t=TT), xb,
                                  ALU.add).then_inc(ln3.s, 1)
                dve.wait_ge(ln3.s, ln3.now(b, 1))
                norm(ln3, rs3, X, lambda t: X[:, b * TT + t, :], b, 1)

            ln_mid(0)
            with dve.Fori(0, B - 1) as b:
                ln_mid(b + 1)
                ln_out(b)
            ln_out(B - 1)

            for g in (kev, qev, vev, ksd, qsd, sqe, mxs, mneg, odv, ln4):
                dve.sem_inc(g.s, g.per)
            dve.wait_ge(ln3.s, ln3.now(B - 1, 1 + 3 * TT))
            dve.memset(Vb, 0.0).then_inc(vset, 1)
            dve.wait_ge(vset, 1)
            dve.memset(Vb[:, :, :, HD:HD + 1], 1.0).then_inc(vset, 1)
            dve.memset(KTs[SK:SX, :, :], 1.0).then_inc(vset, 1)

            piece = lambda m, n, k=1: m.rearrange("p t h s -> p (t h) s")[:, :, n * HD:(n + k) * HD]
            k_src = kq.rearrange("p (a d) -> p a d", d=HD)
            q_src = qt.rearrange("p (a d) -> p a d", d=HD)

            def dve_key(b, m):
                dve.wait_ge(kpr.s, kpr.now(b, m + 1))
                dve.wait_ge(ksd.s, ksd.before(b, 2))
                dve.tensor_tensor(kq[:, 512 * m:512 * m + 512].rearrange("p (t n) -> p t n", t=2),
                                  spare(m).rearrange("p (t n) -> p t n", t=2),
                                  wide(row[:, R_K:R_K + D], 2), ALU.add).then_inc(kev.s, 1)

            def dve_split_k(b, k):
                if k == 1:
                    dve.wait_ge(ksa.s, ksa.now(b, 1))
                    dve.tensor_tensor(k_src, k_src, piece(st, 0), ALU.subtract).then_inc(ksd.s, 1)
                elif k == 3:
                    dve.wait_ge(ksa.s, ksa.now(b, 2))
                    dve.wait_ge(ksd.s, ksd.now(b, 1))
                    dve.tensor_tensor(piece(st, 2), k_src, piece(st, 1), ALU.subtract)\
                        .then_inc(ksd.s, 1)

            def dve_query(b, m):
                dve.wait_ge(qpr.s, qpr.now(b, m + 1))
                dve.wait_ge(qsd.s, qsd.before(b, 5))
                dve.tensor_tensor(qt[:, 512 * m:512 * m + 512].rearrange("p (t n) -> p t n", t=2),
                                  spare(m).rearrange("p (t n) -> p t n", t=2),
                                  wide(row[:, R_Q:R_Q + D], 2), ALU.add).then_inc(qev.s, 1)

            def dve_split_q(b, k):
                if k == 1:
                    dve.wait_ge(qsa.s, qsa.now(b, 1))
                    dve.tensor_tensor(q_src, q_src, piece(stq, 0), ALU.subtract)\
                        .then_inc(qsd.s, 1)
                    for n in (1, 2):
                        dve.tensor_copy(piece(stq, n), piece(stq, 0)).then_inc(qsd.s, 1)
                elif k == 3:
                    dve.wait_ge(qsa.s, qsa.now(b, 2))
                    dve.wait_ge(qsd.s, qsd.now(b, 1))
                    dve.tensor_tensor(piece(stq, 5), q_src, piece(stq, 3), ALU.subtract)\
                        .then_inc(qsd.s, 1)
                    dve.tensor_copy(piece(stq, 4), piece(stq, 3)).then_inc(qsd.s, 1)

            def dve_value(b, m):
                dve.wait_ge(vpr.s, vpr.now(b, m + 1))
                dve.wait_ge(pvs.s, pvs.before(b, 2 * TT * (m + 1)))
                bias = row[:, R_V + P * m:R_V + P * m + P].rearrange("p (h d) -> p h d", d=HD)
                for t in range(TT):
                    ins = dve.tensor_tensor(Vb[:, t, 8 * m:8 * m + 8, 0:HD],
                                            spare(m)[:, t * P:(t + 1) * P]
                                            .rearrange("p (h d) -> p h d", d=HD), bias, ALU.add)
                ins.then_inc(vev.s, 1)

            def dve_stack_q(b, n):
                dve.wait_ge(sqt.s, sqt.now(b, n + 1))
                q, m = n // 2, n % 2
                dve.tensor_copy(QTs[0:SK, GH * q:GH * q + GH, 2 * P * m:2 * P * (m + 1)],
                                spare(n).bitcast(BF16)[0:SK, :]
                                .rearrange("p (h n) -> p h n", h=GH)).then_inc(sqe.s, 1)

            def maxima(b, g, i):
                for h in range(GH):
                    n = g * 16 + i * GH + h
                    if i == 0 and h == 0:
                        dve.wait_ge(mneg.s, mneg.now(b, 4 * (g - 1)) if g >= 2
                                    else mneg.before(b, 4 * (NG + g - 1)))
                    dve.wait_ge(mxs.s, mxs.now(b, n - 1) if n >= 2 else mxs.before(b, 64 + n - 1))
                    dve.sem_inc(dve_held, 1)
                    dve.wait_ge(smm.s, smm.now(b, n + 1))
                    dve.sem_inc(dve_held, 1)
                    w = (i + 1) * P
                    dve.tensor_tensor_reduce(junk[:, n % 2, 0:w], bank(n % 2)[:, 0:w],
                                             causal[:, T - w:], 1.0, NEG, ALU.add, ALU.max,
                                             Mx[:, g % 2, i, h:h + 1]).then_inc(mxs.s, 1)

            def negate(b, g):
                m, d = Mx[:, g % 2], nst[:, g % 2]
                dve.wait_ge(mxs.s, mxs.now(b, 16 * (g + 1)))
                dve.wait_ge(ntp.s, ntp.now(b, 2 * (g - 1)) if g >= 2
                            else ntp.before(b, 2 * (NG + g - 1)))
                dve.tensor_scalar(d[:, :, :, 0], m, -1.0, None, ALU.mult).then_inc(mneg.s, 1)
                dve.wait_ge(mneg.s, mneg.now(b, 4 * g + 1))
                dve.scalar_tensor_tensor(Mr[:], m, -1.0, d[:, :, :, 0], ALU.mult, ALU.subtract)\
                    .then_inc(mneg.s, 1)
                dve.wait_ge(mneg.s, mneg.now(b, 4 * g + 2))
                dve.tensor_copy(d[:, :, :, 1], Mr[:]).then_inc(mneg.s, 1)
                dve.wait_ge(mneg.s, mneg.now(b, 4 * g + 3))
                dve.tensor_tensor(d[:, :, :, 2], Mr[:], d[:, :, :, 1], ALU.subtract)\
                    .then_inc(mneg.s, 1)

            def divide(b, g):
                o = spare(1).rearrange("p (t h v) -> p t h v", t=TT, h=GH)
                dve.wait_ge(otp.s, otp.now(b, g + 1))
                if g == 0:
                    dve.wait_ge(o2t.s, o2t.before(b, KT))
                dve.reciprocal(rden[:], o[:, :, :, HD]).then_inc(odv.s, 1)
                dve.wait_ge(odv.s, odv.now(b, 2 * g + 1))
                dve.tensor_tensor(
                    otok[:, :, g * GH * HD:(g + 1) * GH * HD]
                    .rearrange("p t (h v) -> p t h v", h=GH), o[:, :, :, 0:HD],
                    rden[:].unsqueeze(3).to_broadcast([P, TT, GH, HD]), ALU.mult)\
                    .then_inc(odv.s, 1)

            def dve_output(b, m):
                dve.wait_ge(omm.s, omm.now(b, m + 1))
                dve.wait_ge(xob.s, xob.now(b, 1))
                dve.wait_ge(x2o.s, x2o.before(b, 2))
                dve.wait_ge(x2t.s, x2t.before(b, KT))
                dve.tensor_tensor(x2b[:, 2 * m:2 * m + 2, :],
                                  spare(m).rearrange("p (t n) -> p t n", t=2),
                                  X[:, bass.ds(b * TT + 2 * m, 2), :], ALU.add).then_inc(ln4.s, 1)
                if m == 1:
                    dve.wait_ge(ln4.s, ln4.now(b, 2))
                    norm(ln4, rs4, x2b, lambda t: x2b[:, t, :], None, 2, at=b)

            dve_steps = {"key": dve_key, "query": dve_query, "value": dve_value,
                         "split_k": dve_split_k, "split_q": dve_split_q,
                         "stack_q": dve_stack_q, "output": dve_output}

            def dve_do(steps):
                for name, c, k in steps:
                    if name in dve_steps:
                        dve_steps[name](c, k)

            def dve_slot(b, g, j, prev, then, *steps):
                if j == 0 and prev is not None:
                    divide(*prev)
                dve_do(steps[0])
                if then is not None:
                    for i in SCORED[j]:
                        maxima(*then, i)
                    if j == 2:
                        negate(*then)
                dve_do(steps[1] + steps[2])

            dve_do([(name, 0, k) for name, k in all_steps(PREPARE)])
            for i in range(TT):
                maxima(0, 0, i)
            negate(0, 0)
            slots(0, dve_slot, first=True)
            with dve.Fori(0, B - 1) as b:
                slots(b, dve_slot)
            slots(B - 1, dve_slot, last=True)
            divide(B - 1, NG - 1)
            dve_do([(name, B - 1, k) for name, k in all_steps(FINISH)])

            for g in (hed, hbs, yws):
                dve.sem_inc(g.s, g.per)
            steps = [0]

            def then(ins):
                steps[0] += 1
                ins.then_inc(topk, 1)
                dve.wait_ge(topk, steps[0])

            dve.wait_ge(lge.s, lge.now(B - 1, 1))
            for a in range(2):
                then(dve.tensor_copy(LG2[64 * a:64 * a + 64, :].rearrange("p (b n) -> p b n", b=2),
                                     LGs[:, 2 * a:2 * a + 2, :]))
            for r in range(CAP // 8):
                v = top_v[:, 8 * r:8 * r + 8]
                then(dve.max(v, LG2))
                then(dve.max_index(top_i[:, 8 * r:8 * r + 8], v, LG2))
                if r + 1 < CAP // 8:
                    then(dve.match_replace(LG2, v, LG2, NEG))
            then(dve.tensor_copy(top_f, top_i))
            then(dve.tensor_scalar(top_f[64:P, :], top_f[64:P, :], float(B * T // 2), None, ALU.add))
            lo = slice(0, 64)
            then(dve.tensor_copy(far_v[lo, :], top_v[64:P, ::-1]))
            then(dve.tensor_copy(far_i[lo, :], top_f[64:P, ::-1]))
            then(dve.tensor_tensor(pick[lo, :], top_v[lo, :], far_v[lo, :], ALU.is_ge))
            then(dve.tensor_tensor(sel_v[lo, :], top_v[lo, :], far_v[lo, :], ALU.max))
            then(dve.tensor_tensor(sel_i[lo, :], top_f[lo, :], far_i[lo, :], ALU.subtract))
            then(dve.tensor_tensor(sel_i[lo, :], sel_i[lo, :], pick[lo, :], ALU.mult))
            then(dve.tensor_tensor(sel_i[lo, :], sel_i[lo, :], far_i[lo, :], ALU.add))
            then(dve.tensor_reduce(smx[lo, 0:1], sel_v[lo, :], AX.X, ALU.max))
            then(dve.tensor_scalar(smx[lo, 1:2], smx[lo, 0:1], -1.0, None, ALU.mult))
            shifted = steps[0]
            assert shifted == SHIFTED, shifted
            dve.wait_ge(wexp, 1)
            then(dve.reciprocal(smx[lo, 3:4], smx[lo, 2:3]))
            then(dve.tensor_scalar(sel_v[lo, :], sel_v[lo, :], smx[lo, 3:4], None, ALU.mult))
            for a in range(2):
                rows_a = slice(32 * a, 32 * a + 32)
                then(dve.tensor_copy(tw[:, CAP * a:CAP * a + CAP], sel_v[rows_a, :]))
                then(dve.tensor_copy(ti[:, CAP * a:CAP * a + CAP], sel_i[rows_a, :]))
            assert steps[0] == CHOSEN, steps
            dve.wait_ge(icm, 1)
            then(dve.tensor_copy(wcol, bank(0)[:, 0:NP]))
            then(dve.tensor_copy(icf, bank(0)[:, 32:32 + NP]))
            then(dve.tensor_copy(icol, icf))
            dve.wait_ge(offs, 4)
            then(dve.tensor_scalar(jcf, icf, off, None, ALU.add))
            then(dve.tensor_copy(jcol, jcf))
            assert steps[0] == TOPK, steps
            dve.wait_ge(b1_in, 16)

            def second_half(p):
                dve.wait_ge(h1m.s, h1m.now(p, 2))
                dve.wait_ge(htm.s, htm.before(p, 2))
                dve.tensor_copy(HB[:, 512:1024], bank(2)).then_inc(hed.s, 1)

            def hidden_bias(p):
                for a in range(2):
                    dve.wait_ge(htm.s, htm.now(p, a + 1))
                    if a == 0:
                        dve.wait_ge(y2m.s, y2m.before(p, 1))
                    dve.tensor_tensor(
                        hb[:, a * 512:(a + 1) * 512].rearrange("p (c n) -> p c n", c=8),
                        bank(3 + a).rearrange("p (c n) -> p c n", c=8),
                        b1_s[:, bass.ds(p, 1), 4 * a:4 * a + 4, :]
                        .rearrange("p e c a -> p (e c a)").unsqueeze(2).to_broadcast([P, 8, CAP]),
                        ALU.add).then_inc(hbs.s, 1)

            def weigh(p, u):
                dve.wait_ge(y2m.s, y2m.now(p, 1))
                dve.wait_ge(added.s, p + 1)
                dve.tensor_scalar(ye[u % 3], bank(5 + u % 2)[:, 0:D], wcol[:, bass.ds(p, 1)], None,
                                  ALU.mult).then_inc(yws.s, 1)

            second_half(0)
            hidden_bias(0)
            with dve.Fori(0, NP // RING - 1) as r:
                for u in range(RING):
                    p = r * RING + u
                    second_half(p + 1)
                    weigh(p, u)
                    hidden_bias(p + 1)
            for u in range(RING):
                p = NP - RING + u
                if p + 1 < NP:
                    second_half(p + 1)
                weigh(p, u)
                if p + 1 < NP:
                    hidden_bias(p + 1)

            for b in range(B):
                xb = X[:, b * TT:(b + 1) * TT, :]
                dve.wait_ge(fin_in[b], 32)
                dve.tensor_tensor(xb, xb, Y[:, b * TT:(b + 1) * TT, :], ALU.add).then_inc(fsum, 1)
                dve.wait_ge(fsum, b + 1)
                for t in range(b * TT, (b + 1) * TT):
                    dve.bn_stats(fstats[:, t, :], X[:, t, :]).then_inc(fstat, 1)
                for t in range(b * TT, (b + 1) * TT):
                    dve.wait_ge(fstat, t + 1)
                    dve.bn_aggr(fmv[:, t, :], fstats[:, t, :]).then_inc(fvar, 1)

        @block.scalar
        def _(act):
            for g in (xe1, gact, xe2, silu):
                act.sem_inc(g.s, g.per)
            act.dma_start(vec[:], vecs).then_inc(w_one, 16)
            act.dma_start(row[:], rows.to_broadcast([P, RCOLS])).then_inc(w_one, 16)
            act.dma_start(wi_s, w_in.rearrange("(k p) n -> p k n", p=P)).then_inc(w_one, 16)
            act.dma_start(wout_s, w_out.rearrange("v p n -> p v n")).then_inc(w_one, 16)
            act.wait_ge(setup_cb, 1)
            for g in range(2 * CH):
                act.dma_start(cb_s[CK * g:CK * g + CK, CK * g:CK * g + CK],
                              coupling[g % CH]).then_inc(w_one, 16)
            act.dma_start(wg_s, w_gate.rearrange("(k p) n -> p k n", p=P)).then_inc(w_one, 16)
            act.dma_start(wm1_s, w_mlp1.rearrange("(k p) n -> p k n", p=P)).then_inc(w_mlp, 16)
            act.dma_start(wm2_s, w_mlp2.rearrange("(k p) n -> p k n", p=P)).then_inc(w_mlp, 16)
            act.dma_start(wkv_s[:], w_kv.rearrange("(k p) n -> p k n", p=P)).then_inc(w_att, 16)
            act.dma_start(wq_s[:], w_q.rearrange("(k p) n -> p k n", p=P)).then_inc(w_att, 16)
            act.dma_start(wo_s[:], w_o.rearrange("(k p) n -> p k n", p=P)).then_inc(w_att, 16)
            act.wait_ge(consts, CONSTS)
            act.dma_start(wr_s[:, :, 0:NP], w_r[0].rearrange("(k p) n -> p k n", p=P))\
                .then_inc(w_att, 16)
            act.dma_start(wr_s[:, :, 32:32 + NP], w_r[1].rearrange("(k p) n -> p k n", p=P))\
                .then_inc(w_att, 16)
            act.wait_ge(w_one, W_ONE)
            act.activation(mag, vec[:, V_DEC:V_DEC + 1], ACT.Sigmoid).then_inc(trig, 1)
            act.wait_ge(setup, 9)
            act.activation(sin_t[:], rot[:, 0:C], ACT.Sin).then_inc(trig, 1)
            act.wait_ge(setup, 16)
            act.activation(cos_t[:], rot[:, C:2 * C], ACT.Sin).then_inc(trig, 1)

            def turned(xt, xe, used, g, be, b):
                act.wait_ge(xt.s, xt.now(b, 1))
                act.wait_ge(used[0].s, used[0].before(b, used[1]))
                for k in range(KT):
                    act.activation(xT[:, k, :], bank(k), ACT.Identity, bias=vec[:, be + k:be + k + 1],
                                   scale=vec[:, g + k:g + k + 1]).then_inc(xe.s, 1)

            with act.Fori(0, B) as b:
                turned(xt1, xe1, (beta, 2), V_G1, V_B1, b)
                act.wait_ge(gpre.s, gpre.now(b, 1))
                act.activation(gz, gz, ACT.Sigmoid).then_inc(gact.s, 1)
            act.wait_ge(beta.s, beta.now(B - 1, 2))
            turned(xt2, xe2, (m1, MT), V_G2, V_B2, 0)
            def hidden(b):
                for m in range(MT):
                    act.wait_ge(m1.s, m1.now(b, m + 1))
                    act.wait_ge(m2.s, m2.before(b, 1))
                    act.activation(hid[:, m, :], bank(2 + m % 4), ACT.Silu,
                                   bias=vec[:, V_BM + m:V_BM + m + 1]).then_inc(silu.s, 1)
            with act.Fori(0, B - 1) as b:
                hidden(b)
                turned(xt2, xe2, (m1, MT), V_G2, V_B2, b + 1)
            hidden(B - 1)

            for g in (cte, xte, ksa, qsa, ske, nte, exq, oev, o2e, x2e, lge):
                act.sem_inc(g.s, g.per)
            act.wait_ge(m2.s, m2.now(B - 1, 1))
            act.wait_ge(ln3.s, ln3.now(B - 1, 1 + 3 * TT))

            piece = lambda m, n, k=1: m.rearrange("p t h s -> p (t h) s")[:, :, n * HD:(n + k) * HD]
            k_src = kq.rearrange("p (a d) -> p a d", d=HD)
            q_src = qt.rearrange("p (a d) -> p a d", d=HD)

            def plain(written, read, dst):
                def step(b, k):
                    act.wait_ge(written.s, written.now(b, k + 1))
                    act.activation(dst[:, k, :], spare(k), ACT.Copy).then_inc(read.s, 1)
                return step

            def act_split_k(b, k):
                if k == 0:
                    act.wait_ge(kev.s, kev.now(b, 2))
                    act.wait_ge(skt.s, skt.before(b, 2 * NG))
                    act.activation(piece(st, 0), k_src, ACT.Copy).then_inc(ksa.s, 1)
                elif k == 2:
                    act.wait_ge(ksd.s, ksd.now(b, 1))
                    act.activation(piece(st, 1), k_src, ACT.Copy).then_inc(ksa.s, 1)
                elif k == 4:
                    act.wait_ge(ksa.s, ksa.now(b, 2))
                    act.activation(piece(st, 3, 2), piece(st, 0, 2), ACT.Copy).then_inc(ksa.s, 1)
                    act.activation(piece(st, 5), piece(st, 0), ACT.Copy).then_inc(ksa.s, 1)

            def act_split_q(b, k):
                if k == 0:
                    act.wait_ge(qev.s, qev.now(b, 2))
                    act.wait_ge(sqt.s, sqt.before(b, 2 * NG))
                    act.activation(piece(stq, 0), q_src, ACT.Copy).then_inc(qsa.s, 1)
                elif k == 2:
                    act.wait_ge(qsd.s, qsd.now(b, 1))
                    act.activation(piece(stq, 3), q_src, ACT.Copy).then_inc(qsa.s, 1)

            def act_stack_k(b, n):
                act.wait_ge(skt.s, skt.now(b, n + 1))
                q, m = n // 2, n % 2
                act.activation(KTs[0:SK, GH * q:GH * q + GH, 2 * P * m:2 * P * (m + 1)],
                               spare(n).bitcast(BF16)[0:SK, :]
                               .rearrange("p (h n) -> p h n", h=GH), ACT.Copy).then_inc(ske.s, 1)

            def act_logits(b, k):
                act.wait_ge(lgm.s, lgm.now(b, 1))
                act.activation(LGs[:, b, :], spare(0)[0:64, :], ACT.Copy).then_inc(lge.s, 1)

            def minus_max(b, g):
                for m in range(2):
                    act.wait_ge(ntp.s, ntp.now(b, 2 * g + m + 1))
                    act.activation(QTs[SK:SX, GH * g + 2 * m:GH * g + 2 * m + 2, :],
                                   spare(m).bitcast(BF16)[SK:SX, :]
                                   .rearrange("p (h n) -> p h n", h=2), ACT.Copy)\
                        .then_inc(nte.s, 1)

            def exponentials(b, g, j):
                w = T - j * P
                t = g * TT + j
                for n, heads in enumerate(SHARED[j], FIRST[j]):
                    if n == FIRST[j]:
                        act.wait_ge(pvs.s, pvs.now(b, t - 1) if t >= 2
                                    else pvs.before(b, NG * TT + t - 1))
                    act.wait_ge(stm.s, stm.now(b, g * NSH + n + 1))
                    act.activation(
                        pb[j % 2][:, heads[0]:heads[-1] + 1, 0:w],
                        bank(2 + n % 3)[:, 0:len(heads) * w]
                        .rearrange("p (h n) -> p h n", h=len(heads)),
                        ACT.Exp, scale=float(HD) ** -0.5).then_inc(exq.s, 1)

            def group_out(b, g):
                act.wait_ge(otp.s, otp.now(b, g) if g > 0 else otp.before(b, NG))
                act.wait_ge(pvs.s, pvs.now(b, TT * (g + 1)))
                act.activation(oTs, bank(6), ACT.Copy).then_inc(oev.s, 1)

            act_steps = {"context": plain(ctp, cte, cT), "query_in": plain(xtp, xte, aT),
                         "heads": plain(o2t, o2e, oT2), "turn": plain(x2t, x2e, x2T),
                         "split_k": act_split_k, "split_q": act_split_q,
                         "stack_k": act_stack_k, "logits": act_logits}

            def act_do(steps):
                for name, c, k in steps:
                    if name in act_steps:
                        act_steps[name](c, k)

            def act_slot(b, g, j, prev, then, *steps):
                if j == 0 and prev is not None:
                    group_out(*prev)
                exponentials(b, g, j)
                act_do(steps[0] + steps[1])
                if j == TT - 1 and then is not None:
                    minus_max(*then)
                act_do(steps[2])

            act_do([(name, 0, k) for name, k in all_steps(PREPARE)])
            minus_max(0, 0)
            slots(0, act_slot, first=True)
            with act.Fori(0, B - 1) as b:
                slots(b, act_slot)
            slots(B - 1, act_slot, last=True)
            group_out(B - 1, NG - 1)
            act_do([(name, B - 1, k) for name, k in all_steps(FINISH)])

            for g in (xge, hea, gel):
                act.sem_inc(g.s, g.per)
            act.wait_ge(topk, SHIFTED)
            act.activation(sel_v[0:64, :], sel_v[0:64, :], ACT.Exp, bias=smx[0:64, 1:2],
                           accum_out=smx[0:64, 2:3]).then_inc(wexp, 1)

            def tokens(p):
                act.wait_ge(xgt.s, xgt.now(p, 1))
                act.wait_ge(h1m.s, h1m.before(p, 2))
                act.activation(xgT.rearrange("p k n -> p (k n)"), bank(0)[:, 0:KT * P], ACT.Copy)\
                    .then_inc(xge.s, 1)

            def first_half(p):
                act.wait_ge(h1m.s, h1m.now(p, 1))
                act.wait_ge(htm.s, htm.before(p, 1))
                act.activation(HB[:, 0:512], bank(1), ACT.Copy).then_inc(hea.s, 1)

            def gelu(p):
                for a in range(2):
                    act.wait_ge(hbs.s, hbs.now(p, a + 1))
                    act.activation(hb[:, a * 512:(a + 1) * 512], hb[:, a * 512:(a + 1) * 512],
                                   ACT.Gelu).then_inc(gel.s, 1)

            tokens(0)
            first_half(0)
            tokens(1)
            gelu(0)
            with act.Fori(0, NP // RING - 1) as r:
                for u in range(RING):
                    p = r * RING + u
                    first_half(p + 1)
                    tokens(p + 2)
                    gelu(p + 1)
            for u in range(RING):
                p = NP - RING + u
                if p + 1 < NP:
                    first_half(p + 1)
                if p + 2 < NP:
                    tokens(p + 2)
                if p + 1 < NP:
                    gelu(p + 1)

            for b in range(B):
                act.wait_ge(froot, 4 * b + 4)
                for t in range(b * TT, (b + 1) * TT):
                    act.activation(X[:, t, :], X[:, t, :], ACT.Identity, bias=fshift[:, t:t + 1],
                                   scale=frstd[:, t:t + 1]).then_inc(fout, 1)

        @block.tensor
        def _(pe):
            for g in (xt1, beta, hmm, xt2, m1, m2):
                pe.sem_inc(g.s, g.per)
            pe.wait_ge(w_one, W_ONE)
            for v in range(2):
                mm = pe.matmul(PS[:, v * D:(v + 1) * D], cb_s, wout_s[:, v, :], start=True,
                               stop=True)
            mm.then_inc(wc_mm, 1)
            pe.wait_ge(consts, CONSTS)

            def turn(ln, xe, xt, b):
                pe.wait_ge(xe.s, xe.before(b, KT))
                for t in range(TT):
                    pe.wait_ge(ln.s, ln.now(b, 2 * TT + t + 1))
                    for j in range(KT):
                        mm = pe.transpose(bank(j)[:, t * P:(t + 1) * P],
                                          xn[:, t, j * P:(j + 1) * P], ident[:])
                mm.then_inc(xt.s, 1)

            def project(b):
                pe.wait_ge(xe1.s, xe1.now(b, KT))
                pe.wait_ge(rots.s, rots.before(b, 5))
                for v in range(2):
                    for k in range(KT):
                        mm = pe.matmul(bank(2 + v), wi_s[:, k, v * P:(v + 1) * P], xT[:, k, :],
                                       start=(k == 0), stop=(k == KT - 1))
                mm.then_inc(beta.s, 1)
                pe.wait_ge(gpre.s, gpre.before(b, 1))
                for t in range(TT):
                    for k in range(KT):
                        mm = pe.matmul(PS[:, 4 * 512 + t * D:4 * 512 + (t + 1) * D],
                                       xT[:, k, t * P:(t + 1) * P], wg_s[:, k, :],
                                       start=(k == 0), stop=(k == KT - 1))
                mm.then_inc(beta.s, 1)

            def mix(b):
                pe.wait_ge(yrot.s, yrot.now(b, 2))
                pe.wait_ge(hgs.s, hgs.before(b, 1))
                for t in range(TT):
                    for k, y in enumerate((yc, ys)):
                        mm = pe.matmul(PS[:, 6 * 512 + t * D:6 * 512 + (t + 1) * D],
                                       y[:, t * P:(t + 1) * P], wc_s[:, k, :],
                                       start=(k == 0), stop=(k == 1))
                mm.then_inc(hmm.s, 1)

            pe.wait_ge(setup, SETUP)
            turn(ln1, xe1, xt1, 0)
            project(0)
            with pe.Fori(1, B) as b:
                turn(ln1, xe1, xt1, b)
                mix(b - 1)
                project(b)
            mix(B - 1)

            def expand(b):
                pe.wait_ge(xe2.s, xe2.now(b, KT))
                for m in range(MT):
                    if m < 4:
                        pe.wait_ge(silu.s, silu.before(b, m + 5))
                    else:
                        pe.wait_ge(silu.s, silu.now(b, m - 3))
                    for k in range(KT):
                        mm = pe.matmul(bank(2 + m % 4), wm1_s[:, k, m * P:(m + 1) * P],
                                       xT[:, k, :], start=(k == 0), stop=(k == KT - 1))
                    mm.then_inc(m1.s, 1)

            def shrink(b):
                pe.wait_ge(silu.s, silu.now(b, MT))
                pe.wait_ge(ln3.s, ln3.before(b, 1))
                for t in range(TT):
                    for m in range(MT):
                        mm = pe.matmul(PS[:, 6 * 512 + t * D:6 * 512 + (t + 1) * D],
                                       hid[:, m, t * P:(t + 1) * P], wm2_s[:, m, :],
                                       start=(m == 0), stop=(m == MT - 1))
                mm.then_inc(m2.s, 1)

            pe.wait_ge(w_mlp, 32)
            pe.wait_ge(xe1.s, xe1.now(B - 1, KT))
            turn(ln2, xe2, xt2, 0)
            pe.wait_ge(gpre.s, gpre.now(B - 1, 1))
            pe.wait_ge(rots.s, rots.now(B - 1, 5))
            with pe.Fori(0, B - 1) as b:
                expand(b)
                turn(ln2, xe2, xt2, b + 1)
                shrink(b)
            expand(B - 1)
            shrink(B - 1)

            for g in (ctp, xtp, kpr, qpr, vpr, skt, sqt, smm, ntp, stm, pvs, otp, o2t, omm, x2t, lgm):
                pe.sem_inc(g.s, g.per)
            pe.wait_ge(w_att, 16 * 5)
            pe.wait_ge(silu.s, silu.now(B - 1, MT))
            pe.wait_ge(ln3.s, ln3.now(B - 1, 1))
            pe.wait_ge(vset, 3)

            read_by = {0: None, 1: None}

            def take(k, sig, value):
                if read_by[k % 2] is not None:
                    pe.wait_ge(*read_by[k % 2])
                read_by[k % 2] = (sig.s, value)
                return spare(k)

            def turned(o, src, k):
                for t in range(TT):
                    mm = pe.transpose(o[:, t * P:(t + 1) * P], src[:, t, k * P:(k + 1) * P],
                                      ident[:])
                return mm

            def pe_context(b, k):
                if k == 0:
                    pe.wait_ge(c_in.s, c_in.now(b, 1))
                turned(take(k, cte, cte.now(b, k + 1)), ctxb, k).then_inc(ctp.s, 1)

            def pe_query_in(b, k):
                if k == 0:
                    pe.wait_ge(xs_in.s, xs_in.now(b, 1))
                turned(take(k, xte, xte.now(b, k + 1)), xs, k).then_inc(xtp.s, 1)

            def projected(o, xt, w, m):
                for t in range(2):
                    for k in range(KT):
                        mm = pe.matmul(o[:, t * D:(t + 1) * D],
                                       xt[:, k, (2 * m + t) * P:(2 * m + t + 1) * P], w[:, k, :],
                                       start=(k == 0), stop=(k == KT - 1))
                return mm

            def pe_key(b, m):
                pe.wait_ge(cte.s, cte.now(b, KT))
                projected(take(m, kev, kev.now(b, m + 1)), cT, wkv_s[:, :, 0:D], m)\
                    .then_inc(kpr.s, 1)

            def pe_query(b, m):
                pe.wait_ge(xte.s, xte.now(b, KT))
                projected(take(m, qev, qev.now(b, m + 1)), aT, wq_s, m).then_inc(qpr.s, 1)

            def pe_value(b, m):
                pe.wait_ge(cte.s, cte.now(b, KT))
                o = take(m, vev, vev.now(b, m + 1))
                for t in range(TT):
                    for k in range(KT):
                        mm = pe.matmul(o[:, t * P:(t + 1) * P], cT[:, k, t * P:(t + 1) * P],
                                       wkv_s[:, k, D + m * P:D + (m + 1) * P],
                                       start=(k == 0), stop=(k == KT - 1))
                mm.then_inc(vpr.s, 1)

            def pe_stack(src, done, read, made):
                def step(b, n):
                    if n == 0:
                        for g in made:
                            pe.wait_ge(g.s, g.now(b, g.per))
                    o = take(n, read, read.now(b, n + 1)).bitcast(BF16)
                    for h in range(GH):
                        for t in range(2):
                            mm = pe.transpose(o[0:SK, (2 * h + t) * P:(2 * h + t + 1) * P],
                                              src[:, 2 * (n % 2) + t, GH * (n // 2) + h, :],
                                              identb[:])
                    mm.then_inc(done.s, 1)
                return step

            def scores(b, g, i):
                if i == 0:
                    pe.wait_ge(ske.s, ske.now(b, 2 * (g + 1)))
                    pe.wait_ge(sqe.s, sqe.now(b, 2 * (g + 1)))
                for h in range(GH):
                    n = g * 16 + i * GH + h
                    pe.wait_ge(mxs.s, mxs.now(b, n - 1) if n >= 2 else mxs.before(b, 64 + n - 1))
                    pe.matmul(bank(n % 2)[:, 0:(i + 1) * P],
                              QTs[0:SK, g * GH + h, i * P:(i + 1) * P],
                              KTs[0:SK, g * GH + h, 0:(i + 1) * P], start=True, stop=True)\
                        .then_inc(smm.s, 1)

            def minus_max(b, g):
                pe.wait_ge(mneg.s, mneg.now(b, 4 * (g + 1)))
                for m in range(2):
                    o = take(m, nte, nte.now(b, 2 * g + m + 1)).bitcast(BF16)
                    for h in range(2):
                        for i in range(TT):
                            mm = pe.transpose(o[SK:SX, (TT * h + i) * P:(TT * h + i + 1) * P],
                                              nst[:, g % 2, i, 2 * m + h, :], identb[:])
                    mm.then_inc(ntp.s, 1)

            def shifted(b, g, j):
                w = T - j * P
                if j == 0:
                    pe.wait_ge(nte.s, nte.now(b, 2 * g + 2))
                for n, heads in enumerate(SHARED[j], FIRST[j]):
                    if n >= 3:
                        pe.wait_ge(exq.s, exq.now(b, g * NSH + n - 2))
                    elif g > 0:
                        pe.wait_ge(exq.s, exq.now(b, (g - 1) * NSH + (10, 11, 9)[n]))
                    else:
                        pe.wait_ge(exq.s, exq.before(b, (NG - 1) * NSH + (10, 11, 9)[n]))
                    for a, h in enumerate(heads):
                        mm = pe.matmul(bank(2 + n % 3)[:, a * w:(a + 1) * w],
                                       KTs[0:SX, g * GH + h, j * P:(j + 1) * P],
                                       QTs[0:SX, g * GH + h, j * P:T], start=True, stop=True)
                    mm.then_inc(stm.s, 1)

            def values(b, g, j):
                pe.wait_ge(msk.s, msk.now(b, g * TT + j + 1))
                if j == 0:
                    pe.wait_ge(oev.s, oev.now(b, g) if g > 0 else oev.before(b, NG))
                    if g % 2 == 0:
                        pe.wait_ge(vev.s, vev.now(b, g // 2 + 1))
                for h in range(GH):
                    mm = pe.matmul(bank(6)[VW * h:VW * (h + 1), j * P:T], Vb[:, j, g * GH + h, :],
                                   pb[j % 2][:, h, 0:T - j * P], start=(j == 0),
                                   stop=(j == TT - 1))
                mm.then_inc(pvs.s, 1)

            def heads_out(b, g):
                pe.wait_ge(oev.s, oev.now(b, g + 1))
                o = take(1, odv, odv.now(b, 2 * g + 2))
                for t in range(TT):
                    mm = pe.transpose(o[:, t * P:(t + 1) * P], oTs[:, t * P:(t + 1) * P], ident[:])
                mm.then_inc(otp.s, 1)

            def pe_heads(b, k):
                pe.wait_ge(odv.s, odv.now(b, 2 * NG))
                turned(take(k, o2e, o2e.now(b, k + 1)), otok, k).then_inc(o2t.s, 1)

            def pe_output(b, m):
                pe.wait_ge(o2e.s, o2e.now(b, KT))
                projected(take(m, ln4, ln4.now(b, m + 1)), oT2, wo_s, m).then_inc(omm.s, 1)

            def pe_turn(b, k):
                pe.wait_ge(ln4.s, ln4.now(b, 2 + 3 * TT))
                turned(take(k, x2e, x2e.now(b, k + 1)), x2b, k).then_inc(x2t.s, 1)

            def pe_logits(b, k):
                pe.wait_ge(x2e.s, x2e.now(b, KT))
                o = take(0, lge, lge.now(b, 1))
                for k in range(KT):
                    mm = pe.matmul(o[0:64, :], wr_s[:, k, :], x2T[:, k, :],
                                   start=(k == 0), stop=(k == KT - 1))
                mm.then_inc(lgm.s, 1)

            pe_steps = {"context": pe_context, "query_in": pe_query_in, "key": pe_key,
                        "query": pe_query, "value": pe_value, "heads": pe_heads,
                        "stack_k": pe_stack(st, skt, ske, (ksa, ksd)),
                        "stack_q": pe_stack(stq, sqt, sqe, (qsa, qsd)),
                        "output": pe_output, "turn": pe_turn, "logits": pe_logits}

            def pe_do(steps):
                for name, c, k in steps:
                    if name in pe_steps:
                        pe_steps[name](c, k)

            def pe_slot(b, g, j, prev, then, *steps):
                shifted(b, g, j)
                if j == 0 and prev is not None:
                    heads_out(*prev)
                pe_do(steps[0])
                if then is not None:
                    for i in SCORED[j]:
                        scores(*then, i)
                pe_do(steps[1])
                if j > 0:
                    values(b, g, j - 1)
                if j == TT - 1:
                    if then is not None:
                        minus_max(*then)
                    values(b, g, j)
                pe_do(steps[2])

            pe_do([(name, 0, k) for name, k in all_steps(PREPARE)])
            for i in range(TT):
                scores(0, 0, i)
            minus_max(0, 0)
            slots(0, pe_slot, first=True)
            for k in range(2):
                pe.wait_ge(*read_by[k])
            with pe.Fori(0, B - 1) as b:
                read_by.update({0: (lge.s, lge.before(b, 1)), 1: (x2e.s, x2e.before(b, KT))})
                slots(b, pe_slot)
            read_by.update({0: (lge.s, lge.now(B - 2, 1)), 1: (x2e.s, x2e.now(B - 2, KT))})
            slots(B - 1, pe_slot, last=True)
            heads_out(B - 1, NG - 1)
            pe_do([(name, B - 1, k) for name, k in all_steps(FINISH)])

            for g in (xgt, h1m, htm, y2m):
                pe.sem_inc(g.s, g.per)
            pe.wait_ge(topk, CHOSEN)
            pe.transpose(bank(0)[:, 0:32], tw, ident[0:32, 0:32])
            pe.transpose(bank(0)[:, 32:64], ti, ident[0:32, 0:32]).then_inc(icm, 1)
            pe.wait_ge(topk, TOPK)
            pe.wait_ge(lge.s, lge.now(B - 1, 1))

            def tokens(p, u, r):
                pe.wait_ge(gathered[u], 16 * (r + 1))
                pe.wait_ge(xge.s, xge.before(p, 1))
                for k in range(KT):
                    mm = pe.transpose(bank(0)[:, k * P:(k + 1) * P],
                                      xg[u][:, k * P:(k + 1) * P], ident[:])
                mm.then_inc(xgt.s, 1)

            def first(p, u, r):
                pe.wait_ge(xge.s, xge.now(p, 1))
                pe.wait_ge(w_ring[u].s, w_ring[u].now(r, 1))
                for n in range(2):
                    pe.wait_ge((hea, hed)[n].s, (hea, hed)[n].before(p, 1))
                    for k in range(KT):
                        for e in range(2):
                            mm = pe.matmul(bank(1 + n)[CAP * e:CAP * (e + 1), :],
                                           xgT[:, k, CAP * e:CAP * (e + 1)],
                                           w1_of[u][:, e, k, n * 512:(n + 1) * 512],
                                           start=(k == 0), stop=(k == KT - 1))
                    mm.then_inc(h1m.s, 1)

            def across(p):
                for a in range(2):
                    pe.wait_ge((hea, hed)[a].s, (hea, hed)[a].now(p, 1))
                    pe.wait_ge(hbs.s, hbs.before(p, a + 1))
                    for c in range(4):
                        n = 4 * a + c
                        mm = pe.transpose(bank(3 + a)[:, c * P:(c + 1) * P],
                                          HB[:, n * P:(n + 1) * P], ident[:])
                    mm.then_inc(htm.s, 1)

            def second(p, u, r):
                pe.wait_ge(b_ring[u].s, b_ring[u].now(r, 1))
                pe.wait_ge(gel.s, gel.now(p, 2))
                pe.wait_ge(yws.s, yws.before(p, 1))
                y = bank(5 + u % 2)
                pe.matmul(y[:, 0:D], pair_of, b2_s[u], start=True, stop=False,
                          skip_group_check=True)
                for sl in range(S):
                    for m in range(M2 // P):
                        c = sl * (M2 // P) + m
                        for e in range(2):
                            mm = pe.matmul(y[CAP * e:CAP * (e + 1), sl * KO:(sl + 1) * KO],
                                           hb[:, c * P + CAP * e:c * P + CAP * (e + 1)],
                                           w2_of[u][:, e, sl, m, :], start=False,
                                           stop=(m == M2 // P - 1), skip_group_check=True)
                mm.then_inc(y2m.s, 1)

            pe.wait_ge(offs, 4)
            tokens(0, 0, 0)
            first(0, 0, 0)
            tokens(1, 1, 0)
            across(0)
            with pe.Fori(0, NP // RING - 1) as r:
                for u in range(RING):
                    p = r * RING + u
                    v = (u + 1) % RING
                    first(p + 1, v, r + (u + 1) // RING)
                    tokens(p + 2, (u + 2) % RING, r + (u + 2) // RING)
                    second(p, u, r)
                    across(p + 1)
            r = NP // RING - 1
            for u in range(RING):
                p = NP - RING + u
                if p + 1 < NP:
                    first(p + 1, u + 1, r)
                if p + 2 < NP:
                    tokens(p + 2, (u + 2) % RING, r + (u + 2) // RING)
                second(p, u, r)
                if p + 1 < NP:
                    across(p + 1)


def kernel(**inputs):
    from concourse import bacc as _bacc
    from concourse.bass_utils import run_bass_kernel_spmd as _run

    i = {k: np.asarray(v) for k, v in inputs.items()}
    w = lambda n: i["L0_" + n]
    col = lambda v: v.reshape(-1, P).T
    twice = lambda v: np.concatenate([v, v])[:, None]
    swap = lambda m: np.concatenate([m[NK:], m[:NK]])
    wi, wo = w("attn_w_in"), w("attn_w_out").T
    w1 = w("ffn_W1").reshape(NP, 2, S, KT, P, M2).transpose(0, 4, 1, 3, 2, 5).reshape(NP, P, W1C)
    w2 = w("ffn_W2").reshape(NP, 2, S, M2 // P, P, KO).transpose(0, 4, 1, 2, 3, 5)\
        .reshape(NP, P, W2C)
    arrays = {
        "x": i["x"], "ctx_in": i["ctx_1024"],
        "w_in": np.concatenate([wi, swap(wi)]).T,
        "w_gate": w("attn_w_gate").T,
        "w_out": np.stack([wo, swap(wo)]),
        "coupling": w("attn_coupling"),
        "w_mlp1": w("attn_w_mlp1").T, "w_mlp2": w("attn_w_mlp2").T,
        "w_q": w("xattn_wq_w").T,
        "w_kv": np.concatenate([w("xattn_wk_w"), w("xattn_wv_w")]).T,
        "w_o": w("xattn_wo_w").T,
        "w_r": np.stack([w("ffn_Wr")[0::2].T, w("ffn_Wr")[1::2].T]),
        "vecs": np.concatenate([col(w("attn_ln1_g")), col(w("attn_ln1_b")), col(w("attn_ln2_g")),
                                col(w("attn_ln2_b")), col(w("attn_b_mlp1")),
                                twice(w("attn_log_decay")), twice(w("attn_frequency"))], axis=1),
        "rows": np.concatenate([w("attn_b_gate"), w("attn_b_mlp2"), w("xattn_wk_b"),
                                w("xattn_wv_b"), w("xattn_wq_b"), w("xattn_wo_b")])[None],
        "b1": w("ffn_b1").reshape(NP, 2, S * M2 // P, P).transpose(3, 0, 2, 1),
        "b2": w("ffn_b2").reshape(NP, 2, D),
        "experts": np.concatenate([w1, w2], axis=2),
    }
    arrays = {n: np.ascontiguousarray(a) for n, a in arrays.items()}
    nc = _bacc.Bacc("TRN2", target_bir_lowering=False, num_devices=1)
    args = [nc.dram_tensor(n, a.shape, mybir.dt.from_np(a.dtype), kind="ExternalInput").ap()
            for n, a in arrays.items()]
    out = nc.dram_tensor("out", (B, T, D), F32, kind="ExternalOutput").ap()
    build(nc, *args, out)
    return _run(nc, [arrays], core_ids=[0]).results[0]["out"]
```

```python
from contextlib import ExitStack

import numpy as np
import concourse.bass as bass
from concourse import mybir

F32 = mybir.dt.float32
BF16 = mybir.dt.bfloat16
U32 = mybir.dt.uint32
I32 = mybir.dt.int32
ALU = mybir.AluOpType
ACT = mybir.ActivationFunctionType
AX = mybir.AxisListType

P = 128
B, T, D = 4, 512, 256
TT = T // P
KT = D // P
NK = 64
C = 64
NCH = T // C
CH, CK = 4, 16
MLP = 1024
MT = MLP // P
NH, HD = 16, 16
GH = 4
NG = NH // GH
NPC = 3
NPR = 6
SK = NPR * HD
SX = SK + NPC
VW = 32
E, S = 48, 4
M2 = 256
KO = D // S
CAP = int(1.5 * B * T / E)
NP = E // 2
RING = 6
W1C = 2 * KT * S * M2
W2C = 2 * S * (M2 // P) * KO
ARENA = 21120
EPS = 1e-5
NEG = -3.0e38

SHARED = [[(0,), (1,), (2,), (3,)], [(0,), (1,), (2,), (3,)], [(0, 1), (2, 3)], [(0, 1, 2, 3)]]
FIRST = [0, 4, 8, 10]
NSH = 11
SHARED_Q = SHARED[::-1]
FOUND = [int(n) for n in np.cumsum([len(heads) for tile in SHARED_Q for heads in tile])]
TILES_OF = [(0, 1), (2,), (3,), ()]
CUTS = [(2, 3), (2, 3), (0, 4), (0, 0)]


def _cut(tiles, cuts):
    banks = [(i, n, heads) for i in tiles
             for n, heads in enumerate(SHARED_Q[i], sum(len(q) for q in SHARED_Q[:i]))]
    return banks[:cuts[0]], banks[cuts[0]:cuts[1]], banks[cuts[1]:]


SCORED = [_cut(tiles, cuts) for tiles, cuts in zip(TILES_OF, CUTS)]

PREPARE = {
    (1, 0): ([("context", 0)], [], [("context", 1), ("query_in", 0)]),
    (1, 1): ([("query_in", 1), ("key", 0)], [("key", 1), ("split_k", 0)],
            [("split_k", 1), ("query", 0)]),
    (1, 2): ([("split_k", 2)], [("query", 1)], [("split_k", 3), ("split_q", 0)]),
    (1, 3): ([], [("split_q", 1)], [("split_q", 2), ("value", 0)]),
    (2, 0): ([("split_q", 3)], [], []),
    (2, 1): ([("stack_k", 0), ("stack_k", 1)], [], [("stack_q", 0)]),
    (2, 2): ([], [], [("stack_q", 1)]),
    (2, 3): ([], [], [("stack_k", 2)]),
    (3, 0): ([], [("stack_k", 3)], []),
    (3, 1): ([], [("stack_q", 2), ("stack_q", 3)], []),
    (3, 2): ([("stack_k", 4), ("stack_k", 5)], [("stack_q", 4)], []),
    (3, 3): ([("stack_q", 5)], [], []),
}
ENTER = {
    (0, 0): ([], [], [("value", 1)]),
    (0, 2): ([("stack_k", 6)], [("stack_k", 7), ("stack_q", 6)], []),
    (0, 3): ([], [("stack_q", 7)], []),
}
FINISH = {
    (0, 0): ([], [("heads", 0)], []),
    (0, 1): ([("heads", 1)], [("output", 0)], [("output", 1), ("stats", 0)]),
    (0, 2): ([], [], [("norm", 0)]),
    (0, 3): ([], [], [("turn", 0), ("turn", 1), ("logits", 0)]),
}

TWO_PI_HI = 6.28125
TWO_PI_LO = 2 * np.pi - 6.28125
ROUND = 12582912.0

V_G1, V_B1, V_G2, V_B2, V_BM, V_DEC, V_FRQ = 0, 2, 4, 6, 8, 16, 17
VCOLS = 18
R_GATE, R_M2, R_K, R_V, R_Q, R_O = (256 * n for n in range(6))
RCOLS = 6 * 256


class Signal:

    def __init__(self, sem, per, unit=1):
        self.s, self.per, self.unit = sem, per, unit

    def now(self, b, k):
        return (b * self.per + (self.per + k)) * self.unit

    def before(self, b, k):
        return (b * self.per + k) * self.unit


def build(nc, x, ctx_in, w_in, w_gate, w_out, coupling, w_mlp1, w_mlp2, w_q, w_kv, w_o, w_r,
          vecs, rows, b1, b2, experts, out):
    x2_rows = nc.dram_tensor("x2_rows", (B * T, D), F32, kind="Internal").ap()
    sums = nc.dram_tensor("sums", (2 * B * T, D), F32, kind="Internal").ap()

    stack = ExitStack()
    with stack:
        def sb(name, shape, dt=F32):
            return stack.enter_context(nc.sbuf_tensor(name, shape, dt))

        def sem(name):
            return stack.enter_context(nc.semaphore(name))

        def signal(name, per, unit=1):
            return Signal(sem(name), per, unit)

        PS = stack.enter_context(nc.psum_tensor("PS", [P, 8 * 512], F32))

        def bank(n, k=1):
            return PS[:, n * 512:(n + k) * 512]

        X = sb("X", [P, B * TT, D])
        Y = sb("Y", [P, B * TT, D])
        A = sb("arena", [P, ARENA])
        ring_a = sb("ring_a", [P, 3, W1C + W2C])
        ident = sb("ident", [P, P])
        identb = sb("identb", [P, P], BF16)
        cos_t = sb("cos_t", [P, C])
        sin_t = sb("sin_t", [P, C])
        vec = sb("vec", [P, VCOLS])
        row = sb("row", [P, RCOLS])
        wq_s = sb("wq_s", [P, KT, D])
        wkv_s = sb("wkv_s", [P, KT, 2 * D])
        wo_s = sb("wo_s", [P, KT, D])
        wr_s = sb("wr_s", [P, KT, 64])
        stats = sb("stats", [P, TT, 6])
        mv = sb("mv", [P, TT, 2])
        ve = sb("ve", [P, TT])
        rstd = sb("rstd", [P, TT])
        mhalf = sb("mhalf", [P, TT])
        causal = sb("causal", [P, T], BF16)
        junk = sb("junk", [P, 2, T], BF16)
        Mx = sb("Mx", [P, 2, TT, GH])
        Mr = sb("Mr", [P, TT, GH])
        nst = sb("nst", [P, 2, TT, GH, NPC], BF16)
        zrow = sb("zrow", [P, D])
        rden = sb("rden", [P, TT, GH])

        used = [0]

        def carve(n):
            a = used[0]
            used[0] += n
            assert used[0] <= ARENA, used
            return A[:, a:a + n]

        wm1_s = carve(KT * MLP).rearrange("p (k n) -> p k n", k=KT)
        wm2_s = carve(MT * D).rearrange("p (k n) -> p k n", k=MT)
        hid = carve(MT * T).rearrange("p (k n) -> p k n", k=MT)
        xT2 = carve(KT * T).rearrange("p (k n) -> p k n", k=KT)
        xn = carve(TT * D).rearrange("p (t n) -> p t n", t=TT)
        mlp_end = used[0]
        wi_s = carve(KT * 256).rearrange("p (k n) -> p k n", k=KT)
        wg_s = carve(KT * D).rearrange("p (k n) -> p k n", k=KT)
        wc_s = carve(2 * D).rearrange("p (k n) -> p k n", k=2)
        wout_s = carve(2 * D).rearrange("p (k n) -> p k n", k=2)
        cb_s = carve(P)
        decay = carve(T)
        rot = carve(T)
        rot2 = carve(T)
        ysc = carve(T)
        yc = carve(T)
        ys = carve(T)
        xT1 = carve(KT * T).rearrange("p (k n) -> p k n", k=KT)
        gz = carve(TT * D).rearrange("p (t n) -> p t n", t=TT)
        hg = carve(TT * D).rearrange("p (t n) -> p t n", t=TT)
        ph_i = carve(C).bitcast(I32)
        ph = carve(C)
        ph_n = carve(C)
        ph_m = carve(C)
        mag = carve(1)
        used[0] = 0
        KTs = carve(NH * T // 2).bitcast(BF16).rearrange("p (h n) -> p h n", h=NH)
        QTs = carve(NH * T // 2).bitcast(BF16).rearrange("p (h n) -> p h n", h=NH)
        pbs = carve(2 * GH * T)
        pb = [pbs[:, n * GH * T:(n + 1) * GH * T].rearrange("p (h n) -> p h n", h=GH)
              for n in range(2)]
        oTs = carve(T)
        assert used[0] >= mlp_end
        aT = carve(KT * T).rearrange("p (k n) -> p k n", k=KT)
        Vb = carve(TT * NH * VW).rearrange("p (t h v) -> p t h v", t=TT, h=NH)
        prepared = used[0]
        cT = carve(KT * T).rearrange("p (k n) -> p k n", k=KT)
        kq = carve(TT * D)
        st = carve(TT * NH * (SK + 4) // 2).bitcast(BF16)\
            .rearrange("p (t h s) -> p t h s", t=TT, h=NH)
        over = ring_a[:, 0, :]
        stq = over[:, 0:TT * NH * SK // 2].bitcast(BF16)\
            .rearrange("p (t h s) -> p t h s", t=TT, h=NH)
        qt = over[:, TT * NH * SK // 2:TT * NH * SK // 2 + TT * D]
        x2b = over[:, TT * NH * SK // 2 + TT * D:TT * NH * SK // 2 + 2 * TT * D]\
            .rearrange("p (t n) -> p t n", t=TT)
        yr = Y[:, :, :].rearrange("p a d -> p (a d)")
        ctxb = yr[:, 0:1024].rearrange("p (t n) -> p t n", t=TT)
        otok = yr[:, 1024:2048].rearrange("p (t n) -> p t n", t=TT)
        oT2 = yr[:, 2048:3072].rearrange("p (k n) -> p k n", k=KT)
        xs = yr[:, 3072:4096].rearrange("p (t n) -> p t n", t=TT)
        x2T = aT
        LGs = sb("LGs", [64, B, T])
        assert W1C <= TT * NH * SK // 2 + TT * D
        used[0] = 0
        slot = [ring_a[:, n, :] for n in range(3)] + [A[:, prepared:prepared + W1C + W2C]]
        slot += [carve(W1C + W2C) for _ in range(3)]
        assert used[0] <= prepared <= ARENA - W1C - W2C
        w1_of = [w[:, 0:W1C].rearrange("p (e k n) -> p e k n", e=2, k=KT) for w in slot]
        w2_of = [w[:, W1C:].rearrange("p (e s m k) -> p e s m k", e=2, s=S, m=M2 // P)
                 for w in slot]
        x_flat = X[:, :, :].rearrange("p a d -> p (a d)")
        LG2 = yr[:, 0:1024]
        top_v = yr[:, 1024:1088]
        top_i = yr[:, 1088:1152].bitcast(U32)
        top_f = yr[:, 1152:1216]
        pick = yr[:, 1216:1280]
        sel_v = yr[:, 1280:1344]
        sel_i = yr[:, 1344:1408]
        far_v = yr[:, 1408:1472]
        far_i = yr[:, 1472:1536]
        tw = yr[0:32, 1536:1664]
        ti = yr[0:32, 1664:1792]
        smx = yr[:, 1792:1800]
        wcol = yr[:, 1800:1824]
        icol = yr[:, 1824:1848].bitcast(U32)
        jcol = yr[:, 1848:1872].bitcast(U32)
        icf = yr[:, 1872:1896]
        jcf = yr[:, 1896:1920]
        off = yr[:, 1920:1921]
        b1_s = yr[:, 2048:2432].rearrange("p (e c a) -> p e c a", e=NP, a=2)
        pair_of = yr[0:2, 2432:2560]
        HB = x_flat[:, 0:1024]
        hb = x_flat[:, 1024:2048]
        b2_s = [x_flat[0:2, 2048 + n * D:2048 + (n + 1) * D] for n in range(4)]
        b2_s += [yr[0:2, 3072 + n * D:3072 + (n + 1) * D] for n in range(2)]
        flat = [m[:, :, :].rearrange("p k n -> p (k n)") for m in (wkv_s, wq_s, wo_s)] + [row]
        free = [(m, a) for m in flat for a in range(0, m.shape[1], D)]

        def reuse():
            m, a = free.pop(0)
            return m[:, a:a + D]

        xg = [reuse() for _ in range(RING)]
        xgT = x_flat[:, 3584:3840].rearrange("p (k n) -> p k n", k=KT)
        ye = [reuse() for _ in range(RING)]
        small = reuse()
        gidx = [small[:, n:n + 1].bitcast(U32) for n in range(RING)]
        sidx = [small[:, RING + n:RING + n + 1].bitcast(U32) for n in range(RING)]
        fstats = small[:, 128:128 + B * TT * 6].rearrange("p (a n) -> p a n", n=6)
        fmv = small[:, 32:32 + B * TT * 2].rearrange("p (a n) -> p a n", n=2)
        fve = small[:, 64:64 + B * TT]
        frstd = small[:, 80:80 + B * TT]
        fshift = small[:, 96:96 + B * TT]

        w_one = sem("w_one")
        w_mlp = sem("w_mlp")
        w_att = sem("w_att")
        consts = sem("consts")
        setup = sem("setup")
        trig = sem("trig")
        wc_mm = sem("wc_mm")
        x_in = signal("x_in", 1, 16)
        ln1 = signal("ln1", 2 * TT + TT)
        rs1 = signal("rs1", 2)
        xt1 = signal("xt1", 1)
        xe1 = signal("xe1", 2)
        beta = signal("beta", 2)
        rots = signal("rots", 5)
        gpre = signal("gpre", 1)
        gact = signal("gact", 1)
        yrot = signal("yrot", 2)
        hmm = signal("hmm", 1)
        hgs = signal("hgs", 1)
        res = signal("res", 3)
        ln2 = signal("ln2", 3 * TT)
        rs2 = signal("rs2", 2)
        xt2 = signal("xt2", 1)
        xe2 = signal("xe2", 2)
        m1 = signal("m1", MT)
        silu = signal("silu", MT)
        m2 = signal("m2", 1)
        ln3 = signal("ln3", 1 + 3 * TT)
        rs3 = signal("rs3", 2)
        c_in = signal("c_in", 1, 16)
        xs_in = signal("xs_in", 1, 16)
        xob = signal("xob", 1)
        ctp = signal("ctp", KT)
        cte = signal("cte", KT)
        xtp = signal("xtp", KT)
        xte = signal("xte", KT)
        kpr = signal("kpr", 2)
        kev = signal("kev", 2)
        qpr = signal("qpr", 2)
        qev = signal("qev", 2)
        vpr = signal("vpr", 2)
        vev = signal("vev", 2)
        ksa = signal("ksa", 2)
        ksd = signal("ksd", 4)
        qsa = signal("qsa", 2)
        qsd = signal("qsd", 5)
        skt = signal("skt", 2 * NG)
        ske = signal("ske", 2 * NG)
        sqt = signal("sqt", 2 * NG)
        sqe = signal("sqe", 2 * NG)
        smm = signal("smm", NG * NSH)
        mxs = signal("mxs", NG * 16)
        mneg = signal("mneg", NG * 4)
        ntp = signal("ntp", NG * 2)
        nte = signal("nte", NG * 2)
        stm = signal("stm", NG * NSH)
        exq = signal("exq", NG * NSH)
        msk = signal("msk", NG * TT)
        pvs = signal("pvs", NG * TT)
        oev = signal("oev", NG)
        otp = signal("otp", NG)
        odv = signal("odv", NG * 2)
        o2t = signal("o2t", KT)
        o2e = signal("o2e", KT)
        omm = signal("omm", 2)
        ln4 = signal("ln4", 2 + 3 * TT)
        rs4 = signal("rs4", 2)
        x2t = signal("x2t", KT)
        x2e = signal("x2e", KT)
        lgm = signal("lgm", 1)
        lge = signal("lge", 1)
        x2o = signal("x2o", 2, 16)
        zsum = sem("zsum")
        b1_in = sem("b1_in")
        topk = sem("topk")
        wexp = sem("wexp")
        icm = sem("icm")
        w1_ring = [signal(f"w1_ring{n}", 1, 16) for n in range(RING + 1)]
        w2_ring = [signal(f"w2_ring{n}", 1, 16) for n in range(RING + 1)]
        b_ring = [signal(f"b_ring{n}", 1, 16) for n in range(RING)]
        gix = signal("gix", 1)
        six = signal("six", 1)
        gathered = [sem(f"gathered{n}") for n in range(RING)]
        scattered = sem("scattered")
        added = signal("added", RING)
        xgt = signal("xgt", 1)
        xge = signal("xge", 1)
        h1m = signal("h1m", 2)
        hea = signal("hea", 1)
        hed = signal("hed", 1)
        htm = signal("htm", 2)
        hbs = signal("hbs", 2)
        gel = signal("gel", 2)
        y2m = signal("y2m", 1)
        yws = signal("yws", 2)
        fin_in = [sem(f"fin_in{n}") for n in range(B)]
        fsum = sem("fsum")
        fstat = sem("fstat")
        fvar = sem("fvar")
        froot = sem("froot")
        fout = sem("fout")
        stored = sem("stored")
        vset = sem("vset")
        pool_held = sem("pool_held")
        dve_held = sem("dve_held")
        setup_cb = sem("setup_cb")
        offs = sem("offs")
        SHIFTED, CHOSEN, TOPK = 36, 42, 47
        CONSTS, SETUP, W_ONE = 12, 19, 16 * 13

        x_v = x.rearrange("b (t p) d -> b p t d", p=P)
        ctx_v = ctx_in.rearrange("b (t p) d -> b p t d", p=P)
        out_v = out.rearrange("b (t p) d -> p (b t) d", p=P)
        x2_v = x2_rows.rearrange("(b t p) d -> b p t d", p=P, b=B)
        sums_v = sums.rearrange("(a b t p) d -> a b p t d", p=P, b=B, a=2)

        def wide(ap, n):
            return ap.unsqueeze(1).to_broadcast([ap.shape[0], n, ap.shape[1]])

        spare_banks = [5, 7]

        def spare(k):
            return bank(spare_banks[k % 2])

        def slots(b, do, first=False, last=False):
            for g in ([0] if first else range(1, NG) if last else [1, 2, 3, 0]):
                c = b + 1 if g == 0 and not first else b
                prev = None if first else (c, g - 1) if g > 0 else (b, NG - 1)
                then = None if last and g == NG - 1 else (c, g + 1) if g + 1 < NG else (c + 1, 0)
                for j in range(TT):
                    tables = []
                    if not first and not last:
                        tables.append((PREPARE, b + 1))
                        tables.append((FINISH, b))
                    if g == 0:
                        tables.append((ENTER, c))
                    steps = [], [], []
                    for table, batch in tables:
                        for n, names in enumerate(table.get((g, j), steps[:0])):
                            steps[n].extend((name, batch, k) for name, k in names)
                    do(c, g, j, prev, then, *steps)

        def all_steps(table):
            return [step for lists in table.values() for names in lists for step in names]

        after = ("stack_k", 0), ("stack_q", 0)
        first_steps = all_steps(PREPARE)
        split_at = min(first_steps.index(step) for step in after)
        early = [(name, 0, k) for name, k in first_steps[:split_at]]
        late = [(name, 0, k) for name, k in first_steps[split_at:]]

        block = stack.enter_context(nc.Block())

        @block.sync
        def _(sp):
            sp.sem_inc(x_in.s, 16)
            with sp.Fori(0, B) as b:
                sp.wait_ge(x_in.s, x_in.before(b, 1))
                sp.dma_start(X[:, bass.ts(b, TT), :], x_v[b]).then_inc(x_in.s, 16)

            def weights(u, p, first=True, second=True):
                if first:
                    sp.dma_start(slot[u][:, 0:W1C], experts[p][:, 0:W1C])\
                        .then_inc(w1_ring[u].s, 16)
                if second:
                    sp.dma_start(slot[u][:, W1C:], experts[p][:, W1C:])\
                        .then_inc(w2_ring[u].s, 16)

            for u in (1, 2):
                weights(u, u)
            sp.wait_ge(consts, CONSTS)
            sp.dma_start(sums[B * T:, :].rearrange("(a p) d -> p a d", p=P), wide(zrow[:], B * TT))\
                .then_inc(zsum, 16)
            sp.sem_inc(c_in.s, 16)
            sp.sem_inc(xs_in.s, 16)
            sp.sem_inc(x2o.s, 32)

            def inputs(b):
                sp.wait_ge(ctp.s, ctp.before(b, KT))
                sp.dma_start(ctxb, ctx_v[b]).then_inc(c_in.s, 16)
                sp.wait_ge(ln3.s, ln3.now(b, 1 + 3 * TT))
                sp.wait_ge(xtp.s, xtp.before(b, KT))
                sp.dma_start(xs, X[:, bass.ts(b, TT), :]).then_inc(xs_in.s, 16)

            def outputs(b):
                sp.wait_ge(ln4.s, ln4.now(b, 2 + 3 * TT))
                sp.dma_start(x2_v[b], x2b).then_inc(x2o.s, 16)
                sp.dma_start(sums_v[0, b], x2b).then_inc(x2o.s, 16)

            sp.wait_ge(ln2.s, ln2.now(B - 1, 3 * TT))
            sp.wait_ge(res.s, res.now(B - 1, 3))
            inputs(0)
            with sp.Fori(0, B - 1) as b:
                inputs(b + 1)
                outputs(b)
            sp.wait_ge(skt.s, skt.now(B - 1, 2 * NG))
            sp.wait_ge(vpr.s, vpr.now(B - 1, 2))
            weights(3, 3)
            sp.wait_ge(sqt.s, sqt.now(B - 1, 2 * NG))
            weights(0, 0, second=False)
            outputs(B - 1)

            for g in w1_ring + w2_ring + b_ring:
                sp.sem_inc(g.s, 16)
            sp.wait_ge(lge.s, lge.now(B - 1, 1))
            sp.dma_start(b1_s, b1).then_inc(b1_in, 16)
            sp.wait_ge(x2o.s, x2o.now(B - 1, 2))
            sp.wait_ge(x2t.s, x2t.now(B - 1, KT))
            for u in range(RING):
                if u not in (1, 2, 3):
                    weights(u, u, first=(u > 0))
                sp.dma_start(b2_s[u], b2[u]).then_inc(b_ring[u].s, 16)
            weights(RING, NP - 1)

            def refill(r, ring):
                for u in ring:
                    sp.wait_ge(h1m.s, h1m.now((r - 1) * RING + u, 2))
                    weights(u, r * RING + u, second=False)
                    sp.wait_ge(y2m.s, y2m.now((r - 1) * RING + u, 1))
                    weights(u, r * RING + u, first=False)
                    sp.dma_start(b2_s[u], b2[r * RING + u]).then_inc(b_ring[u].s, 16)

            with sp.Fori(1, NP // RING - 1) as r:
                refill(r, range(RING))
            refill(NP // RING - 1, range(RING - 1))
            sp.wait_ge(y2m.s, y2m.now(NP - RING - 1, 1))
            sp.dma_start(b2_s[RING - 1], b2[NP - 1]).then_inc(b_ring[RING - 1].s, 16)
            sp.wait_ge(scattered, 16 * NP)
            for b in range(B):
                sp.dma_start(X[:, b * TT:(b + 1) * TT, :], sums_v[0, b]).then_inc(fin_in[b], 16)
                sp.dma_start(Y[:, b * TT:(b + 1) * TT, :], sums_v[1, b]).then_inc(fin_in[b], 16)
            for b in range(B):
                sp.wait_ge(fout, (b + 1) * TT)
                sp.dma_start(out_v[:, b * TT:(b + 1) * TT, :], X[:, b * TT:(b + 1) * TT, :])\
                    .then_inc(stored, 16)
            sp.wait_ge(stored, 16 * B)

        @block.gpsimd
        def _(pool):
            for g in (rs1, yrot, res, rs2, rs3):
                pool.sem_inc(g.s, g.per)
            step = [0]

            def const(ins):
                step[0] += 1
                ins.then_inc(consts, 1)

            def settle():
                pool.wait_ge(consts, step[0])

            const(pool.memset(ident[:], 0.0))
            pool.memset(cb_s, 0.0).then_inc(setup_cb, 1)
            const(pool.memset(identb[:], 0.0))
            const(pool.memset(causal[:], 0.0))
            const(pool.memset(mhalf[:], -0.5))
            const(pool.memset(wr_s[:], 0.0))
            const(pool.memset(zrow[:], 0.0))
            const(pool.memset(decay, 1.0))
            const(pool.iota(ph_i, pattern=[[1, C]], base=0, channel_multiplier=0))
            settle()
            for m in (ident, identb):
                const(pool.affine_select(out=m[:], in_=m[:], compare_op=ALU.not_equal, fill=1.0,
                                         base=0, pattern=[[-1, P]], channel_multiplier=1))
            const(pool.affine_select(out=causal[:, T - P:], in_=causal[:, T - P:],
                                     compare_op=ALU.is_ge, fill=NEG, base=0,
                                     pattern=[[-1, P]], channel_multiplier=1))
            settle()
            const(pool.memset(decay.rearrange("p (n c) -> p n c", c=C)[:, :, C - 1:C], 0.0))

            def root(norm, rs, b, k):
                pool.wait_ge(norm.s, norm.now(b, k))
                pool.sem_inc(pool_held, 1)
                pool.tensor_scalar(ve[:], mv[:, :, 1], EPS, None, ALU.add).then_inc(rs.s, 1)
                pool.wait_ge(rs.s, rs.now(b, 1))
                pool.tensor_tensor(rstd[:], ve[:], mhalf[:], ALU.pow).then_inc(rs.s, 1)

            def rotated(b):
                pool.wait_ge(rots.s, rots.now(b, 5))
                pool.wait_ge(hmm.s, hmm.before(b, 1))
                y3 = ysc.rearrange("p (n c) -> p n c", c=C)
                pool.tensor_tensor(yc.rearrange("p (n c) -> p n c", c=C), y3,
                                   wide(cos_t[:], NCH), ALU.mult).then_inc(yrot.s, 1)
                pool.tensor_tensor(ys.rearrange("p (n c) -> p n c", c=C), y3,
                                   wide(sin_t[:], NCH), ALU.mult).then_inc(yrot.s, 1)

            def residual(b):
                pool.wait_ge(hgs.s, hgs.now(b, 1))
                pool.sem_inc(pool_held, 1)
                xb, yb = X[:, bass.ts(b, TT), :], Y[:, bass.ts(b, TT), :]
                pool.tensor_tensor(yb, xb, hg, ALU.add).then_inc(res.s, 1)

            def ahead(b):
                xb, yb = X[:, bass.ts(b, TT), :], Y[:, bass.ts(b, TT), :]
                pool.wait_ge(res.s, res.now(b, 1))
                pool.sem_inc(pool_held, 1)
                pool.tensor_tensor(xb, xb, yb, ALU.add).then_inc(res.s, 1)
                pool.wait_ge(res.s, res.now(b, 2))
                pool.sem_inc(pool_held, 1)
                pool.tensor_tensor(xb, xb, wide(row[:, R_M2:R_M2 + D], TT), ALU.add)\
                    .then_inc(res.s, 1)

            def recurrence(b):
                rotated(b)
                residual(b)
                root(ln2, rs2, b, 2 * TT)
                ahead(b)

            root(ln1, rs1, 0, 2 * TT)
            pool.wait_ge(w_one, W_ONE)
            recurrence(0)
            with pool.Fori(0, B - 1) as b:
                root(ln1, rs1, b + 1, 2 * TT)
                recurrence(b + 1)
                root(ln3, rs3, b, 1 + 2 * TT)
            pool.wait_ge(hmm.s, hmm.now(B - 1, 1))
            pool.memset(Vb, 0.0).then_inc(vset, 1)
            pool.wait_ge(vset, 1)
            pool.memset(Vb[:, :, :, HD:HD + 1], 1.0).then_inc(vset, 1)
            pool.wait_ge(vset, 2)
            pool.memset(st[:, :, :, SK:SX], 1.0).then_inc(vset, 1)
            pool.wait_ge(vset, 3)
            root(ln3, rs3, B - 1, 1 + 2 * TT)
            pool.wait_ge(rs3.s, rs3.now(B - 1, 2))

            for g in (xob, msk, rs4):
                pool.sem_inc(g.s, g.per)

            def with_bias(b):
                xb = X[:, bass.ts(b, TT), :]
                pool.wait_ge(xs_in.s, xs_in.now(b, 1))
                pool.sem_inc(pool_held, 1)
                pool.tensor_tensor(xb, xb, wide(row[:, R_O:R_O + D], TT), ALU.add)\
                    .then_inc(xob.s, 1)

            def pool_slot(b, g, j, prev, then, *steps):
                pool.wait_ge(exq.s, exq.now(b, g * NSH + FIRST[j] + len(SHARED[j])))
                pool.sem_inc(pool_held, 1)
                pool.affine_select(out=pb[j % 2][:, :, 0:P], in_=pb[j % 2][:, :, 0:P],
                                   compare_op=ALU.is_ge, fill=0.0, base=0,
                                   pattern=[[0, GH], [1, P]], channel_multiplier=-1)\
                    .then_inc(msk.s, 1)
                for name, c, k in steps[0] + steps[1] + steps[2]:
                    if name == "value" and k == 0:
                        with_bias(c)
                    elif name == "stats":
                        root(ln4, rs4, c, 2 + 2 * TT)

            with_bias(0)
            slots(0, pool_slot, first=True)
            with pool.Fori(0, B - 1) as b:
                slots(b, pool_slot)
            slots(B - 1, pool_slot, last=True)
            root(ln4, rs4, B - 1, 2 + 2 * TT)

            for g in (gix, six, added):
                pool.sem_inc(g.s, g.per * g.unit)
            pool.wait_ge(lge.s, lge.now(B - 1, 1))
            pool.wait_ge(xtp.s, xtp.now(B - 1, KT))
            pool.memset(off[0:64, :], 0.0).then_inc(offs, 1)
            pool.memset(off[64:P, :], float(B * T)).then_inc(offs, 1)
            pool.memset(pair_of, 0.0).then_inc(offs, 1)
            pool.wait_ge(offs, 3)
            pool.affine_select(out=pair_of, in_=pair_of, compare_op=ALU.not_equal, fill=1.0, base=0,
                               pattern=[[-1, 2], [0, CAP]], channel_multiplier=1).then_inc(offs, 1)
            pool.wait_ge(topk, TOPK)
            pool.wait_ge(zsum, 16)
            pool.wait_ge(x2o.s, x2o.now(B - 1, 2))

            def gather(p, u, again=False):
                if again:
                    pool.wait_ge(xgt.s, xgt.now(p - RING, 1))
                    pool.sem_inc(pool_held, 1)
                pool.tensor_copy(gidx[u], icol[:, bass.ds(p, 1)]).then_inc(gix.s, 1)
                pool.wait_ge(gix.s, gix.now(p, 1))
                pool.sem_inc(pool_held, 1)
                pool.indirect_dma_start(
                    xg[u], None, x2_rows,
                    bass.IndirectOffsetOnAxis(ap=gidx[u], axis=0)).then_inc(gathered[u], 16)

            def scatter(p, u):
                pool.tensor_copy(sidx[u % RING], jcol[:, bass.ds(p, 1)]).then_inc(six.s, 1)
                pool.wait_ge(six.s, six.now(p, 1))
                pool.sem_inc(pool_held, 1)
                pool.wait_ge(yws.s, p + 3)
                pool.sem_inc(pool_held, 1)
                pool.indirect_dma_start(
                    sums, bass.IndirectOffsetOnAxis(ap=sidx[u % RING], axis=0), ye[u % RING], None,
                    compute_op=ALU.add).then_inc(scattered, 16)

            def after_addition(p):
                pool.wait_ge(scattered, (p + 1) * 16)
                pool.sem_inc(added.s, 1)

            for p in range(RING):
                gather(p, p)
            with pool.Fori(0, NP // RING - 1) as r:
                for u in range(RING):
                    p = r * RING + u
                    scatter(p, u)
                    gather(p + RING, u, again=True)
                    after_addition(p)
            for p in range(NP - RING, NP):
                scatter(p, p)
                after_addition(p)
            for b in range(B):
                tiles = slice(b * TT, (b + 1) * TT)
                pool.wait_ge(fvar, (b + 1) * TT)
                pool.tensor_scalar(fve[:, tiles], fmv[:, tiles, 1], EPS, None, ALU.add)\
                    .then_inc(froot, 1)
                pool.wait_ge(froot, 4 * b + 1)
                pool.tensor_tensor(frstd[:, tiles], fve[:, tiles], mhalf[:], ALU.pow)\
                    .then_inc(froot, 1)
                pool.wait_ge(froot, 4 * b + 2)
                pool.tensor_tensor(fshift[:, tiles], fmv[:, tiles, 0], frstd[:, tiles], ALU.mult)\
                    .then_inc(froot, 1)
                pool.wait_ge(froot, 4 * b + 3)
                pool.tensor_scalar(fshift[:, tiles], fshift[:, tiles], -1.0, None, ALU.mult)\
                    .then_inc(froot, 1)

        @block.vector
        def _(dve):
            for g in (ln1, rots, gpre, hgs, ln2, ln3):
                dve.sem_inc(g.s, g.per)
            step = [0]

            def link(ins):
                step[0] += 1
                ins.then_inc(setup, 1)
                dve.wait_ge(setup, step[0])

            def statistics(sig, src, first, b, k):
                tile = lambda t: src[:, first + t, :]
                dve.sem_inc(dve_held, 1)
                for t in range(TT):
                    dve.bn_stats(stats[:, t, :], tile(t)).then_inc(sig.s, 1)
                dve.wait_ge(sig.s, sig.now(b, k + TT))
                dve.sem_inc(dve_held, 1)
                for t in range(TT):
                    dve.bn_aggr(mv[:, t, :], stats[:, t, :]).then_inc(sig.s, 1)

            def norm(sig, rs, src, dst, first, b, before=None):
                tile = lambda t: src[:, first + t, :]
                dve.wait_ge(rs.s, rs.now(b, 2))
                if before is not None:
                    dve.wait_ge(*before)
                for t in range(TT):
                    dve.tensor_scalar(dst(t), tile(t),
                                      mv[:, t, 0:1], rstd[:, t:t + 1],
                                      ALU.subtract, ALU.mult).then_inc(sig.s, 1)

            def ln_in(b):
                dve.wait_ge(x_in.s, x_in.now(b, 1))
                statistics(ln1, X, b * TT, b, 0)
                norm(ln1, rs1, X, lambda t: xn[:, t, :], b * TT, b, (xt2.s, xt2.before(b, 1)))

            ln_in(0)
            dve.wait_ge(consts, CONSTS)
            dve.wait_ge(w_one, W_ONE)
            link(dve.tensor_copy(ph, ph_i))
            link(dve.tensor_scalar(ph, ph, vec[:, V_FRQ:V_FRQ + 1], None, ALU.mult))
            for turn, dst in ((0.0, rot[:, 0:C]), (0.25, rot[:, C:2 * C])):
                link(dve.tensor_scalar(ph_n, ph, float(1 / (2 * np.pi)), turn, ALU.mult, ALU.add))
                link(dve.tensor_scalar(ph_n, ph_n, ROUND, None, ALU.add))
                link(dve.tensor_scalar(ph_n, ph_n, ROUND, None, ALU.subtract))
                link(dve.scalar_tensor_tensor(ph_m, ph_n, -TWO_PI_HI, ph, ALU.mult, ALU.add))
                link(dve.scalar_tensor_tensor(ph_m, ph_n, -TWO_PI_LO, ph_m, ALU.mult, ALU.add))
                link(dve.tensor_scalar(ph_m, ph_m, 2 * np.pi * turn, 3.1415925, ALU.add, ALU.min))
                link(dve.tensor_scalar(dst, ph_m, -3.1415925, None, ALU.max))
            dve.wait_ge(trig, 3)
            link(dve.tensor_scalar(decay, decay, mag, None, ALU.mult))
            link(dve.tensor_scalar(sin_t[0:NK, :], sin_t[0:NK, :], -1.0, None, ALU.mult))
            dve.wait_ge(wc_mm, 1)
            link(dve.tensor_copy(wc_s, bank(4).rearrange("p (k n) -> p k n", k=2)))
            assert step[0] == SETUP, step

            def rotate(b):
                ps0 = bank(2).rearrange("p (n c) -> p n c", c=C)
                ps1 = bank(3).rearrange("p (n c) -> p n c", c=C)
                dve.wait_ge(beta.s, beta.now(b, 1))
                dve.tensor_tensor(rot.rearrange("p (n c) -> p n c", c=C), ps0,
                                  wide(cos_t[:], NCH), ALU.mult).then_inc(rots.s, 1)
                dve.tensor_tensor(rot2.rearrange("p (n c) -> p n c", c=C), ps1,
                                  wide(sin_t[:], NCH), ALU.mult).then_inc(rots.s, 1)
                dve.wait_ge(rots.s, rots.now(b, 2))
                dve.tensor_tensor(rot, rot, rot2, ALU.add).then_inc(rots.s, 1)
                dve.wait_ge(rots.s, rots.now(b, 3))
                dve.wait_ge(yrot.s, yrot.before(b, 2))
                dve.tensor_tensor_scan(ysc[:, ::-1], decay[:, ::-1], rot[:, ::-1], 0.0,
                                       ALU.mult, ALU.add).then_inc(rots.s, 1)
                dve.wait_ge(rots.s, rots.now(b, 4))
                first = ysc.rearrange("p (n c) -> p n c", c=C)[:, 1:, 0]
                dve.tensor_tensor(first, first, ps0[:, :NCH - 1, C - 1], ALU.add)\
                    .then_inc(rots.s, 1)

            def gate_in(b):
                dve.wait_ge(beta.s, beta.now(b, 2))
                dve.wait_ge(hgs.s, hgs.before(b, 1))
                dve.tensor_tensor(gz, bank(6, 2).rearrange("p (t n) -> p t n", t=TT),
                                  wide(row[:, R_GATE:R_GATE + D], TT), ALU.add)\
                    .then_inc(gpre.s, 1)

            def gate_out(b):
                dve.wait_ge(gact.s, gact.now(b, 1))
                dve.wait_ge(hmm.s, hmm.now(b, 1))
                dve.wait_ge(res.s, res.before(b, 1))
                dve.tensor_tensor(hg, bank(2, 2).rearrange("p (t n) -> p t n", t=TT), gz,
                                  ALU.mult).then_inc(hgs.s, 1)

            def ln_mid(b):
                dve.wait_ge(res.s, res.now(b, 1))
                statistics(ln2, Y, b * TT, b, 0)
                norm(ln2, rs2, Y, lambda t: xn[:, t, :], b * TT, b, (xt1.s, xt1.now(b, 1)))

            def ln_out(b):
                dve.wait_ge(res.s, res.now(b, 3))
                dve.wait_ge(m2.s, m2.now(b, 1))
                xb = X[:, bass.ts(b, TT), :]
                dve.tensor_tensor(xb, bank(6, 2).rearrange("p (t n) -> p t n", t=TT), xb,
                                  ALU.add).then_inc(ln3.s, 1)

            def ln_out_norm(b):
                dve.wait_ge(ln3.s, ln3.now(b, 1))
                statistics(ln3, X, b * TT, b, 1)
                norm(ln3, rs3, X, lambda t: X[:, b * TT + t, :], b * TT, b)

            def recurrence(b):
                rotate(b)
                gate_in(b)
                gate_out(b)
                ln_mid(b)

            recurrence(0)
            with dve.Fori(0, B - 1) as b:
                ln_in(b + 1)
                recurrence(b + 1)
                ln_out(b)
                ln_out_norm(b)

            for g in (kev, qev, vev, ksd, qsd, sqe, mxs, mneg, odv, ln4):
                dve.sem_inc(g.s, g.per)
            dve.wait_ge(res.s, res.now(B - 1, 1))
            piece = lambda m, n, k=1: m.rearrange("p t h s -> p (t h) s")[:, :, n * HD:(n + k) * HD]
            k_src = kq.rearrange("p (a d) -> p a d", d=HD)
            q_src = qt.rearrange("p (a d) -> p a d", d=HD)

            def dve_key(b, m):
                dve.wait_ge(kpr.s, kpr.now(b, m + 1))
                dve.wait_ge(ksd.s, ksd.before(b, 2))
                dve.tensor_tensor(kq[:, 512 * m:512 * m + 512].rearrange("p (t n) -> p t n", t=2),
                                  spare(m).rearrange("p (t n) -> p t n", t=2),
                                  wide(row[:, R_K:R_K + D], 2), ALU.add).then_inc(kev.s, 1)

            def dve_split_k(b, k):
                if k == 1:
                    dve.wait_ge(ksa.s, ksa.now(b, 1))
                    dve.tensor_tensor(k_src, k_src, piece(st, 0), ALU.subtract).then_inc(ksd.s, 1)
                elif k == 3:
                    dve.wait_ge(ksa.s, ksa.now(b, 2))
                    dve.wait_ge(ksd.s, ksd.now(b, 1))
                    dve.tensor_tensor(piece(st, 2), k_src, piece(st, 1), ALU.subtract)\
                        .then_inc(ksd.s, 1)
                    dve.tensor_copy(piece(st, 3, 2), piece(st, 0, 2)).then_inc(ksd.s, 1)
                    dve.tensor_copy(piece(st, 5), piece(st, 0)).then_inc(ksd.s, 1)

            def dve_query(b, m):
                dve.wait_ge(qpr.s, qpr.now(b, m + 1))
                dve.wait_ge(qsd.s, qsd.before(b, 5))
                dve.tensor_tensor(qt[:, 512 * m:512 * m + 512].rearrange("p (t n) -> p t n", t=2),
                                  spare(m).rearrange("p (t n) -> p t n", t=2),
                                  wide(row[:, R_Q:R_Q + D], 2), ALU.add).then_inc(qev.s, 1)

            def dve_split_q(b, k):
                if k == 1:
                    dve.wait_ge(qsa.s, qsa.now(b, 1))
                    dve.tensor_tensor(q_src, q_src, piece(stq, 0), ALU.subtract)\
                        .then_inc(qsd.s, 1)
                    for n in (1, 2):
                        dve.tensor_copy(piece(stq, n), piece(stq, 0)).then_inc(qsd.s, 1)
                elif k == 3:
                    dve.wait_ge(qsa.s, qsa.now(b, 2))
                    dve.wait_ge(qsd.s, qsd.now(b, 1))
                    dve.tensor_tensor(piece(stq, 5), q_src, piece(stq, 3), ALU.subtract)\
                        .then_inc(qsd.s, 1)
                    dve.tensor_copy(piece(stq, 4), piece(stq, 3)).then_inc(qsd.s, 1)

            def dve_value(b, m):
                dve.wait_ge(vpr.s, vpr.now(b, m + 1))
                dve.wait_ge(vset, 2)
                dve.wait_ge(pvs.s, pvs.before(b, 2 * TT * (m + 1)))
                bias = row[:, R_V + P * m:R_V + P * m + P].rearrange("p (h d) -> p h d", d=HD)
                for t in range(TT):
                    ins = dve.tensor_tensor(Vb[:, t, 8 * m:8 * m + 8, 0:HD],
                                            spare(m)[:, t * P:(t + 1) * P]
                                            .rearrange("p (h d) -> p h d", d=HD), bias, ALU.add)
                ins.then_inc(vev.s, 1)

            def dve_stack_q(b, n):
                dve.wait_ge(sqt.s, sqt.now(b, n + 1))
                q, m = n // 2, n % 2
                dve.tensor_copy(QTs[0:SK, GH * q:GH * q + GH, 2 * P * m:2 * P * (m + 1)],
                                spare(n).bitcast(BF16)[0:SK, :]
                                .rearrange("p (h n) -> p h n", h=GH)).then_inc(sqe.s, 1)

            def maxima(group, banks):
                for i, u, heads in banks:
                    b, g = group
                    w = (i + 1) * P
                    for a, h in enumerate(heads):
                        n = g * 16 + i * GH + h
                        if i == 0 and h == 0:
                            dve.wait_ge(mneg.s, mneg.now(b, 4 * (g - 1)) if g >= 2
                                        else mneg.before(b, 4 * (NG + g - 1)))
                        dve.wait_ge(mxs.s, mxs.now(b, n - 1) if n >= 2
                                    else mxs.before(b, 64 + n - 1))
                        dve.sem_inc(dve_held, 1)
                        dve.wait_ge(smm.s, smm.now(b, g * NSH + u + 1))
                        dve.sem_inc(dve_held, 1)
                        dve.tensor_tensor_reduce(junk[:, n % 2, 0:w],
                                                 bank((g * NSH + u) % 2)[:, a * w:(a + 1) * w],
                                                 causal[:, T - w:], 1.0, NEG, ALU.add, ALU.max,
                                                 Mx[:, g % 2, i, h:h + 1]).then_inc(mxs.s, 1)

            def negate(b, g):
                m, d = Mx[:, g % 2], nst[:, g % 2]
                dve.wait_ge(mxs.s, mxs.now(b, 16 * (g + 1)))
                dve.wait_ge(ntp.s, ntp.now(b, 2 * (g - 1)) if g >= 2
                            else ntp.before(b, 2 * (NG + g - 1)))
                dve.tensor_scalar(d[:, :, :, 0], m, -1.0, None, ALU.mult).then_inc(mneg.s, 1)
                dve.wait_ge(mneg.s, mneg.now(b, 4 * g + 1))
                dve.scalar_tensor_tensor(Mr[:], m, -1.0, d[:, :, :, 0], ALU.mult, ALU.subtract)\
                    .then_inc(mneg.s, 1)
                dve.wait_ge(mneg.s, mneg.now(b, 4 * g + 2))
                dve.tensor_copy(d[:, :, :, 1], Mr[:]).then_inc(mneg.s, 1)
                dve.wait_ge(mneg.s, mneg.now(b, 4 * g + 3))
                dve.tensor_tensor(d[:, :, :, 2], Mr[:], d[:, :, :, 1], ALU.subtract)\
                    .then_inc(mneg.s, 1)

            def divide(b, g):
                o = spare(1).rearrange("p (t h v) -> p t h v", t=TT, h=GH)
                dve.wait_ge(otp.s, otp.now(b, g + 1))
                if g == 0:
                    dve.wait_ge(o2t.s, o2t.before(b, KT))
                dve.reciprocal(rden[:], o[:, :, :, HD]).then_inc(odv.s, 1)
                dve.wait_ge(odv.s, odv.now(b, 2 * g + 1))
                dve.tensor_tensor(
                    otok[:, :, g * GH * HD:(g + 1) * GH * HD]
                    .rearrange("p t (h v) -> p t h v", h=GH), o[:, :, :, 0:HD],
                    rden[:].unsqueeze(3).to_broadcast([P, TT, GH, HD]), ALU.mult)\
                    .then_inc(odv.s, 1)

            def dve_output(b, m):
                dve.wait_ge(omm.s, omm.now(b, m + 1))
                dve.wait_ge(xob.s, xob.now(b, 1))
                dve.wait_ge(x2o.s, x2o.before(b, 2))
                dve.wait_ge(x2t.s, x2t.before(b, KT))
                dve.tensor_tensor(x2b[:, 2 * m:2 * m + 2, :],
                                  spare(m).rearrange("p (t n) -> p t n", t=2),
                                  X[:, bass.ds(b * TT + 2 * m, 2), :], ALU.add).then_inc(ln4.s, 1)

            def dve_stats(b, k):
                dve.wait_ge(ln4.s, ln4.now(b, 2))
                statistics(ln4, x2b, 0, b, 2)

            def dve_norm(b, k):
                norm(ln4, rs4, x2b, lambda t: x2b[:, t, :], 0, b)

            dve_steps = {"key": dve_key, "query": dve_query, "value": dve_value,
                         "split_k": dve_split_k, "split_q": dve_split_q,
                         "stack_q": dve_stack_q, "output": dve_output,
                         "stats": dve_stats, "norm": dve_norm}

            def dve_do(steps):
                for name, c, k in steps:
                    if name in dve_steps:
                        dve_steps[name](c, k)

            def dve_slot(b, g, j, prev, then, *steps):
                shares = SCORED[j] if then is not None else ([], [], [])
                maxima(then, shares[0])
                if j == 0 and prev is not None:
                    divide(*prev)
                dve_do(steps[0])
                maxima(then, shares[1])
                dve_do(steps[1])
                maxima(then, shares[2])
                if j == 2 and then is not None:
                    negate(*then)
                dve_do(steps[2])

            spare_banks[:] = 0, 1
            dve_do(early)
            ln_out(B - 1)
            dve_do(late)
            spare_banks[:] = 5, 7
            for share in SCORED:
                for banks in share:
                    maxima((0, 0), banks)
            negate(0, 0)
            ln_out_norm(B - 1)
            slots(0, dve_slot, first=True)
            with dve.Fori(0, B - 1) as b:
                slots(b, dve_slot)
            slots(B - 1, dve_slot, last=True)
            divide(B - 1, NG - 1)
            dve_do([(name, B - 1, k) for name, k in all_steps(FINISH)])

            for g in (hed, hbs, yws):
                dve.sem_inc(g.s, g.per)
            steps = [0]

            def then(ins):
                steps[0] += 1
                ins.then_inc(topk, 1)
                dve.wait_ge(topk, steps[0])

            dve.wait_ge(lge.s, lge.now(B - 1, 1))
            for a in range(2):
                then(dve.tensor_copy(LG2[64 * a:64 * a + 64, :].rearrange("p (b n) -> p b n", b=2),
                                     LGs[:, 2 * a:2 * a + 2, :]))
            for r in range(CAP // 8):
                v = top_v[:, 8 * r:8 * r + 8]
                then(dve.max(v, LG2))
                then(dve.max_index(top_i[:, 8 * r:8 * r + 8], v, LG2))
                if r + 1 < CAP // 8:
                    then(dve.match_replace(LG2, v, LG2, NEG))
            then(dve.tensor_copy(top_f, top_i))
            then(dve.tensor_scalar(top_f[64:P, :], top_f[64:P, :], float(B * T // 2), None,
                                   ALU.add))
            lo = slice(0, 64)
            then(dve.tensor_copy(far_v[lo, :], top_v[64:P, ::-1]))
            then(dve.tensor_copy(far_i[lo, :], top_f[64:P, ::-1]))
            then(dve.tensor_tensor(pick[lo, :], top_v[lo, :], far_v[lo, :], ALU.is_ge))
            then(dve.tensor_tensor(sel_v[lo, :], top_v[lo, :], far_v[lo, :], ALU.max))
            then(dve.tensor_tensor(sel_i[lo, :], top_f[lo, :], far_i[lo, :], ALU.subtract))
            then(dve.tensor_tensor(sel_i[lo, :], sel_i[lo, :], pick[lo, :], ALU.mult))
            then(dve.tensor_tensor(sel_i[lo, :], sel_i[lo, :], far_i[lo, :], ALU.add))
            then(dve.tensor_reduce(smx[lo, 0:1], sel_v[lo, :], AX.X, ALU.max))
            then(dve.tensor_scalar(smx[lo, 1:2], smx[lo, 0:1], -1.0, None, ALU.mult))
            shifted = steps[0]
            assert shifted == SHIFTED, shifted
            dve.wait_ge(wexp, 1)
            then(dve.reciprocal(smx[lo, 3:4], smx[lo, 2:3]))
            then(dve.tensor_scalar(sel_v[lo, :], sel_v[lo, :], smx[lo, 3:4], None, ALU.mult))
            for a in range(2):
                rows_a = slice(32 * a, 32 * a + 32)
                then(dve.tensor_copy(tw[:, CAP * a:CAP * a + CAP], sel_v[rows_a, :]))
                then(dve.tensor_copy(ti[:, CAP * a:CAP * a + CAP], sel_i[rows_a, :]))
            assert steps[0] == CHOSEN, steps
            dve.wait_ge(icm, 1)
            then(dve.tensor_copy(wcol, bank(0)[:, 0:NP]))
            then(dve.tensor_copy(icf, bank(0)[:, 32:32 + NP]))
            then(dve.tensor_copy(icol, icf))
            dve.wait_ge(offs, 4)
            then(dve.tensor_scalar(jcf, icf, off, None, ALU.add))
            then(dve.tensor_copy(jcol, jcf))
            assert steps[0] == TOPK, steps
            dve.wait_ge(b1_in, 16)

            def second_half(p):
                dve.wait_ge(h1m.s, h1m.now(p, 2))
                dve.wait_ge(htm.s, htm.before(p, 2))
                dve.tensor_copy(HB[:, 512:1024], bank(2)).then_inc(hed.s, 1)

            def hidden_bias(p):
                for a in range(2):
                    dve.wait_ge(htm.s, htm.now(p, a + 1))
                    if a == 0:
                        dve.wait_ge(y2m.s, y2m.before(p, 1))
                    dve.tensor_tensor(
                        hb[:, a * 512:(a + 1) * 512].rearrange("p (c n) -> p c n", c=8),
                        bank(3 + a).rearrange("p (c n) -> p c n", c=8),
                        b1_s[:, bass.ds(p, 1), 4 * a:4 * a + 4, :]
                        .rearrange("p e c a -> p (e c a)").unsqueeze(2).to_broadcast([P, 8, CAP]),
                        ALU.add).then_inc(hbs.s, 1)

            def weigh(p, u):
                dve.wait_ge(y2m.s, y2m.now(p, 1))
                dve.wait_ge(added.s, p + 1)
                dve.tensor_scalar(ye[u % RING], bank(5 + u % 2)[:, 0:D], wcol[:, bass.ds(p, 1)],
                                  None, ALU.mult).then_inc(yws.s, 1)

            second_half(0)
            hidden_bias(0)
            with dve.Fori(0, NP // RING - 1) as r:
                for u in range(RING):
                    p = r * RING + u
                    second_half(p + 1)
                    hidden_bias(p + 1)
                    weigh(p, u)
            for u in range(RING):
                p = NP - RING + u
                if p + 1 < NP:
                    second_half(p + 1)
                    hidden_bias(p + 1)
                weigh(p, u)

            for b in range(B):
                xb = X[:, b * TT:(b + 1) * TT, :]
                dve.wait_ge(fin_in[b], 32)
                dve.tensor_tensor(xb, xb, Y[:, b * TT:(b + 1) * TT, :], ALU.add).then_inc(fsum, 1)
                dve.wait_ge(fsum, b + 1)
                for t in range(b * TT, (b + 1) * TT):
                    dve.bn_stats(fstats[:, t, :], X[:, t, :]).then_inc(fstat, 1)
                for t in range(b * TT, (b + 1) * TT):
                    dve.wait_ge(fstat, t + 1)
                    dve.bn_aggr(fmv[:, t, :], fstats[:, t, :]).then_inc(fvar, 1)

        @block.scalar
        def _(act):
            for g in (xe1, gact, xe2, silu):
                act.sem_inc(g.s, g.per)
            act.dma_start(vec[:], vecs).then_inc(w_one, 16)
            act.dma_start(row[:], rows.to_broadcast([P, RCOLS])).then_inc(w_one, 16)
            act.dma_start(wi_s, w_in.rearrange("(k p) n -> p k n", p=P)).then_inc(w_one, 16)
            act.dma_start(wout_s, w_out.rearrange("v p n -> p v n")).then_inc(w_one, 16)
            act.wait_ge(setup_cb, 1)
            for g in range(2 * CH):
                act.dma_start(cb_s[CK * g:CK * g + CK, CK * g:CK * g + CK],
                              coupling[g % CH]).then_inc(w_one, 16)
            act.dma_start(wg_s, w_gate.rearrange("(k p) n -> p k n", p=P)).then_inc(w_one, 16)
            act.dma_start(wm1_s, w_mlp1.rearrange("(k p) n -> p k n", p=P)).then_inc(w_mlp, 16)
            act.dma_start(wm2_s, w_mlp2.rearrange("(k p) n -> p k n", p=P)).then_inc(w_mlp, 16)
            act.dma_start(wkv_s[:], w_kv.rearrange("(k p) n -> p k n", p=P)).then_inc(w_att, 16)
            act.dma_start(wq_s[:], w_q.rearrange("(k p) n -> p k n", p=P)).then_inc(w_att, 16)
            act.dma_start(wo_s[:], w_o.rearrange("(k p) n -> p k n", p=P)).then_inc(w_att, 16)
            act.wait_ge(consts, CONSTS)
            act.dma_start(wr_s[:, :, 0:NP], w_r[0].rearrange("(k p) n -> p k n", p=P))\
                .then_inc(w_att, 16)
            act.dma_start(wr_s[:, :, 32:32 + NP], w_r[1].rearrange("(k p) n -> p k n", p=P))\
                .then_inc(w_att, 16)
            act.wait_ge(w_one, W_ONE)
            act.activation(mag, vec[:, V_DEC:V_DEC + 1], ACT.Sigmoid).then_inc(trig, 1)
            act.wait_ge(setup, 9)
            act.activation(sin_t[:], rot[:, 0:C], ACT.Sin).then_inc(trig, 1)
            act.wait_ge(setup, 16)
            act.activation(cos_t[:], rot[:, C:2 * C], ACT.Sin).then_inc(trig, 1)

            def turned(xT, xt, xe, used, g, be, b):
                act.wait_ge(xt.s, xt.now(b, 1))
                act.wait_ge(*used)
                for k in range(KT):
                    act.activation(xT[:, k, :], bank(k), ACT.Identity,
                                   bias=vec[:, be + k:be + k + 1],
                                   scale=vec[:, g + k:g + k + 1]).then_inc(xe.s, 1)

            def turned_1(b):
                turned(xT1, xt1, xe1, (beta.s, beta.before(b, 2)), V_G1, V_B1, b)

            def turned_2(b):
                turned(xT2, xt2, xe2, (m1.s, m1.before(b, MT)), V_G2, V_B2, b)

            def sigmoid(b):
                act.wait_ge(gpre.s, gpre.now(b, 1))
                act.activation(gz, gz, ACT.Sigmoid).then_inc(gact.s, 1)

            def hidden(b, tiles):
                for m in tiles:
                    act.wait_ge(m1.s, m1.now(b, m + 1))
                    act.wait_ge(m2.s, m2.before(b, 1))
                    act.activation(hid[:, m, :], bank(4 + m % 2), ACT.Silu,
                                   bias=vec[:, V_BM + m:V_BM + m + 1]).then_inc(silu.s, 1)

            turned_1(0)
            sigmoid(0)
            turned_2(0)
            with act.Fori(0, B - 1) as b:
                hidden(b, range(5))
                turned_1(b + 1)
                hidden(b, range(5, MT))
                sigmoid(b + 1)
                turned_2(b + 1)

            for g in (cte, xte, ksa, qsa, ske, nte, exq, oev, o2e, x2e, lge):
                act.sem_inc(g.s, g.per)
            act.wait_ge(res.s, res.now(B - 1, 1))

            piece = lambda m, n, k=1: m.rearrange("p t h s -> p (t h) s")[:, :, n * HD:(n + k) * HD]
            k_src = kq.rearrange("p (a d) -> p a d", d=HD)
            q_src = qt.rearrange("p (a d) -> p a d", d=HD)

            def plain(written, read, dst):
                def step(b, k):
                    act.wait_ge(written.s, written.now(b, k + 1))
                    act.activation(dst[:, k, :], spare(k), ACT.Copy).then_inc(read.s, 1)
                return step

            def act_split_k(b, k):
                if k == 0:
                    act.wait_ge(kev.s, kev.now(b, 2))
                    act.wait_ge(skt.s, skt.before(b, 2 * NG))
                    act.activation(piece(st, 0), k_src, ACT.Copy).then_inc(ksa.s, 1)
                elif k == 2:
                    act.wait_ge(ksd.s, ksd.now(b, 1))
                    act.activation(piece(st, 1), k_src, ACT.Copy).then_inc(ksa.s, 1)

            def act_split_q(b, k):
                if k == 0:
                    act.wait_ge(qev.s, qev.now(b, 2))
                    act.wait_ge(sqt.s, sqt.before(b, 2 * NG))
                    act.activation(piece(stq, 0), q_src, ACT.Copy).then_inc(qsa.s, 1)
                elif k == 2:
                    act.wait_ge(qsd.s, qsd.now(b, 1))
                    act.activation(piece(stq, 3), q_src, ACT.Copy).then_inc(qsa.s, 1)

            def act_stack_k(b, n):
                act.wait_ge(skt.s, skt.now(b, n + 1))
                q, m = n // 2, n % 2
                act.activation(KTs[0:SX, GH * q:GH * q + GH, 2 * P * m:2 * P * (m + 1)],
                               spare(n).bitcast(BF16)[0:SX, :]
                               .rearrange("p (h n) -> p h n", h=GH), ACT.Copy).then_inc(ske.s, 1)

            def act_logits(b, k):
                act.wait_ge(lgm.s, lgm.now(b, 1))
                act.activation(LGs[:, b, :], spare(0)[0:64, :], ACT.Copy).then_inc(lge.s, 1)

            def minus_max(b, g):
                for m in range(2):
                    act.wait_ge(ntp.s, ntp.now(b, 2 * g + m + 1))
                    act.activation(QTs[SK:SX, GH * g + 2 * m:GH * g + 2 * m + 2, :],
                                   spare(m).bitcast(BF16)[SK:SX, :]
                                   .rearrange("p (h n) -> p h n", h=2), ACT.Copy)\
                        .then_inc(nte.s, 1)

            def exponentials(b, g, j):
                w = T - j * P
                t = g * TT + j
                for n, heads in enumerate(SHARED[j], FIRST[j]):
                    if n == FIRST[j]:
                        act.wait_ge(pvs.s, pvs.now(b, t - 1) if t >= 2
                                    else pvs.before(b, NG * TT + t - 1))
                    act.wait_ge(stm.s, stm.now(b, g * NSH + n + 1))
                    act.activation(
                        pb[j % 2][:, heads[0]:heads[-1] + 1, 0:w],
                        bank(2 + n % 3)[:, 0:len(heads) * w]
                        .rearrange("p (h n) -> p h n", h=len(heads)),
                        ACT.Exp, scale=float(HD) ** -0.5).then_inc(exq.s, 1)

            def group_out(b, g):
                act.wait_ge(otp.s, otp.now(b, g) if g > 0 else otp.before(b, NG))
                act.wait_ge(pvs.s, pvs.now(b, TT * (g + 1)))
                act.activation(oTs, bank(6), ACT.Copy).then_inc(oev.s, 1)

            act_steps = {"context": plain(ctp, cte, cT), "query_in": plain(xtp, xte, aT),
                         "heads": plain(o2t, o2e, oT2), "turn": plain(x2t, x2e, x2T),
                         "split_k": act_split_k, "split_q": act_split_q,
                         "stack_k": act_stack_k, "logits": act_logits}

            def act_do(steps):
                for name, c, k in steps:
                    if name in act_steps:
                        act_steps[name](c, k)

            def act_slot(b, g, j, prev, then, *steps):
                if j == 0 and prev is not None:
                    group_out(*prev)
                exponentials(b, g, j)
                act_do(steps[0] + steps[1])
                if j == TT - 1 and then is not None:
                    minus_max(*then)
                act_do(steps[2])

            spare_banks[:] = 0, 1
            hidden(B - 1, range(4))
            act_do(early[:2 * KT])
            hidden(B - 1, range(4, MT))
            act_do(early[2 * KT:] + late)
            spare_banks[:] = 5, 7
            minus_max(0, 0)
            slots(0, act_slot, first=True)
            with act.Fori(0, B - 1) as b:
                slots(b, act_slot)
            slots(B - 1, act_slot, last=True)
            group_out(B - 1, NG - 1)
            act_do([(name, B - 1, k) for name, k in all_steps(FINISH)])

            for g in (xge, hea, gel):
                act.sem_inc(g.s, g.per)
            act.wait_ge(topk, SHIFTED)
            act.activation(sel_v[0:64, :], sel_v[0:64, :], ACT.Exp, bias=smx[0:64, 1:2],
                           accum_out=smx[0:64, 2:3]).then_inc(wexp, 1)

            def tokens(p):
                act.wait_ge(xgt.s, xgt.now(p, 1))
                act.wait_ge(h1m.s, h1m.before(p, 2))
                act.activation(xgT.rearrange("p k n -> p (k n)"), bank(0)[:, 0:KT * P], ACT.Copy)\
                    .then_inc(xge.s, 1)

            def first_half(p):
                act.wait_ge(h1m.s, h1m.now(p, 1))
                act.wait_ge(htm.s, htm.before(p, 1))
                act.activation(HB[:, 0:512], bank(1), ACT.Copy).then_inc(hea.s, 1)

            def gelu(p):
                for a in range(2):
                    act.wait_ge(hbs.s, hbs.now(p, a + 1))
                    act.activation(hb[:, a * 512:(a + 1) * 512], hb[:, a * 512:(a + 1) * 512],
                                   ACT.Gelu).then_inc(gel.s, 1)

            tokens(0)
            first_half(0)
            tokens(1)
            gelu(0)
            with act.Fori(0, NP // RING - 1) as r:
                for u in range(RING):
                    p = r * RING + u
                    first_half(p + 1)
                    tokens(p + 2)
                    gelu(p + 1)
            for u in range(RING):
                p = NP - RING + u
                if p + 1 < NP:
                    first_half(p + 1)
                if p + 2 < NP:
                    tokens(p + 2)
                if p + 1 < NP:
                    gelu(p + 1)

            for b in range(B):
                act.wait_ge(froot, 4 * b + 4)
                for t in range(b * TT, (b + 1) * TT):
                    act.activation(X[:, t, :], X[:, t, :], ACT.Identity, bias=fshift[:, t:t + 1],
                                   scale=frstd[:, t:t + 1]).then_inc(fout, 1)

        @block.tensor
        def _(pe):
            for g in (xt1, beta, hmm, xt2, m1, m2):
                pe.sem_inc(g.s, g.per)
            def turn(ln, xt, b, read):
                pe.wait_ge(*read)
                for t in range(TT):
                    pe.wait_ge(ln.s, ln.now(b, 2 * TT + t + 1))
                    for j in range(KT):
                        mm = pe.transpose(bank(j)[:, t * P:(t + 1) * P],
                                          xn[:, t, j * P:(j + 1) * P], ident[:])
                mm.then_inc(xt.s, 1)

            def project(b, free=None):
                pe.wait_ge(xe1.s, xe1.now(b, KT))
                pe.wait_ge(hgs.s, hgs.before(b, 1))
                for v in range(2):
                    for k in range(KT):
                        mm = pe.matmul(bank(2 + v), wi_s[:, k, v * P:(v + 1) * P], xT1[:, k, :],
                                       start=(k == 0), stop=(k == KT - 1))
                mm.then_inc(beta.s, 1)
                if free is not None:
                    pe.wait_ge(ln3.s, free)
                for t in range(TT):
                    for k in range(KT):
                        mm = pe.matmul(PS[:, 6 * 512 + t * D:6 * 512 + (t + 1) * D],
                                       xT1[:, k, t * P:(t + 1) * P], wg_s[:, k, :],
                                       start=(k == 0), stop=(k == KT - 1))
                mm.then_inc(beta.s, 1)

            def mix(b):
                pe.wait_ge(yrot.s, yrot.now(b, 2))
                for t in range(TT):
                    for k, y in enumerate((yc, ys)):
                        mm = pe.matmul(PS[:, 2 * 512 + t * D:2 * 512 + (t + 1) * D],
                                       y[:, t * P:(t + 1) * P], wc_s[:, k, :],
                                       start=(k == 0), stop=(k == 1))
                mm.then_inc(hmm.s, 1)

            def expand(b, tiles):
                pe.wait_ge(xe2.s, xe2.now(b, KT))
                for m in tiles:
                    pe.wait_ge(silu.s, silu.before(b, MT + m - 1) if m < 2 else silu.now(b, m - 1))
                    for k in range(KT):
                        mm = pe.matmul(bank(4 + m % 2), wm1_s[:, k, m * P:(m + 1) * P],
                                       xT2[:, k, :], start=(k == 0), stop=(k == KT - 1))
                    mm.then_inc(m1.s, 1)

            def shrink(b, tiles):
                pe.wait_ge(silu.s, silu.now(b, MT))
                for t in tiles:
                    for m in range(MT):
                        mm = pe.matmul(PS[:, 6 * 512 + t * D:6 * 512 + (t + 1) * D],
                                       hid[:, m, t * P:(t + 1) * P], wm2_s[:, m, :],
                                       start=(m == 0), stop=(m == MT - 1))
                if t == TT - 1:
                    mm.then_inc(m2.s, 1)

            pe.wait_ge(consts, CONSTS)
            turn(ln1, xt1, 0, (xe1.s, KT))
            pe.wait_ge(w_one, W_ONE)
            for v in range(2):
                mm = pe.matmul(PS[:, 4 * 512 + v * D:4 * 512 + (v + 1) * D], cb_s, wout_s[:, v, :],
                               start=True, stop=True)
            mm.then_inc(wc_mm, 1)
            project(0)
            pe.wait_ge(setup, SETUP)
            mix(0)
            turn(ln2, xt2, 0, (xe1.s, xe1.now(0, KT)))
            pe.wait_ge(w_mlp, 32)
            with pe.Fori(0, B - 1) as b:
                expand(b, range(5))
                turn(ln1, xt1, b + 1, (xe2.s, xe2.now(b, KT)))
                expand(b, range(5, 6))
                project(b + 1, ln3.before(b, 1))
                expand(b, range(6, MT))
                pe.wait_ge(gpre.s, gpre.now(b + 1, 1))
                shrink(b, [0])
                mix(b + 1)
                shrink(b, [1, 2])
                turn(ln2, xt2, b + 1, (xe1.s, xe1.now(b + 1, KT)))
                shrink(b, [3])

            for g in (ctp, xtp, kpr, qpr, vpr, skt, sqt, smm, ntp, stm, pvs, otp, o2t, omm, x2t,
                      lgm):
                pe.sem_inc(g.s, g.per)
            pe.wait_ge(w_att, 16 * 5)

            read_by = {0: None, 1: None}

            def take(k, sig, value):
                if read_by[k % 2] is not None:
                    pe.wait_ge(*read_by[k % 2])
                read_by[k % 2] = (sig.s, value)
                return spare(k)

            def turned(o, src, k):
                for t in range(TT):
                    mm = pe.transpose(o[:, t * P:(t + 1) * P], src[:, t, k * P:(k + 1) * P],
                                      ident[:])
                return mm

            def pe_context(b, k):
                if k == 0:
                    pe.wait_ge(c_in.s, c_in.now(b, 1))
                turned(take(k, cte, cte.now(b, k + 1)), ctxb, k).then_inc(ctp.s, 1)

            def pe_query_in(b, k):
                if k == 0:
                    pe.wait_ge(xs_in.s, xs_in.now(b, 1))
                turned(take(k, xte, xte.now(b, k + 1)), xs, k).then_inc(xtp.s, 1)

            def projected(o, xt, w, m):
                for t in range(2):
                    for k in range(KT):
                        mm = pe.matmul(o[:, t * D:(t + 1) * D],
                                       xt[:, k, (2 * m + t) * P:(2 * m + t + 1) * P], w[:, k, :],
                                       start=(k == 0), stop=(k == KT - 1))
                return mm

            def pe_key(b, m):
                pe.wait_ge(cte.s, cte.now(b, KT))
                projected(take(m, kev, kev.now(b, m + 1)), cT, wkv_s[:, :, 0:D], m)\
                    .then_inc(kpr.s, 1)

            def pe_query(b, m):
                pe.wait_ge(xte.s, xte.now(b, KT))
                projected(take(m, qev, qev.now(b, m + 1)), aT, wq_s, m).then_inc(qpr.s, 1)

            def pe_value(b, m):
                pe.wait_ge(cte.s, cte.now(b, KT))
                o = take(m, vev, vev.now(b, m + 1))
                for t in range(TT):
                    for k in range(KT):
                        mm = pe.matmul(o[:, t * P:(t + 1) * P], cT[:, k, t * P:(t + 1) * P],
                                       wkv_s[:, k, D + m * P:D + (m + 1) * P],
                                       start=(k == 0), stop=(k == KT - 1))
                mm.then_inc(vpr.s, 1)

            def pe_stack(src, rows, done, read, made):
                def step(b, n):
                    if n == 0:
                        for g in made:
                            pe.wait_ge(g.s, g.now(b, g.per))
                    o = take(n, read, read.now(b, n + 1)).bitcast(BF16)
                    for h in range(GH):
                        for t in range(2):
                            mm = pe.transpose(o[0:rows, (2 * h + t) * P:(2 * h + t + 1) * P],
                                              src[:, 2 * (n % 2) + t, GH * (n // 2) + h, 0:rows],
                                              identb[:])
                    mm.then_inc(done.s, 1)
                return step

            def scores(group, banks):
                for i, u, heads in banks:
                    b, g = group
                    w = (i + 1) * P
                    if u == 0:
                        pe.wait_ge(ske.s, ske.now(b, 2 * (g + 1)))
                        pe.wait_ge(sqe.s, sqe.now(b, 2 * (g + 1)))
                    if u >= 2:
                        pe.wait_ge(mxs.s, mxs.now(b, 16 * g + FOUND[u - 2]))
                    elif g > 0:
                        pe.wait_ge(mxs.s, mxs.now(b, 16 * (g - 1) + FOUND[NSH + u - 2]))
                    else:
                        pe.wait_ge(mxs.s, mxs.before(b, 16 * (NG - 1) + FOUND[NSH + u - 2]))
                    for a, h in enumerate(heads):
                        mm = pe.matmul(bank((g * NSH + u) % 2)[:, a * w:(a + 1) * w],
                                       QTs[0:SK, g * GH + h, i * P:(i + 1) * P],
                                       KTs[0:SK, g * GH + h, 0:w], start=True, stop=True)
                    mm.then_inc(smm.s, 1)

            def minus_max(b, g):
                pe.wait_ge(mneg.s, mneg.now(b, 4 * (g + 1)))
                for m in range(2):
                    o = take(m, nte, nte.now(b, 2 * g + m + 1)).bitcast(BF16)
                    for h in range(2):
                        for i in range(TT):
                            mm = pe.transpose(o[SK:SX, (TT * h + i) * P:(TT * h + i + 1) * P],
                                              nst[:, g % 2, i, 2 * m + h, :], identb[:])
                    mm.then_inc(ntp.s, 1)

            def shifted(b, g, j):
                w = T - j * P
                if j == 0:
                    pe.wait_ge(nte.s, nte.now(b, 2 * g + 2))
                for n, heads in enumerate(SHARED[j], FIRST[j]):
                    if n >= 3:
                        pe.wait_ge(exq.s, exq.now(b, g * NSH + n - 2))
                    elif g > 0:
                        pe.wait_ge(exq.s, exq.now(b, (g - 1) * NSH + (10, 11, 9)[n]))
                    else:
                        pe.wait_ge(exq.s, exq.before(b, (NG - 1) * NSH + (10, 11, 9)[n]))
                    for a, h in enumerate(heads):
                        mm = pe.matmul(bank(2 + n % 3)[:, a * w:(a + 1) * w],
                                       KTs[0:SX, g * GH + h, j * P:(j + 1) * P],
                                       QTs[0:SX, g * GH + h, j * P:T], start=True, stop=True)
                    mm.then_inc(stm.s, 1)
                    yield

            def values(b, g, j):
                pe.wait_ge(msk.s, msk.now(b, g * TT + j + 1))
                if j == 0:
                    pe.wait_ge(oev.s, oev.now(b, g) if g > 0 else oev.before(b, NG))
                    if g % 2 == 0:
                        pe.wait_ge(vev.s, vev.now(b, g // 2 + 1))
                for h in range(GH):
                    mm = pe.matmul(bank(6)[VW * h:VW * (h + 1), j * P:T], Vb[:, j, g * GH + h, :],
                                   pb[j % 2][:, h, 0:T - j * P], start=(j == 0),
                                   stop=(j == TT - 1))
                mm.then_inc(pvs.s, 1)

            def heads_out(b, g):
                pe.wait_ge(oev.s, oev.now(b, g + 1))
                o = take(1, odv, odv.now(b, 2 * g + 2))
                for t in range(TT):
                    mm = pe.transpose(o[:, t * P:(t + 1) * P], oTs[:, t * P:(t + 1) * P], ident[:])
                mm.then_inc(otp.s, 1)

            def pe_heads(b, k):
                pe.wait_ge(odv.s, odv.now(b, 2 * NG))
                turned(take(k, o2e, o2e.now(b, k + 1)), otok, k).then_inc(o2t.s, 1)

            def pe_output(b, m):
                pe.wait_ge(o2e.s, o2e.now(b, KT))
                projected(take(m, ln4, ln4.now(b, m + 1)), oT2, wo_s, m).then_inc(omm.s, 1)

            def pe_turn(b, k):
                pe.wait_ge(ln4.s, ln4.now(b, 2 + 3 * TT))
                turned(take(k, x2e, x2e.now(b, k + 1)), x2b, k).then_inc(x2t.s, 1)

            def pe_logits(b, k):
                pe.wait_ge(x2e.s, x2e.now(b, KT))
                o = take(0, lge, lge.now(b, 1))
                for k in range(KT):
                    mm = pe.matmul(o[0:64, :], wr_s[:, k, :], x2T[:, k, :],
                                   start=(k == 0), stop=(k == KT - 1))
                mm.then_inc(lgm.s, 1)

            pe_steps = {"context": pe_context, "query_in": pe_query_in, "key": pe_key,
                        "query": pe_query, "value": pe_value, "heads": pe_heads,
                        "stack_k": pe_stack(st, SX, skt, ske, (ksa, ksd)),
                        "stack_q": pe_stack(stq, SK, sqt, sqe, (qsa, qsd)),
                        "output": pe_output, "turn": pe_turn, "logits": pe_logits}

            def pe_do(steps):
                for name, c, k in steps:
                    if name in pe_steps:
                        pe_steps[name](c, k)

            def pe_slot(b, g, j, prev, then, *steps):
                shares = SCORED[j] if then is not None else ([], [], [])
                for n, _ in enumerate(shifted(b, g, j)):
                    of = len(SHARED[j])
                    scores(then, shares[0][n * len(shares[0]) // of:
                                           (n + 1) * len(shares[0]) // of])
                if j == 0 and prev is not None:
                    heads_out(*prev)
                pe_do(steps[0])
                scores(then, shares[1])
                pe_do(steps[1])
                if j == TT - 1 and then is not None:
                    minus_max(*then)
                if j > 0:
                    values(b, g, j - 1)
                scores(then, shares[2])
                if j == TT - 1:
                    values(b, g, j)
                pe_do(steps[2])

            spare_banks[:] = 0, 1
            expand(B - 1, range(4))
            read_by.update({k: (xe2.s, xe2.now(B - 1, KT)) for k in range(2)})
            pe_do(early[:2 * KT])
            expand(B - 1, range(4, MT))
            pe_do(early[2 * KT:])
            pe.wait_ge(ln3.s, ln3.now(B - 2, 1))
            shrink(B - 1, range(TT))
            pe.wait_ge(vset, 3)
            pe_do(late)
            for k in range(2):
                pe.wait_ge(*read_by[k])
            pe.wait_ge(silu.s, silu.now(B - 1, MT))
            pe.wait_ge(ln3.s, ln3.now(B - 1, 1))
            read_by.update({0: None, 1: None})
            spare_banks[:] = 5, 7
            for share in SCORED:
                for banks in share:
                    scores((0, 0), banks)
            minus_max(0, 0)
            slots(0, pe_slot, first=True)
            for k in range(2):
                pe.wait_ge(*read_by[k])
            with pe.Fori(0, B - 1) as b:
                read_by.update({0: (lge.s, lge.before(b, 1)), 1: (x2e.s, x2e.before(b, KT))})
                slots(b, pe_slot)
            read_by.update({0: (lge.s, lge.now(B - 2, 1)), 1: (x2e.s, x2e.now(B - 2, KT))})
            slots(B - 1, pe_slot, last=True)
            heads_out(B - 1, NG - 1)
            pe_do([(name, B - 1, k) for name, k in all_steps(FINISH)])

            for g in (xgt, h1m, htm, y2m):
                pe.sem_inc(g.s, g.per)
            pe.wait_ge(topk, CHOSEN)
            pe.transpose(bank(0)[:, 0:32], tw, ident[0:32, 0:32])
            pe.transpose(bank(0)[:, 32:64], ti, ident[0:32, 0:32]).then_inc(icm, 1)
            pe.wait_ge(topk, TOPK)
            pe.wait_ge(lge.s, lge.now(B - 1, 1))

            def tokens(p, u, r):
                pe.wait_ge(gathered[u], 16 * (r + 1))
                pe.wait_ge(xge.s, xge.before(p, 1))
                for k in range(KT):
                    mm = pe.transpose(bank(0)[:, k * P:(k + 1) * P],
                                      xg[u][:, k * P:(k + 1) * P], ident[:])
                mm.then_inc(xgt.s, 1)

            def first(p, u, r):
                pe.wait_ge(xge.s, xge.now(p, 1))
                pe.wait_ge(w1_ring[u].s, w1_ring[u].now(r, 1))
                for n in range(2):
                    pe.wait_ge((hea, hed)[n].s, (hea, hed)[n].before(p, 1))
                    for k in range(KT):
                        for e in range(2):
                            mm = pe.matmul(bank(1 + n)[CAP * e:CAP * (e + 1), :],
                                           xgT[:, k, CAP * e:CAP * (e + 1)],
                                           w1_of[u][:, e, k, n * 512:(n + 1) * 512],
                                           start=(k == 0), stop=(k == KT - 1))
                    mm.then_inc(h1m.s, 1)

            def across(p):
                for a in range(2):
                    pe.wait_ge((hea, hed)[a].s, (hea, hed)[a].now(p, 1))
                    pe.wait_ge(hbs.s, hbs.before(p, a + 1))
                    for c in range(4):
                        n = 4 * a + c
                        mm = pe.transpose(bank(3 + a)[:, c * P:(c + 1) * P],
                                          HB[:, n * P:(n + 1) * P], ident[:])
                    mm.then_inc(htm.s, 1)

            def second(p, u, r, weights=None):
                pe.wait_ge(b_ring[u].s, b_ring[u].now(r, 1))
                y = bank(5 + u % 2)
                v, filling = weights or (u, r)
                pe.wait_ge(w2_ring[v].s, w2_ring[v].now(filling, 1))
                pe.wait_ge(gel.s, gel.now(p, 2))
                pe.wait_ge(yws.s, p + 1)
                pe.matmul(y[:, 0:D], pair_of, b2_s[u], start=True, stop=False,
                          skip_group_check=True)
                for sl in range(S):
                    for m in range(M2 // P):
                        c = sl * (M2 // P) + m
                        for e in range(2):
                            mm = pe.matmul(y[CAP * e:CAP * (e + 1), sl * KO:(sl + 1) * KO],
                                           hb[:, c * P + CAP * e:c * P + CAP * (e + 1)],
                                           w2_of[v][:, e, sl, m, :], start=False,
                                           stop=(m == M2 // P - 1), skip_group_check=True)
                mm.then_inc(y2m.s, 1)

            pe.wait_ge(offs, 4)
            tokens(0, 0, 0)
            first(0, 0, 0)
            tokens(1, 1, 0)
            across(0)
            with pe.Fori(0, NP // RING - 1) as r:
                for u in range(RING):
                    p = r * RING + u
                    v = (u + 1) % RING
                    first(p + 1, v, r + (u + 1) // RING)
                    tokens(p + 2, (u + 2) % RING, r + (u + 2) // RING)
                    second(p, u, r)
                    across(p + 1)
            r = NP // RING - 1
            for u in range(RING):
                p = NP - RING + u
                if p + 1 < NP:
                    first(p + 1, *((u + 1, r) if p + 1 < NP - 1 else (RING, 0)))
                if p + 2 < NP:
                    tokens(p + 2, (u + 2) % RING, r + (u + 2) // RING)
                second(p, u, r, (RING, 0) if p == NP - 1 else None)
                if p + 1 < NP:
                    across(p + 1)


def kernel(**inputs):
    from concourse import bacc as _bacc
    from concourse.bass_utils import run_bass_kernel_spmd as _run

    i = {k: np.asarray(v) for k, v in inputs.items()}
    w = lambda n: i["L0_" + n]
    col = lambda v: v.reshape(-1, P).T
    twice = lambda v: np.concatenate([v, v])[:, None]
    swap = lambda m: np.concatenate([m[NK:], m[:NK]])
    wi, wo = w("attn_w_in"), w("attn_w_out").T
    w1 = w("ffn_W1").reshape(NP, 2, S, KT, P, M2).transpose(0, 4, 1, 3, 2, 5).reshape(NP, P, W1C)
    w2 = w("ffn_W2").reshape(NP, 2, S, M2 // P, P, KO).transpose(0, 4, 1, 2, 3, 5)\
        .reshape(NP, P, W2C)
    arrays = {
        "x": i["x"], "ctx_in": i["ctx_1024"],
        "w_in": np.concatenate([wi, swap(wi)]).T,
        "w_gate": w("attn_w_gate").T,
        "w_out": np.stack([wo, swap(wo)]),
        "coupling": w("attn_coupling"),
        "w_mlp1": w("attn_w_mlp1").T, "w_mlp2": w("attn_w_mlp2").T,
        "w_q": w("xattn_wq_w").T,
        "w_kv": np.concatenate([w("xattn_wk_w"), w("xattn_wv_w")]).T,
        "w_o": w("xattn_wo_w").T,
        "w_r": np.stack([w("ffn_Wr")[0::2].T, w("ffn_Wr")[1::2].T]),
        "vecs": np.concatenate([col(w("attn_ln1_g")), col(w("attn_ln1_b")), col(w("attn_ln2_g")),
                                col(w("attn_ln2_b")), col(w("attn_b_mlp1")),
                                twice(w("attn_log_decay")), twice(w("attn_frequency"))], axis=1),
        "rows": np.concatenate([w("attn_b_gate"), w("attn_b_mlp2"), w("xattn_wk_b"),
                                w("xattn_wv_b"), w("xattn_wq_b"), w("xattn_wo_b")])[None],
        "b1": w("ffn_b1").reshape(NP, 2, S * M2 // P, P).transpose(3, 0, 2, 1),
        "b2": w("ffn_b2").reshape(NP, 2, D),
        "experts": np.concatenate([w1, w2], axis=2),
    }
    arrays = {n: np.ascontiguousarray(a) for n, a in arrays.items()}
    nc = _bacc.Bacc("TRN2", target_bir_lowering=False, num_devices=1)
    args = [nc.dram_tensor(n, a.shape, mybir.dt.from_np(a.dtype), kind="ExternalInput").ap()
            for n, a in arrays.items()]
    out = nc.dram_tensor("out", (B, T, D), F32, kind="ExternalOutput").ap()
    build(nc, *args, out)
    return _run(nc, [arrays], core_ids=[0]).results[0]["out"]
```
